# Optimizing a Trainium2 kernel written in Bass

```python
import numpy as np
import jax
import jax.numpy as jnp

def _softmax(x, axis=-1):
    return jax.nn.softmax(x, axis=axis)

def _gelu(x):
    return jax.nn.gelu(x, approximate=True)

def _silu(x):
    return jax.nn.silu(x)

def _sigmoid(x):
    return jax.nn.sigmoid(x)

def _layernorm(x, axis=-1, eps=1e-05):
    m = jnp.mean(x, axis=axis, keepdims=True)
    v = jnp.var(x, axis=axis, keepdims=True)
    return (x - m) / jnp.sqrt(v + eps)

def _scatter_add(tgt, idx, src, axis=0):
    return tgt.at[idx].add(src)

def _segment_sum(src, seg, n):
    return jax.ops.segment_sum(src, seg, n)
kernel_name = 'mk_xattn_ffn_d2_seqx_r8_2cc2ec'

def setup_inputs(seed: int=0):
    np.random.seed(seed)
    _w = jnp.asarray

    def _rec_inputs():
        import jax
        import jax.numpy as jnp
        _rk = jax.random.key(seed)
        x = -0.0002928 + 1 * jax.random.normal(jax.random.fold_in(_rk, 1), (8, 256, 128), jnp.float32)
        _lenS = 256 - jax.random.randint(jax.random.fold_in(_rk, 7), (8,), 0, max(1, 256 // 4) + 1, jnp.int32)
        _lenS2 = 256 - jax.random.randint(jax.random.fold_in(_rk, 8), (8,), 0, max(1, 256 // 4) + 1, jnp.int32)
        _ctx_768P = jax.random.normal(jax.random.fold_in(_rk, 11), (8, 16, 96), jnp.float32)
        _ctx_768c = jax.random.dirichlet(jax.random.fold_in(_rk, 511), 0.3 * jnp.ones((16,), jnp.float32), (8, 256))
        _ctx_768t = jnp.einsum('bsk,bkd->bsd', _ctx_768c, _ctx_768P)
        _ctx_768t = _ctx_768t * jax.lax.rsqrt(jnp.mean(jnp.square(_ctx_768t)) + 1e-12) * 0.953939
        ctx_768 = -0.00055796 + 0.999787 * (_ctx_768t + 0.3 * jax.random.normal(jax.random.fold_in(_rk, 611), (8, 256, 96), jnp.float32))
        return (x, ctx_768)
    x, ctx_768 = _rec_inputs()

    def _L0_xattn_setup():
        import jax, jax.numpy as jnp
        import numpy as np
        HEADS = 16
        DIM_HEAD = 64
        key = jax.random.key(seed)
        ks = jax.random.split(key, 7)
        b, n, m = (2, 256, 128)
        query_dim, context_dim = (128, 96)
        inner = HEADS * DIM_HEAD
        s_q = 1.0 / np.sqrt(query_dim)
        s_c = 1.0 / np.sqrt(context_dim)
        s_i = 1.0 / np.sqrt(inner)
        return {'x': jax.random.normal(ks[0], (b, n, query_dim), jnp.float32), 'context': jax.random.normal(ks[1], (b, m, context_dim), jnp.float32), 'Wq': jax.random.normal(ks[2], (query_dim, inner), jnp.float32) * s_q, 'Wk': jax.random.normal(ks[3], (context_dim, inner), jnp.float32) * s_c, 'Wv': jax.random.normal(ks[4], (context_dim, inner), jnp.float32) * s_c, 'Wo': jax.random.normal(ks[5], (inner, query_dim), jnp.float32) * s_i, 'bo': jax.random.normal(ks[6], (query_dim,), jnp.float32) * 0.01}
    _L0_xattn_all = _L0_xattn_setup()
    _L0_xattn_in = {k: v for k, v in _L0_xattn_all.items() if k in ('Wq', 'Wk', 'Wv', 'Wo', 'bo')}
    del _L0_xattn_all

    def _L0_ffn_setup():
        import jax, jax.numpy as jnp
        import numpy as np
        TOP_K = 2
        EPS = 1e-09
        key = jax.random.key(seed)
        ks = jax.random.split(key, 6)
        B, T, D, H, E = (4, 256, 128, 256, 8)
        x = jax.random.normal(ks[0], (B, T, D), dtype=jnp.float32)
        Wg = jax.random.normal(ks[1], (E, D), dtype=jnp.float32) * 0.02
        W1 = jax.random.normal(ks[2], (E, 2 * H, D), dtype=jnp.float32) * 0.02
        b1 = jax.random.normal(ks[3], (E, 2 * H), dtype=jnp.float32) * 0.02
        Wo = jax.random.normal(ks[4], (D, H), dtype=jnp.float32) * 0.02
        bo = jax.random.normal(ks[5], (D,), dtype=jnp.float32) * 0.02
        return {'x': x, 'Wg': Wg, 'W1': W1, 'b1': b1, 'Wo': Wo, 'bo': bo}
    _L0_ffn_all = _L0_ffn_setup()
    _L0_ffn_in = {k: v for k, v in _L0_ffn_all.items() if k in ('Wg', 'W1', 'b1', 'Wo', 'bo')}
    del _L0_ffn_all

    def _L1_xattn_setup():
        import jax, jax.numpy as jnp
        import numpy as np
        NUM_HEAD = 16
        LN_EPS = 1e-05

        def _layernorm(x, g, b):
            m = jnp.mean(x, axis=-1, keepdims=True)
            v = jnp.var(x, axis=-1, keepdims=True)
            return (x - m) * jax.lax.rsqrt(v + LN_EPS) * g + b
        B, T, N, D, L = (32, 64, 77, 128, 96)
        ks = jax.random.split(jax.random.key(seed), 6)
        s = 0.02
        return {'x': jax.random.normal(ks[0], (B, T, D), jnp.float32), 'xf': jax.random.normal(ks[1], (B, N, L), jnp.float32), 'q_w': jax.random.normal(ks[2], (D, D), jnp.float32) * s, 'q_b': jnp.zeros((D,), jnp.float32), 'k_w': jax.random.normal(ks[3], (L, D), jnp.float32) * s, 'k_b': jnp.zeros((D,), jnp.float32), 'v_w': jax.random.normal(ks[4], (L, D), jnp.float32) * s, 'v_b': jnp.zeros((D,), jnp.float32), 'ln_g': jnp.ones((D,), jnp.float32), 'ln_b': jnp.zeros((D,), jnp.float32), 'tln_g': jnp.ones((L,), jnp.float32), 'tln_b': jnp.zeros((L,), jnp.float32)}
    _L1_xattn_all = _L1_xattn_setup()
    _L1_xattn_in = {k: v for k, v in _L1_xattn_all.items() if k in ('q_w', 'q_b', 'k_w', 'k_b', 'v_w', 'v_b', 'ln_g', 'ln_b', 'tln_g', 'tln_b')}
    del _L1_xattn_all

    def _L1_ffn_setup():
        import jax, jax.numpy as jnp
        import numpy as np
        QMAX = 127.0

        def _ste_round(v):
            return v + jax.lax.stop_gradient(jnp.round(v) - v)

        def _act_fake_quant(x, clip_factor):
            scale = jax.nn.sigmoid(clip_factor) * jnp.max(jnp.abs(x)) / QMAX
            return jnp.clip(_ste_round(x / scale), -QMAX - 1.0, QMAX) * scale

        def _weight_fake_quant(w):
            scale = jnp.max(jnp.abs(w), axis=1, keepdims=True) / QMAX
            return jnp.clip(_ste_round(w / scale), -QMAX - 1.0, QMAX) * scale
        key = jax.random.key(seed)
        k1, k2, k3, k4 = jax.random.split(key, 4)
        B, S, H, I = (8, 1024, 128, 352)
        return {'x': jax.random.normal(k1, (B, S, H), dtype=jnp.float32), 'clip_x': jnp.full((1,), 4.0, dtype=jnp.float32), 'clip_down': jnp.full((1,), 4.0, dtype=jnp.float32), 'w_gate': jax.random.normal(k2, (I, H), dtype=jnp.float32) * 0.02, 'w_up': jax.random.normal(k3, (I, H), dtype=jnp.float32) * 0.02, 'w_down': jax.random.normal(k4, (H, I), dtype=jnp.float32) * 0.02}
    _L1_ffn_all = _L1_ffn_setup()
    _L1_ffn_in = {k: v for k, v in _L1_ffn_all.items() if k in ('clip_x', 'clip_down', 'w_gate', 'w_up', 'w_down')}
    del _L1_ffn_all
    return {'x': x, 'ctx_768': ctx_768, 'L0_xattn_Wq': _L0_xattn_in['Wq'], 'L0_xattn_Wk': _L0_xattn_in['Wk'], 'L0_xattn_Wv': _L0_xattn_in['Wv'], 'L0_xattn_Wo': _L0_xattn_in['Wo'], 'L0_xattn_bo': _L0_xattn_in['bo'], 'L0_ffn_Wg': _L0_ffn_in['Wg'], 'L0_ffn_W1': _L0_ffn_in['W1'], 'L0_ffn_b1': _L0_ffn_in['b1'], 'L0_ffn_Wo': _L0_ffn_in['Wo'], 'L0_ffn_bo': _L0_ffn_in['bo'], 'L1_xattn_q_w': _L1_xattn_in['q_w'], 'L1_xattn_q_b': _L1_xattn_in['q_b'], 'L1_xattn_k_w': _L1_xattn_in['k_w'], 'L1_xattn_k_b': _L1_xattn_in['k_b'], 'L1_xattn_v_w': _L1_xattn_in['v_w'], 'L1_xattn_v_b': _L1_xattn_in['v_b'], 'L1_xattn_ln_g': _L1_xattn_in['ln_g'], 'L1_xattn_ln_b': _L1_xattn_in['ln_b'], 'L1_xattn_tln_g': _L1_xattn_in['tln_g'], 'L1_xattn_tln_b': _L1_xattn_in['tln_b'], 'L1_ffn_clip_x': _L1_ffn_in['clip_x'], 'L1_ffn_clip_down': _L1_ffn_in['clip_down'], 'L1_ffn_w_gate': _L1_ffn_in['w_gate'], 'L1_ffn_w_up': _L1_ffn_in['w_up'], 'L1_ffn_w_down': _L1_ffn_in['w_down']}

def reference(x, ctx_768, L0_xattn_Wq, L0_xattn_Wk, L0_xattn_Wv, L0_xattn_Wo, L0_xattn_bo, L0_ffn_Wg, L0_ffn_W1, L0_ffn_b1, L0_ffn_Wo, L0_ffn_bo, L1_xattn_q_w, L1_xattn_q_b, L1_xattn_k_w, L1_xattn_k_b, L1_xattn_v_w, L1_xattn_v_b, L1_xattn_ln_g, L1_xattn_ln_b, L1_xattn_tln_g, L1_xattn_tln_b, L1_ffn_clip_x, L1_ffn_clip_down, L1_ffn_w_gate, L1_ffn_w_up, L1_ffn_w_down):
    import jax
    import jax.numpy as jnp

    def _L0_xattn_ref(x, context, Wq, Wk, Wv, Wo, bo):
        import jax, jax.numpy as jnp
        import numpy as np
        HEADS = 16
        DIM_HEAD = 64
        b, n, _ = x.shape
        h, d = (HEADS, DIM_HEAD)
        scale = d ** (-0.5)
        q = (x @ Wq).reshape(b, n, h, d).transpose(0, 2, 1, 3)
        k = (context @ Wk).reshape(b, -1, h, d).transpose(0, 2, 1, 3)
        v = (context @ Wv).reshape(b, -1, h, d).transpose(0, 2, 1, 3)
        sim = jnp.einsum('bhid,bhjd->bhij', q, k) * scale
        attn = jax.nn.softmax(sim, axis=-1)
        out = jnp.einsum('bhij,bhjd->bhid', attn, v)
        out = out.transpose(0, 2, 1, 3).reshape(b, n, h * d)
        return out @ Wo + bo

    def _L0_ffn_ref(x, Wg, W1, b1, Wo, bo):
        import jax, jax.numpy as jnp
        import numpy as np
        TOP_K = 2
        EPS = 1e-09
        E = Wg.shape[0]
        gate_logits = jnp.einsum('btd,ed->bte', x, Wg)
        gate_scores = jax.nn.softmax(gate_logits, axis=-1)
        topk_val, topk_idx = jax.lax.top_k(gate_scores, TOP_K)
        topk_val = topk_val / (topk_val.sum(axis=-1, keepdims=True) + EPS)
        comb = (jax.nn.one_hot(topk_idx, E, dtype=x.dtype) * topk_val[..., None]).sum(axis=-2)
        out = jnp.zeros_like(x)
        for e in range(E):
            h = jnp.einsum('btd,hd->bth', x, W1[e]) + b1[e]
            a, b = jnp.split(h, 2, axis=-1)
            g = a * jax.nn.sigmoid(b)
            eo = jnp.einsum('bth,dh->btd', g, Wo) + bo
            out = out + eo * comb[..., e:e + 1]
        return out

    def _L1_xattn_ref(x, xf, q_w, q_b, k_w, k_b, v_w, v_b, ln_g, ln_b, tln_g, tln_b):
        import jax, jax.numpy as jnp
        import numpy as np
        NUM_HEAD = 16
        LN_EPS = 1e-05

        def _layernorm(x, g, b):
            m = jnp.mean(x, axis=-1, keepdims=True)
            v = jnp.var(x, axis=-1, keepdims=True)
            return (x - m) * jax.lax.rsqrt(v + LN_EPS) * g + b
        B, T, D = x.shape
        N = xf.shape[1]
        H = NUM_HEAD
        dh = D // H
        xn = _layernorm(x, ln_g, ln_b)
        xfn = _layernorm(xf, tln_g, tln_b)
        q = (xn @ q_w + q_b).reshape(B, T, H, dh)
        k = (xfn @ k_w + k_b).reshape(B, N, H, dh)
        v = (xfn @ v_w + v_b).reshape(B, N, H, dh)
        att = jnp.einsum('bthd,bnhd->btnh', q, k) / np.float32(np.sqrt(dh))
        w = jax.nn.softmax(att, axis=2)
        y = jnp.einsum('btnh,bnhd->bthd', w, v).reshape(B, T, D)
        return y

    def _L1_ffn_ref(x, clip_x, clip_down, w_gate, w_up, w_down):
        import jax, jax.numpy as jnp
        import numpy as np
        QMAX = 127.0

        def _ste_round(v):
            return v + jax.lax.stop_gradient(jnp.round(v) - v)

        def _act_fake_quant(x, clip_factor):
            scale = jax.nn.sigmoid(clip_factor) * jnp.max(jnp.abs(x)) / QMAX
            return jnp.clip(_ste_round(x / scale), -QMAX - 1.0, QMAX) * scale

        def _weight_fake_quant(w):
            scale = jnp.max(jnp.abs(w), axis=1, keepdims=True) / QMAX
            return jnp.clip(_ste_round(w / scale), -QMAX - 1.0, QMAX) * scale
        xq = _act_fake_quant(x, clip_x[0])
        gate = jnp.einsum('bsh,ih->bsi', xq, _weight_fake_quant(w_gate))
        up = jnp.einsum('bsh,ih->bsi', xq, _weight_fake_quant(w_up))
        h = _act_fake_quant(jax.nn.silu(gate) * up, clip_down[0])
        return jnp.einsum('bsi,hi->bsh', h, _weight_fake_quant(w_down))
    x = x + _L0_xattn_ref(_layernorm(x, axis=-1), ctx_768, L0_xattn_Wq, L0_xattn_Wk, L0_xattn_Wv, L0_xattn_Wo, L0_xattn_bo)
    x = x + _L0_ffn_ref(_layernorm(x, axis=-1), L0_ffn_Wg, L0_ffn_W1, L0_ffn_b1, L0_ffn_Wo, L0_ffn_bo)
    x = x + _L1_xattn_ref(_layernorm(x, axis=-1), ctx_768, L1_xattn_q_w, L1_xattn_q_b, L1_xattn_k_w, L1_xattn_k_b, L1_xattn_v_w, L1_xattn_v_b, L1_xattn_ln_g, L1_xattn_ln_b, L1_xattn_tln_g, L1_xattn_tln_b)
    x = x + _L1_ffn_ref(_layernorm(x, axis=-1), L1_ffn_clip_x, L1_ffn_clip_down, L1_ffn_w_gate, L1_ffn_w_up, L1_ffn_w_down)
    return x

_drawn_inputs = setup_inputs


def setup_inputs(seed=0):
    import zlib

    import numpy as np

    out = dict(_drawn_inputs(seed))
    spreads = {'L1_xattn_q_b': (0.0, 0.8),
     'L1_xattn_k_b': (0.0, 0.8),
     'L1_xattn_v_b': (0.0, 0.1),
     'L1_xattn_ln_g': (1.0, 0.6),
     'L1_xattn_ln_b': (0.0, 0.8),
     'L1_xattn_tln_g': (1.0, 0.6),
     'L1_xattn_tln_b': (0.0, 0.474)}
    factors = {'L0_xattn_bo': 5.909,
     'L0_ffn_Wg': 2.827,
     'L0_ffn_b1': 8.0,
     'L0_ffn_bo': 2.782,
     'L1_xattn_q_w': 8.0,
     'L1_xattn_k_w': 8.0,
     'L1_ffn_w_gate': 6.465,
     'L1_ffn_w_up': 6.161,
     'L1_ffn_w_down': 6.222}
    for name, (base, spread) in spreads.items():
        noise = np.random.default_rng([zlib.crc32(name.encode()), seed]).standard_normal(out[name].shape)
        drawn = base * np.exp(spread * noise) if base else spread * noise
        out[name] = jnp.asarray(drawn.astype(out[name].dtype))
    for name, factor in factors.items():
        out[name] = (out[name] * factor).astype(out[name].dtype)
    return out
```

```python
from contextlib import ExitStack

import concourse.bass as bass
from concourse import mybir

F32 = mybir.dt.float32
F16 = mybir.dt.float16
BF16 = mybir.dt.bfloat16
ALU = mybir.AluOpType
ACT = mybir.ActivationFunctionType
AX = mybir.AxisListType

P = 128
B = 8
S = 256
QT = S // P
NT = B * QT
N = B * S
D = 128
C = 96
H0 = 16
DH0 = 64
E = 8
HF = 256
HG = H0 // 4
H1 = 16
DH1 = D // H1
FF = 352
LN_EPS = 1e-5
W_SCALE = 64.0
MAGIC = 12582912.0
QMAX = 127.0
FT = -(-FF // P)
U = B * H0


def wait(eng, semaphore, value):
    if not isinstance(value, int) or value > 0:
        eng.wait_ge(semaphore, value)


def cross_ffn_network(nc, x, ctx_tok, ctx_t, l0_wq_t, l0_wk_t, l0_wv, l0_wo, l0_bo, f0_wg, f0_w1, f0_b1,
                      f0_wo_t, f0_bo, l1_qw, l1_qb, l1_kw, l1_kb, l1_vw, l1_vb, l1_g, l1_b, l1_tg, l1_tb,
                      f1_cx, f1_cd, f1_wg, f1_wu, f1_wd, out):
    with ExitStack() as ctx:
        def sb(name, shape, dt=F32):
            return ctx.enter_context(nc.sbuf_tensor(name, shape, dt))

        def sem(name):
            return ctx.enter_context(nc.semaphore(name))

        banks = [ctx.enter_context(nc.psum_tensor(f"bank{i}", [P, 512], F32)) for i in range(8)]

        height = [min(P, FF - P * i) for i in range(FT)]

        xres = sb("xres", [P, NT, D])
        ident = sb("ident", [P, P])
        ctx_halves = sb("ctx_halves", [P, 2 * N], F16)
        ctx_hi, ctx_lo = ctx_halves[:, 0:N], ctx_halves[:, N:2 * N]
        zt_halves = sb("zt_halves", [P, 2 * N], F16)
        zt_hi, zt_lo = zt_halves[:, 0:N], zt_halves[:, N:2 * N]
        m_hi = sb("m_hi", [P, H0, C], F16)
        m_lo = sb("m_lo", [P, H0, C], F16)
        bo_bc = sb("bo_bc", [P, D])
        wo = sb("wo", [P, H0 // 2, D])
        stats = sb("stats", [P, NT, 6])
        mv = sb("mv", [P, NT, 2])
        var_eps = sb("var_eps", [P, NT])
        rstd = sb("rstd", [P, NT])
        minus_half = sb("minus_half", [P, NT])
        eps_add = sb("eps_add", [P, NT])
        gate = sb("gate", [P, NT, E])
        fbo_bc = sb("fbo_bc", [P, D])
        fwo_t = sb("fwo_t", [P, HF // P, D])
        gu_max = sb("gu_max", [P, 2, FT])
        gu_scale = sb("gu_scale", [P, 2, FT])
        gu_inv = sb("gu_inv", [P, 2, FT])
        wd_max = sb("wd_max", [D, 1])
        wd_scale = sb("wd_scale", [D, 1])
        wd_inv = sb("wd_inv", [D, 1])
        arena_v = sb("arena_v", [P, NT * H0 * (2 * DH0 + 1)], F16)
        arena_o = sb("arena_o", [P, NT * H0 * DH0])
        v_hi = arena_v[:, 0:NT * H0 * (DH0 + 1)].rearrange("p (t h d) -> p t h d", t=NT, h=H0)
        v_lo = arena_v[:, NT * H0 * (DH0 + 1):].rearrange("p (t h d) -> p t h d", t=NT, h=H0)
        o_all = arena_o[:, :].rearrange("p (t h d) -> p t h d", t=NT, h=H0)

        at = 0

        def temp(width):
            nonlocal at
            at += width
            return arena_o[:, at - width:at]

        wq_t = temp(H0 * P).rearrange("p (h d) -> p h d", h=H0)
        wk_t = temp(H0 * P).rearrange("p (h c) -> p h c", h=H0)
        ctx_raw = temp(N)
        wv_raw = temp(H0 * DH0)
        z0 = temp(NT * D).rearrange("p (t d) -> p t d", t=NT)
        wv_hi = temp(H0 * DH0 // 2).bitcast(F16)
        wv_lo = temp(H0 * DH0 // 2).bitcast(F16)

        ld_x, ld_ctx, ld_wq, ld_wk, ld_wv, ld_wo = (sem(f"ld_{n}") for n in ("x", "ctx", "wq", "wk", "wv", "wo"))
        pads, idents, ones_set, consts = sem("pads"), sem("idents"), sem("ones_set"), sem("consts")
        st0, mv0, ve0, rs0, z0_ready = (sem(n) for n in ("st0", "mv0", "ve0", "rs0", "z0_ready"))
        ctx_hi_ready, ctx_lo_ready, wv_hi_ready, wv_lo_ready = (
            sem(n) for n in ("ctx_hi_ready", "ctx_lo_ready", "wv_hi_ready", "wv_lo_ready"))
        p0_mm, p0_hi, p0_lo = sem("p0_mm"), sem("p0_hi"), sem("p0_lo")
        bo_added = sem("bo_added")
        NM = H0 // 4
        NV = NT * 2
        Z_AT = NM + NV
        HH = H0 // 2

        with nc.Block() as block:
            @block.sync
            def _(sp):
                sp.dma_start(xres[:, :, :], x).then_inc(ld_x, 16)
                sp.dma_start(ctx_raw[0:C, :], ctx_t).then_inc(ld_ctx, 16)
                sp.dma_start(wv_raw[0:C, :], l0_wv).then_inc(ld_wv, 16)
                sp.dma_start(wq_t[0:DH0, :, :], l0_wq_t).then_inc(ld_wq, 16)
                sp.dma_start(wk_t[0:DH0, :, 0:C], l0_wk_t).then_inc(ld_wk, 16)
                sp.dma_start(wo[:, :, :], l0_wo).then_inc(ld_wo, 16)
                sp.dma_start(bo_bc[:, :], l0_bo.partition_broadcast(P)).then_inc(ld_wo, 16)

            @block.gpsimd
            def _(pool):
                nc.gpsimd.memset(minus_half[:, :], -0.5).then_inc(consts, 1)
                nc.gpsimd.memset(ident[:, :], 0.0).then_inc(idents, 1)
                pool.wait_ge(idents, 1)
                nc.gpsimd.affine_select(out=ident[:, :], in_=ident[:, :], compare_op=ALU.not_equal, fill=1.0,
                                        base=0, pattern=[[-1, P]], channel_multiplier=1).then_inc(idents, 1)
                pool.wait_ge(ve0, 1)
                pool.wait_ge(consts, 1)
                nc.gpsimd.tensor_tensor(rstd[:, :], var_eps[:, :], minus_half[:, :], ALU.pow).then_inc(rs0, 1)
                pool.wait_ge(z0_ready, NT)
                pool.wait_ge(ld_wo, 32)
                nc.gpsimd.tensor_tensor(xres[:, :, :], xres[:, :, :],
                                        bo_bc[:, :].unsqueeze(1).to_broadcast([P, NT, D]),
                                        ALU.add).then_inc(bo_added, 1)

            @block.scalar
            def _(act):
                act.wait_ge(ld_ctx, 16)
                nc.scalar.activation(ctx_hi[0:C, :], ctx_raw[0:C, :], ACT.Copy).then_inc(ctx_hi_ready, 1)
                act.wait_ge(ld_wv, 16)
                nc.scalar.activation(wv_hi[0:C, :], wv_raw[0:C, :], ACT.Copy).then_inc(wv_hi_ready, 1)
                for n in range(NM):
                    act.wait_ge(p0_mm, n + 1)
                    nc.scalar.activation(m_hi[:, 4 * n:4 * n + 4, :],
                                         banks[n % 8][:, :].rearrange("p (h c) -> p h c", h=4)[:, :, 0:C],
                                         ACT.Copy).then_inc(p0_hi, 1)

                def value_halves(k):
                    for j in range(8):
                        act.wait_ge(p0_mm, k * 8 + (NM + j + 1))
                        nc.scalar.activation(v_hi[:, k * 4 + j // 2, HH * (j % 2):HH * (j % 2) + HH, 0:DH0],
                                             banks[(NM + j) % 8][:, :].rearrange("p (h d) -> p h d", h=HH),
                                             ACT.Copy).then_inc(p0_hi, 1)
                with act.Fori(0, NV // 8) as k:
                    value_halves(k)
                for n in range(NT // 4):
                    act.wait_ge(p0_mm, Z_AT + n + 1)
                    nc.scalar.activation(zt_hi[:, 512 * n:512 * n + 512], banks[(Z_AT + n) % 8][:, :],
                                         ACT.Copy).then_inc(p0_hi, 1)

            @block.vector
            def _(dve):
                nc.vector.memset(wq_t[DH0:P, :, :], 0.0).then_inc(pads, 1)
                nc.vector.memset(wk_t[DH0:P, :, :], 0.0).then_inc(pads, 1)
                nc.vector.memset(wk_t[0:DH0, :, C:P], 0.0).then_inc(pads, 1)
                nc.vector.memset(ctx_hi[C:C + 1, :], 1.0).then_inc(ones_set, 1)
                nc.vector.memset(v_hi[:, :, :, DH0:DH0 + 1], 1.0).then_inc(ones_set, 1)
                dve.wait_ge(ld_x, 16)
                for t in range(NT):
                    nc.vector.bn_stats(stats[:, t, :], xres[:, t, :]).then_inc(st0, 1)
                for t in range(NT):
                    dve.wait_ge(st0, t + 1)
                    nc.vector.bn_aggr(mv[:, t, :], stats[:, t, :]).then_inc(mv0, 1)
                dve.wait_ge(mv0, NT)
                nc.vector.tensor_scalar(var_eps[:, :], mv[:, :, 1], LN_EPS, None, ALU.add).then_inc(ve0, 1)
                dve.wait_ge(ctx_hi_ready, 1)
                nc.vector.tensor_tensor(ctx_lo[0:C, :], ctx_raw[0:C, :], ctx_hi[0:C, :],
                                        ALU.subtract).then_inc(ctx_lo_ready, 1)
                dve.wait_ge(wv_hi_ready, 1)
                nc.vector.tensor_tensor(wv_lo[0:C, :], wv_raw[0:C, :], wv_hi[0:C, :],
                                        ALU.subtract).then_inc(wv_lo_ready, 1)
                dve.wait_ge(rs0, 1)
                for t in range(NT):
                    nc.vector.tensor_scalar(z0[:, t, :], xres[:, t, :], mv[:, t, 0:1], rstd[:, t:t + 1],
                                            ALU.subtract, ALU.mult).then_inc(z0_ready, 1)
                for n in range(NM):
                    dve.wait_ge(p0_hi, n + 1)
                    nc.vector.tensor_tensor(m_lo[:, 4 * n:4 * n + 4, :],
                                            banks[n % 8][:, :].rearrange("p (h c) -> p h c", h=4)[:, :, 0:C],
                                            m_hi[:, 4 * n:4 * n + 4, :], ALU.subtract).then_inc(p0_lo, 1)
                with dve.Fori(0, NV // 8) as k:
                    for j in range(8):
                        heads = slice(HH * (j % 2), HH * (j % 2) + HH)
                        dve.wait_ge(p0_hi, k * 8 + (NM + j + 1))
                        nc.vector.tensor_tensor(v_lo[:, k * 4 + j // 2, heads, :],
                                                banks[(NM + j) % 8][:, :].rearrange("p (h d) -> p h d", h=HH),
                                                v_hi[:, k * 4 + j // 2, heads, 0:DH0],
                                                ALU.subtract).then_inc(p0_lo, 1)
                for n in range(NT // 4):
                    dve.wait_ge(p0_hi, Z_AT + n + 1)
                    nc.vector.tensor_tensor(zt_lo[:, 512 * n:512 * n + 512], banks[(Z_AT + n) % 8][:, :],
                                            zt_hi[:, 512 * n:512 * n + 512], ALU.subtract).then_inc(p0_lo, 1)

            @block.tensor
            def _(pe):
                pe.wait_ge(ld_wq, 16)
                pe.wait_ge(ld_wk, 16)
                pe.wait_ge(pads, 3)
                for h in range(H0):
                    last = nc.tensor.matmul(banks[h // 4][:, P * (h % 4):P * (h % 4) + P],
                                            wq_t[:, h, :], wk_t[:, h, :], start=True, stop=True)
                    if h % 4 == 3:
                        last.then_inc(p0_mm, 1)
                pe.wait_ge(ctx_lo_ready, 1)
                pe.wait_ge(wv_lo_ready, 1)

                def values(k):
                    for j in range(8):
                        wait(pe, p0_lo, k * 8 + (NM + j - 7))
                        tokens = bass.ds(k * 512 + (j // 2) * P, P)
                        heads = slice(512 * (j % 2), 512 * (j % 2) + 512)
                        bank = banks[(NM + j) % 8]
                        nc.tensor.matmul(bank[:, :], ctx_hi[0:C, tokens], wv_hi[0:C, heads], start=True, stop=False)
                        nc.tensor.matmul(bank[:, :], ctx_lo[0:C, tokens], wv_hi[0:C, heads], start=False, stop=False)
                        nc.tensor.matmul(bank[:, :], ctx_hi[0:C, tokens], wv_lo[0:C, heads], start=False,
                                         stop=True).then_inc(p0_mm, 1)
                values(0)
                with pe.Fori(1, NV // 8) as k:
                    values(k)
                pe.wait_ge(idents, 2)
                pe.wait_ge(z0_ready, NT)
                for n in range(NT // 4):
                    wait(pe, p0_lo, Z_AT + n - 7)
                    for j in range(4):
                        last = nc.tensor.transpose(banks[(Z_AT + n) % 8][:, P * j:P * j + P], z0[:, 4 * n + j, :],
                                                   ident[:, :])
                    last.then_inc(p0_mm, 1)

        scratch = ExitStack()

        def sb1(name, shape, dt=F32):
            return scratch.enter_context(nc.sbuf_tensor(name, shape, dt))

        RING = 4
        t_hi = sb1("t_hi", [P, H0, S], F16)
        t_lo = sb1("t_lo", [P, H0, S], F16)
        p32 = sb1("p32", [P, 2, QT * S])
        p_hi = sb1("p_hi", [P, RING, QT * S], F16)
        p_lo = sb1("p_lo", [P, RING, QT * S], F16)
        neg_max = sb1("neg_max", [P, 2, 4 * QT])
        neg_max_t = sb1("neg_max_t", [4 * QT, 2, P], F16)
        rsum = sb1("rsum", [P, 2, QT, 2])
        t_bank, max_bank, score_bank, o_bank = banks[0:2], banks[2:4], banks[4:6], banks[6:8]
        SHIFT_AT = 384
        LEAD_T, LEAD_MAX, LEAD_SHIFT = 12, 10, 5
        LAG_PV = 2
        SCALE0 = DH0 ** -0.5

        t_done, t_hi_ready, t_lo_ready, max_done, max_read = (
            sem(n) for n in ("t_done", "t_hi_ready", "t_lo_ready", "max_done", "max_read"))
        shift_in_psum, shift_read, scores_done, hi_ready, p32_ready, lo_ready, pv_done, sum_inverted, o_read = (
            sem(n) for n in ("shift_in_psum", "shift_read", "scores_done", "hi_ready", "p32_ready", "lo_ready",
                             "pv_done", "sum_inverted", "o_read"))
        shift_row = [sem("shift_row_even"), sem("shift_row_odd")]

        def steps(eng, step):
            for s in range(-LEAD_T, 4):
                step(0, s)
            with eng.Fori(0, B - 1) as b:
                for s in range(4, 4 + H0):
                    step(b, s)
            for s in range(4, H0 + 5):
                step(B - 1, s)

        def there(b, s):
            return not isinstance(b, int) or 0 <= H0 * b + s < U

        def count(b, s):
            return b * H0 + s

        with nc.Block() as block:
            @block.tensor
            def _(pe):
                def make_t(b, s):
                    if s % 2 == 0:
                        wait(pe, t_lo_ready, count(b, s) // 2 - 1 if isinstance(b, int) else b * 8 + (s // 2 - 1))
                    tokens = bass.ds((b + s // H0) * S, S)
                    h = s % H0
                    dst = t_bank[(s // 2) % 2][0:C, S * (s % 2):S * (s % 2) + S]
                    nc.tensor.matmul(dst, m_hi[:, h, :], zt_hi[:, tokens], start=True, stop=False)
                    nc.tensor.matmul(dst, m_hi[:, h, :], zt_lo[:, tokens], start=False, stop=False)
                    nc.tensor.matmul(dst, m_lo[:, h, :], zt_hi[:, tokens], start=False, stop=True).then_inc(t_done, 1)

                def maxima(b, s):
                    pe.wait_ge(t_hi_ready, b * 8 + (s // 2 + 1))
                    wait(pe, max_read, count(b, s) - 1)
                    keys = bass.ds((b + s // H0) * S, S)
                    for q in range(QT):
                        last = nc.tensor.matmul(max_bank[s % 2][:, S * q:S * q + S],
                                                t_hi[0:C, s % H0, P * q:P * q + P], ctx_hi[0:C, keys],
                                                start=True, stop=True)
                    last.then_inc(max_done, 1)

                def shift(b, s):
                    pe.wait_ge(max_read, count(b, s) + 4)
                    wait(pe, shift_read, b * 4 + s // 4)
                    nc.tensor.transpose(o_bank[0][0:4 * QT, SHIFT_AT:SHIFT_AT + P], neg_max[:, (s // 4) % 2, :],
                                        ident[:, :]).then_inc(shift_in_psum, 1)

                def scores(b, s):
                    if s % 4 == 0:
                        pe.wait_ge(shift_row[(s // 4) % 2], b * 32 + 16 * (s // 8 + 1))
                    wait(pe, p32_ready, count(b, s) - 1)
                    h = s % H0
                    if s % 2 == 0:
                        pe.wait_ge(t_lo_ready, b * 8 + (s // 2 + 1))
                    for k in range(QT):
                        dst = score_bank[s % 2][:, S * k:S * k + S]
                        keys = bass.ds((b + s // H0) * S + P * k, P)
                        nc.tensor.matmul(dst, ctx_hi[0:C + 1, keys], t_hi[0:C + 1, h, :], start=True, stop=False)
                        nc.tensor.matmul(dst, ctx_hi[0:C, keys], t_lo[0:C, h, :], start=False, stop=False)
                        last = nc.tensor.matmul(dst, ctx_lo[0:C, keys], t_hi[0:C, h, :], start=False, stop=True)
                    last.then_inc(scores_done, 1)

                def values(b, s):
                    r, h, left = s % RING, s % H0, s % 2
                    if s % 2 == 0:
                        wait(pe, o_read, (count(b, s) // 2 - 1) if isinstance(b, int) else b * 8 + (s // 2 - 1))
                    pe.wait_ge(lo_ready, count(b, s) + 1)
                    for q in range(QT):
                        c0 = (DH0 + 1) * (2 * q + left)
                        dst = o_bank[(s // 2) % 2][:, c0:c0 + DH0 + 1]
                        for k in range(QT):
                            tile = b * QT + (s // H0 * QT + k)
                            w = slice(S * k + P * q, S * k + P * q + P)
                            nc.tensor.matmul(dst, p_hi[:, r, w], v_hi[:, tile, h, :], start=(k == 0), stop=False)
                            nc.tensor.matmul(dst[:, 0:DH0], p_hi[:, r, w], v_lo[:, tile, h, :], start=False, stop=False)
                            last = nc.tensor.matmul(dst, p_lo[:, r, w], v_hi[:, tile, h, :], start=False,
                                                    stop=(k == QT - 1))
                    last.then_inc(pv_done, 1)

                def step(b, s):
                    if there(b, s):
                        scores(b, s)
                    if there(b, s + LEAD_T):
                        make_t(b, s + LEAD_T)
                    if there(b, s + LEAD_MAX):
                        maxima(b, s + LEAD_MAX)
                    if (s + LEAD_SHIFT) % 4 == 0 and there(b, s + LEAD_SHIFT):
                        shift(b, s + LEAD_SHIFT)
                    if there(b, s - LAG_PV):
                        values(b, s - LAG_PV)
                steps(pe, step)

            @block.scalar
            def _(act):
                def exps(b, s):
                    r = s % 2
                    act.wait_ge(scores_done, count(b, s) + 1)
                    wait(act, pv_done, count(b, s) + 1 - RING)
                    nc.scalar.activation(p_hi[:, s % RING, :], score_bank[r][:, :], ACT.Exp, scale=SCALE0).then_inc(hi_ready, 1)
                    wait(act, lo_ready, count(b, s) - 1)
                    nc.scalar.activation(p32[:, r, :], score_bank[r][:, :], ACT.Exp, scale=SCALE0).then_inc(p32_ready, 1)

                def t_halves(b, s):
                    act.wait_ge(t_done, count(b, s) + 1)
                    wait(act, scores_done, count(b, s) + 1 - H0)
                    h = (s - 1) % H0
                    nc.scalar.activation(t_hi[0:C, h:h + 2, :],
                                         t_bank[(s // 2) % 2][0:C, :].rearrange("p (h q) -> p h q", h=2),
                                         ACT.Copy).then_inc(t_hi_ready, 1)

                def step(b, s):
                    if there(b, s):
                        exps(b, s)
                    if s % 2 == 1 and there(b, s + LEAD_T):
                        t_halves(b, s + LEAD_T)
                steps(act, step)

            @block.gpsimd
            def _(pool):
                def step(b, s):
                    if there(b, s):
                        r = s % RING
                        pool.wait_ge(p32_ready, count(b, s) + 1)
                        wait(pool, pv_done, count(b, s) + 1 - RING)
                        nc.gpsimd.tensor_tensor(p_lo[:, r, :], p32[:, s % 2, :], p_hi[:, r, :],
                                                ALU.subtract).then_inc(lo_ready, 1)
                steps(pool, step)

            @block.vector
            def _(dve):
                def t_rest(b, s):
                    pair = b * 8 + ((s - 1) // 2)
                    h = (s - 1) % H0
                    dve.wait_ge(t_hi_ready, pair + 1)
                    nc.vector.tensor_tensor(t_lo[0:C, h:h + 2, :],
                                            t_bank[(s // 2) % 2][0:C, :].rearrange("p (h q) -> p h q", h=2),
                                            t_hi[0:C, h:h + 2, :], ALU.subtract).then_inc(t_lo_ready, 1)

                def max_of(b, s):
                    g, j = (s // 4) % 2, s % 4
                    dve.wait_ge(max_done, count(b, s) + 1)
                    if j == 0:
                        wait(dve, shift_in_psum, (count(b, s) // 4 - 1) if isinstance(b, int) else b * 4 + (s // 4 - 1))
                    nc.vector.tensor_reduce(neg_max[:, g, QT * j:QT * j + QT],
                                            max_bank[s % 2][:, :].rearrange("p (q k) -> p q k", q=QT),
                                            AX.X, ALU.max, negate=True).then_inc(max_read, 1)

                def shift_out(b, s):
                    g = (s // 4) % 2
                    dve.wait_ge(shift_in_psum, b * 4 + (s // 4 + 1))
                    before = b * 32 + 16 * (s // 8)
                    wait(dve, shift_row[g], before)
                    nc.vector.tensor_copy(neg_max_t[:, g, :], o_bank[0][0:4 * QT, SHIFT_AT:SHIFT_AT + P])\
                        .then_inc(shift_read, 1)

                def output(b, s):
                    pair = b * 8 + (s // 2)
                    g, h = (s // 2) % 2, (s - 1) % H0
                    dve.wait_ge(pv_done, count(b, s) + 1)
                    o = o_bank[g][:, 0:QT * 2 * (DH0 + 1)].rearrange("p (q h d) -> p q h d", q=QT, h=2)
                    nc.vector.reciprocal(rsum[:, g, :, :], o[:, :, :, DH0]).then_inc(sum_inverted, 1)
                    dve.wait_ge(sum_inverted, pair + 1)
                    nc.vector.tensor_tensor(o_all[:, bass.ds((b + s // H0) * QT, QT), h:h + 2, :], o[:, :, :, 0:DH0],
                                            rsum[:, g, :, :].unsqueeze(3).to_broadcast([P, QT, 2, DH0]),
                                            ALU.mult).then_inc(o_read, 1)

                def step(b, s):
                    if s % 2 == 1 and there(b, s + LEAD_T):
                        t_rest(b, s + LEAD_T)
                    if there(b, s + LEAD_MAX):
                        max_of(b, s + LEAD_MAX)
                    if (s + LEAD_SHIFT) % 4 == 0 and there(b, s + LEAD_SHIFT):
                        if there(b, s - LAG_PV):
                            dve.wait_ge(pv_done, count(b, s - LAG_PV) + 1)
                        shift_out(b, s + LEAD_SHIFT)
                    if (s - LAG_PV) % 2 == 1 and there(b, s - LAG_PV):
                        output(b, s - LAG_PV)
                steps(dve, step)

            @block.sync
            def _(sp):
                def step(b, s):
                    if (s + LEAD_SHIFT) % 4 == 0 and there(b, s + LEAD_SHIFT):
                        u = s + LEAD_SHIFT
                        g, h = (u // 4) % 2, u % H0
                        sp.wait_ge(shift_read, b * 4 + (u // 4 + 1))
                        sp.dma_start(t_hi[C:C + 1, h:h + 4, :], neg_max_t[:, g, :]).then_inc(shift_row[g], 16)
                steps(sp, step)

        scratch.close()

        scratch = ExitStack()
        at = 0

        def temp_v(width):
            nonlocal at
            at += width
            return arena_v[:, 2 * (at - width):2 * at].bitcast(F32)

        w1_raw = temp_v(E * HG * D).rearrange("p (r d) -> p r d", d=D)
        w1t_hi = temp_v(E * 2 * HF // 2).bitcast(F16)
        w1t_lo = temp_v(E * 2 * HF // 2).bitcast(F16)
        NR = E * 2 * HF // P
        o_t = sb1("o_t", [P, 2, H0 // 2, P])
        z1 = sb1("z1", [P, 2, D])
        b1_cols = sb1("b1_cols", [P, NR])
        wg_raw = sb1("wg_raw", [E, D])
        wg_shift = sb1("wg_shift", [E, D])
        wgt_hi = sb1("wgt_hi", [P, E], F16)
        wgt_lo = sb1("wgt_lo", [P, E], F16)
        logit_max = sb1("logit_max", [P, NT])
        prob = sb1("prob", [P, NT, E])
        over = sb1("over", [P, NT, E, E])
        over_eq = sb1("over_eq", [P, NT, E, E])
        later = sb1("later", [P, E, E])
        earlier = sb1("earlier", [P, E, E])
        rank = sb1("rank", [P, NT, E])
        esum = sb1("esum", [P, NT])
        einv = sb1("einv", [P, NT])
        csum = sb1("csum", [P, NT])
        y_bank, z_bank, g_bank = banks[4:6], banks[6], banks[7]
        ld_w1, ld_wg, ld_b1, ld_f0 = sem("ld_w1"), sem("ld_wg"), sem("ld_b1"), sem("ld_f0")
        o_t_done, o_front_read, o_back_read, y1_done, x1_ready = (
            sem(n) for n in ("o_t_done", "o_front_read", "o_back_read", "y1_done", "x1_ready"))
        st1, mv1, ve1, rs1, z1_ready, z1t_done, z1_hi_ready, z1_lo_ready, z1_ones = (
            sem(n) for n in ("st1", "mv1", "ve1", "rs1", "z1_ready", "z1t_done", "z1_hi_ready", "z1_lo_ready",
                             "z1_ones"))
        wg_shifted, wgt_done, wgt_hi_ready, wgt_lo_ready, gates_done = (
            sem(n) for n in ("wg_shifted", "wgt_done", "wgt_hi_ready", "wgt_lo_ready", "gates_done"))
        w1_shifted, w1_bias, w1t_done, w1t_hi_ready, w1t_lo_ready = (
            sem(n) for n in ("w1_shifted", "w1_bias", "w1t_done", "w1t_hi_ready", "w1t_lo_ready"))
        masks_set, route, prob_ready = sem("masks_set"), sem("route"), sem("prob_ready")
        LAG_PROJECT, LAG_Z, LAG_ZT, LAG_GATE = 1, 2, 3, 4
        LAST = NT + LAG_GATE

        with nc.Block() as block:
            @block.sync
            def _(sp):
                sp.dma_start(wg_raw[:, :], f0_wg).then_inc(ld_wg, 16)
                sp.dma_start(w1_raw, f0_w1).then_inc(ld_w1, 16)
                sp.dma_start(b1_cols[:, :], f0_b1).then_inc(ld_b1, 16)
                sp.dma_start(fwo_t[:, :, :], f0_wo_t).then_inc(ld_f0, 16)
                sp.dma_start(fbo_bc[:, :], f0_bo.partition_broadcast(P)).then_inc(ld_f0, 16)

            @block.tensor
            def _(pe):
                pe.wait_ge(wg_shifted, 2)
                nc.tensor.transpose(z_bank[:, 0:E], wg_shift[:, :], ident[0:E, 0:E]).then_inc(wgt_done, 1)
                for i in range(LAST):
                    t = i
                    if t < NT:
                        wait(pe, o_front_read, t - 1)
                        wait(pe, o_back_read, t - 1)
                        for c in range(H0 // 2):
                            last = nc.tensor.transpose(
                                banks[2 * (t % 2) + c // 4][:, P * (c % 4):P * (c % 4) + P],
                                arena_o[:, (t * 8 + c) * P:(t * 8 + c) * P + P], ident[:, :])
                        last.then_inc(o_t_done, 1)
                    t = i - LAG_PROJECT
                    if 0 <= t < NT:
                        pe.wait_ge(o_front_read, t + 1)
                        pe.wait_ge(o_back_read, t + 1)
                        wait(pe, x1_ready, t - 1)
                        for c in range(H0 // 2):
                            last = nc.tensor.matmul(y_bank[t % 2][:, 0:D], o_t[:, t % 2, c, :], wo[:, c, :],
                                                    start=(c == 0), stop=(c == H0 // 2 - 1))
                        last.then_inc(y1_done, 1)
                    t = i - LAG_ZT
                    if 0 <= t < NT:
                        pe.wait_ge(z1_ready, t + 1)
                        pe.wait_ge(wgt_lo_ready, 1)
                        wait(pe, z1_lo_ready, t)
                        nc.tensor.transpose(z_bank[:, 0:P], z1[:, t % 2, :], ident[:, :]).then_inc(z1t_done, 1)
                    t = i - LAG_GATE
                    if 0 <= t < NT:
                        pe.wait_ge(z1_lo_ready, t + 1)
                        tokens = slice(P * t, P * t + P)
                        nc.tensor.matmul(g_bank[:, E * t:E * t + E], zt_hi[:, tokens], wgt_hi[:, :], start=True, stop=False)
                        nc.tensor.matmul(g_bank[:, E * t:E * t + E], zt_lo[:, tokens], wgt_hi[:, :], start=False, stop=False)
                        nc.tensor.matmul(g_bank[:, E * t:E * t + E], zt_hi[:, tokens], wgt_lo[:, :], start=False,
                                         stop=True).then_inc(gates_done, 1)
                pe.wait_ge(w1_shifted, NT)
                pe.wait_ge(w1_bias, 1)
                for n in range(NR // 4):
                    wait(pe, w1t_lo_ready, n - 3)
                    for j in range(4):
                        last = nc.tensor.transpose(banks[n % 4][:, P * j:P * j + P], w1_raw[:, 4 * n + j, :], ident[:, :])
                    last.then_inc(w1t_done, 1)

            @block.scalar
            def _(act):
                act.wait_ge(wgt_done, 1)
                nc.scalar.activation(wgt_hi[:, :], z_bank[:, 0:E], ACT.Copy, scale=W_SCALE).then_inc(wgt_hi_ready, 1)
                for i in range(LAST):
                    t = i
                    if t < NT:
                        act.wait_ge(o_t_done, t + 1)
                        wait(act, y1_done, t - 1)
                        nc.scalar.activation(o_t[:, t % 2, 0:4, :],
                                             banks[2 * (t % 2)][:, :].rearrange("p (c q) -> p c q", c=4),
                                             ACT.Copy).then_inc(o_front_read, 1)
                    t = i - LAG_ZT
                    if 0 <= t < NT:
                        act.wait_ge(z1t_done, t + 1)
                        nc.scalar.activation(zt_hi[:, P * t:P * t + P], z_bank[:, 0:P], ACT.Copy).then_inc(z1_hi_ready, 1)
                for n in range(NR // 4):
                    act.wait_ge(w1t_done, n + 1)
                    nc.scalar.activation(w1t_hi[:, 512 * n:512 * n + 512], banks[n % 4][:, :], ACT.Copy,
                                         scale=W_SCALE).then_inc(w1t_hi_ready, 1)
                act.wait_ge(route, 2)
                nc.scalar.activation(prob[:, :, :], prob[:, :, :], ACT.Exp, scale=1.0 / W_SCALE).then_inc(prob_ready, 1)

            @block.gpsimd
            def _(pool):
                nc.gpsimd.memset(later[:, :, :], 1.0).then_inc(masks_set, 1)
                nc.gpsimd.memset(earlier[:, :, :], 1.0).then_inc(masks_set, 1)
                pool.wait_ge(masks_set, 2)
                nc.gpsimd.affine_select(out=later[:, :, :], in_=later[:, :, :], compare_op=ALU.is_ge, fill=0.0,
                                        base=0, pattern=[[-1, E], [1, E]], channel_multiplier=0).then_inc(masks_set, 1)
                nc.gpsimd.affine_select(out=earlier[:, :, :], in_=earlier[:, :, :], compare_op=ALU.is_gt, fill=0.0,
                                        base=0, pattern=[[1, E], [-1, E]], channel_multiplier=0).then_inc(masks_set, 1)
                for t in range(NT):
                    if t == 0:
                        pool.wait_ge(ld_w1, 16)
                    rows = slice(2 * t, 2 * t + 2)
                    nc.gpsimd.tensor_tensor(w1_raw[:, rows, 0:D - 1], w1_raw[:, rows, 0:D - 1],
                                            w1_raw[:, rows, D - 1:D].to_broadcast([P, 2, D - 1]),
                                            ALU.subtract).then_inc(w1_shifted, 1)
                    pool.wait_ge(mv1, t + 1)
                    nc.gpsimd.tensor_scalar(var_eps[:, t:t + 1], mv[:, t, 1:2], LN_EPS, None, ALU.add).then_inc(ve1, 1)
                    pool.wait_ge(ve1, t + 1)
                    nc.gpsimd.tensor_tensor(rstd[:, t:t + 1], var_eps[:, t:t + 1], minus_half[:, t:t + 1],
                                            ALU.pow).then_inc(rs1, 1)

            @block.vector
            def _(dve):
                nc.vector.memset(z1[:, :, D - 1:D], 1.0).then_inc(z1_ones, 1)
                dve.wait_ge(ld_wg, 16)
                nc.vector.tensor_scalar(wg_shift[:, :], wg_raw[:, :], wg_raw[:, D - 1:D], None,
                                        ALU.subtract).then_inc(wg_shifted, 1)
                dve.wait_ge(wg_shifted, 1)
                nc.vector.memset(wg_shift[:, D - 1:D], 0.0).then_inc(wg_shifted, 1)
                dve.wait_ge(wgt_hi_ready, 1)
                nc.vector.scalar_tensor_tensor(wgt_lo[:, :], z_bank[:, 0:E], W_SCALE, wgt_hi[:, :], ALU.mult,
                                               ALU.subtract).then_inc(wgt_lo_ready, 1)
                for i in range(LAST):
                    t = i
                    if t < NT:
                        dve.wait_ge(o_t_done, t + 1)
                        wait(dve, y1_done, t - 1)
                        nc.vector.tensor_copy(o_t[:, t % 2, 4:8, :],
                                              banks[2 * (t % 2) + 1][:, :].rearrange("p (c q) -> p c q", c=4))\
                            .then_inc(o_back_read, 1)
                    t = i - LAG_PROJECT
                    if 0 <= t < NT:
                        dve.wait_ge(y1_done, t + 1)
                        nc.vector.tensor_tensor(xres[:, t, :], y_bank[t % 2][:, 0:D], xres[:, t, :],
                                                ALU.add).then_inc(x1_ready, 1)
                        dve.wait_ge(x1_ready, t + 1)
                        nc.vector.bn_stats(stats[:, t, :], xres[:, t, :]).then_inc(st1, 1)
                        dve.wait_ge(st1, t + 1)
                        nc.vector.bn_aggr(mv[:, t, :], stats[:, t, :]).then_inc(mv1, 1)
                    t = i - LAG_Z
                    if 0 <= t < NT:
                        dve.wait_ge(rs1, t + 1)
                        wait(dve, z1t_done, t - 1)
                        nc.vector.tensor_scalar(z1[:, t % 2, 0:D - 1], xres[:, t, 0:D - 1], mv[:, t, 0:1],
                                                rstd[:, t:t + 1], ALU.subtract, ALU.mult).then_inc(z1_ready, 1)
                    t = i - LAG_ZT
                    if 0 <= t < NT:
                        dve.wait_ge(z1_hi_ready, t + 1)
                        nc.vector.tensor_tensor(zt_lo[:, P * t:P * t + P], z_bank[:, 0:P], zt_hi[:, P * t:P * t + P],
                                                ALU.subtract).then_inc(z1_lo_ready, 1)
                dve.wait_ge(w1_shifted, NT)
                dve.wait_ge(ld_b1, 16)
                nc.vector.tensor_copy(w1_raw[:, :, D - 1], b1_cols[:, :]).then_inc(w1_bias, 1)
                for n in range(NR // 4):
                    dve.wait_ge(w1t_hi_ready, n + 1)
                    nc.vector.scalar_tensor_tensor(w1t_lo[:, 512 * n:512 * n + 512], banks[n % 4][:, :], W_SCALE,
                                                   w1t_hi[:, 512 * n:512 * n + 512], ALU.mult,
                                                   ALU.subtract).then_inc(w1t_lo_ready, 1)
                dve.wait_ge(gates_done, NT)
                logits = g_bank[:, 0:NT * E].rearrange("p (t e) -> p t e", e=E)
                nc.vector.tensor_reduce(logit_max[:, :], logits, AX.X, ALU.max).then_inc(route, 1)
                dve.wait_ge(route, 1)
                nc.vector.tensor_tensor(prob[:, :, :], logits, logit_max[:, :].unsqueeze(2).to_broadcast([P, NT, E]),
                                        ALU.subtract).then_inc(route, 1)
                dve.wait_ge(prob_ready, 1)
                nc.vector.tensor_reduce(esum[:, :], prob[:, :, :], AX.X, ALU.add).then_inc(route, 1)
                dve.wait_ge(route, 3)
                nc.vector.reciprocal(einv[:, :], esum[:, :]).then_inc(route, 1)
                dve.wait_ge(route, 4)
                nc.vector.tensor_tensor(prob[:, :, :], prob[:, :, :],
                                        einv[:, :].unsqueeze(2).to_broadcast([P, NT, E]), ALU.mult).then_inc(route, 1)
                dve.wait_ge(route, 5)
                dve.wait_ge(masks_set, 4)
                other = prob[:, :, :].unsqueeze(2).to_broadcast([P, NT, E, E])
                own = prob[:, :, :].unsqueeze(3).to_broadcast([P, NT, E, E])
                nc.vector.tensor_tensor(over[:, :, :, :], other, own, ALU.is_gt).then_inc(route, 1)
                nc.vector.tensor_tensor(over_eq[:, :, :, :], other, own, ALU.is_ge).then_inc(route, 1)
                dve.wait_ge(route, 7)
                nc.vector.tensor_tensor(over[:, :, :, :], over[:, :, :, :],
                                        later[:, :, :].unsqueeze(1).to_broadcast([P, NT, E, E]), ALU.mult).then_inc(route, 1)
                nc.vector.tensor_tensor(over_eq[:, :, :, :], over_eq[:, :, :, :],
                                        earlier[:, :, :].unsqueeze(1).to_broadcast([P, NT, E, E]), ALU.mult).then_inc(route, 1)
                dve.wait_ge(route, 9)
                nc.vector.tensor_tensor(over[:, :, :, :], over[:, :, :, :], over_eq[:, :, :, :], ALU.add).then_inc(route, 1)
                dve.wait_ge(route, 10)
                nc.vector.tensor_reduce(rank[:, :, :], over[:, :, :, :], AX.X, ALU.add).then_inc(route, 1)
                dve.wait_ge(route, 11)
                nc.vector.scalar_tensor_tensor(prob[:, :, :], rank[:, :, :], 1.5, prob[:, :, :], ALU.is_lt,
                                               ALU.mult).then_inc(route, 1)
                dve.wait_ge(route, 12)
                nc.vector.tensor_reduce(esum[:, :], prob[:, :, :], AX.X, ALU.add).then_inc(route, 1)
                dve.wait_ge(route, 13)
                nc.vector.tensor_scalar(csum[:, :], esum[:, :], 1e-9, None, ALU.add).then_inc(route, 1)
                dve.wait_ge(route, 14)
                nc.vector.reciprocal(einv[:, :], csum[:, :]).then_inc(route, 1)
                dve.wait_ge(route, 15)
                nc.vector.tensor_tensor(csum[:, :], esum[:, :], einv[:, :], ALU.mult).then_inc(route, 1)
                nc.vector.tensor_scalar(einv[:, :], einv[:, :], 1.0 / W_SCALE, None, ALU.mult).then_inc(route, 1)
                dve.wait_ge(route, 17)
                nc.vector.tensor_tensor(gate[:, :, :], prob[:, :, :],
                                        einv[:, :].unsqueeze(2).to_broadcast([P, NT, E]), ALU.mult).then_inc(route, 1)
                dve.wait_ge(ld_f0, 32)
                for t in range(NT):
                    last = nc.vector.scalar_tensor_tensor(xres[:, t, :], fbo_bc[:, :], csum[:, t:t + 1], xres[:, t, :],
                                                          ALU.mult, ALU.add)
                    last.then_inc(route, 1)

        scratch.close()

        scratch = ExitStack()
        sig = sb1("sig", [P, 2, HF])
        glu = sb1("glu", [P, 4, HF])
        mix = sb1("mix", [P, 2, HF])
        mix_t = sb1("mix_t", [P, 2, HF // P, P])
        h_bank, mt_bank, y2_bank = banks[0:4], banks[4], banks[6:8]
        h_done, sig_ready, glu_ready, mixed, mix_t_done, mix_t_read, y2_done, x2_ready, st2, mv2 = (
            sem(n) for n in ("h_done", "sig_ready", "glu_ready", "mixed", "mix_t_done", "mix_t_read", "y2_done",
                             "x2_ready", "st2", "mv2"))
        MIXES = E - 1
        AT_TRANSPOSE, AT_COPY, AT_PROJECT = 3, 4, 6

        def tiles_of(eng, tile):
            tile(0, 0)
            tile(0, 1)
            with eng.Fori(0, NT // 2 - 1) as k:
                tile(k, 2)
                tile(k, 3)
            tile(NT // 2, 0)

        with nc.Block() as block:
            @block.tensor
            def _(pe):
                def tile(k, r):
                    final = isinstance(k, int) and 2 * k + r == NT
                    before = not (isinstance(k, int) and 2 * k + r == 0)
                    for e in range(E):
                        if not final:
                            tokens = bass.ds((k * 2 + r) * P, P)
                            bank = h_bank[e % 4]
                            wait(pe, glu_ready, k * (2 * E) + (r * E + e - 3))
                            w = slice(2 * HF * e, 2 * HF * e + 2 * HF)
                            nc.tensor.matmul(bank[:, :], zt_hi[:, tokens], w1t_hi[:, w], start=True, stop=False)
                            nc.tensor.matmul(bank[:, :], zt_lo[:, tokens], w1t_hi[:, w], start=False, stop=False)
                            nc.tensor.matmul(bank[:, :], zt_hi[:, tokens], w1t_lo[:, w], start=False,
                                             stop=True).then_inc(h_done, 1)
                        if before and e == AT_TRANSPOSE:
                            pe.wait_ge(mixed, k * (2 * MIXES) + r * MIXES)
                            wait(pe, mix_t_read, k * 2 + (r - 1))
                            for c in range(HF // P):
                                last = nc.tensor.transpose(mt_bank[:, P * c:P * c + P],
                                                           mix[:, (r - 1) % 2, P * c:P * c + P], ident[:, :])
                            last.then_inc(mix_t_done, 1)
                        if before and e == AT_PROJECT:
                            pe.wait_ge(mix_t_read, k * 2 + r)
                            wait(pe, x2_ready, k * 2 + (r - 2))
                            for c in range(HF // P):
                                last = nc.tensor.matmul(y2_bank[(r - 1) % 2][:, 0:D], mix_t[:, (r - 1) % 2, c, :],
                                                        fwo_t[:, c, :], start=(c == 0), stop=(c == HF // P - 1))
                            last.then_inc(y2_done, 1)
                tiles_of(pe, tile)

            @block.scalar
            def _(act):
                def tile(k, r):
                    final = isinstance(k, int) and 2 * k + r == NT
                    before = not (isinstance(k, int) and 2 * k + r == 0)
                    for e in range(E):
                        if not final:
                            act.wait_ge(h_done, k * (2 * E) + (r * E + e + 1))
                            wait(act, glu_ready, k * (2 * E) + (r * E + e - 1))
                            nc.scalar.activation(sig[:, e % 2, :], h_bank[e % 4][:, HF:2 * HF], ACT.Sigmoid,
                                                 scale=1.0 / W_SCALE).then_inc(sig_ready, 1)
                        if before and e == AT_COPY:
                            act.wait_ge(mix_t_done, k * 2 + r)
                            nc.scalar.activation(mix_t[:, (r - 1) % 2, :, :],
                                                 mt_bank[:, 0:HF].rearrange("p (c q) -> p c q", q=P),
                                                 ACT.Copy).then_inc(mix_t_read, 1)
                tiles_of(act, tile)

            @block.vector
            def _(dve):
                def tile(k, r):
                    final = isinstance(k, int) and 2 * k + r == NT
                    before = not (isinstance(k, int) and 2 * k + r == 0)
                    for e in range(E):
                        if not final:
                            dve.wait_ge(sig_ready, k * (2 * E) + (r * E + e + 1))
                            if e >= 4:
                                dve.wait_ge(mixed, k * (2 * MIXES) + (r * MIXES + max(e - 4, 1)))
                            elif before:
                                dve.wait_ge(mixed, k * (2 * MIXES) + ((r - 1) * MIXES + e + 4))
                            nc.vector.scalar_tensor_tensor(glu[:, e % 4, :], sig[:, e % 2, :],
                                                           gate[:, bass.ds(k * 2 + r, 1), e:e + 1].rearrange("p a b -> p (a b)"),
                                                           h_bank[e % 4][:, 0:HF], ALU.mult,
                                                           ALU.mult).then_inc(glu_ready, 1)
                    if before:
                        prev = bass.ds(k * 2 + (r - 1), 1)
                        dve.wait_ge(y2_done, k * 2 + r)
                        nc.vector.tensor_tensor(xres[:, prev, :], y2_bank[(r - 1) % 2][:, 0:D].unsqueeze(1),
                                                xres[:, prev, :], ALU.add).then_inc(x2_ready, 1)
                        dve.wait_ge(x2_ready, k * 2 + r)
                        nc.vector.bn_stats(stats[:, prev, :], xres[:, prev, :]).then_inc(st2, 1)
                tiles_of(dve, tile)

            @block.gpsimd
            def _(pool):
                def tile(k, r):
                    if isinstance(k, int) and 2 * k + r == NT:
                        return
                    for e in range(1, E):
                        pool.wait_ge(glu_ready, k * (2 * E) + (r * E + e + 1))
                        if e == 1:
                            if not isinstance(k, int) or 2 * k + r >= 2:
                                wait(pool, mix_t_done, k * 2 + (r - 1))
                        else:
                            pool.wait_ge(mixed, k * (2 * MIXES) + (r * MIXES + e - 1))
                        nc.gpsimd.tensor_tensor(mix[:, r % 2, :], glu[:, 0, :] if e == 1 else mix[:, r % 2, :],
                                                glu[:, e % 4, :], ALU.add).then_inc(mixed, 1)
                tiles_of(pool, tile)
        scratch.close()

        scratch = ExitStack()
        GT = H1 // 4
        ROWS = 32
        SHIFT_ROW = 3 * DH1
        at = 0
        zc_t = temp_v(N)[0:C, :]
        ctx_n = temp_v(NT * C).rearrange("p (t c) -> p t c", t=NT)
        q_mix = temp_v(GT * N // 2).bitcast(F16).rearrange("p (g n) -> p g n", g=GT)
        gu_raw = temp_v(2 * FT * D).rearrange("p (s i d) -> p s i d", s=2, i=FT)
        wd_raw = temp_v(FF)
        k_mask = arena_o[:, :].bitcast(F16).rearrange("p (j g n) -> p j g n", j=4, g=GT)
        z2 = ctx_halves[:, :].bitcast(F32).rearrange("p (t d) -> p t d", t=NT)
        z2_t = zt_halves[:, :].bitcast(F32)
        kw_ext = sb1("kw_ext", [C + 1, D])
        vw_ext = sb1("vw_ext", [C + 1, D])
        tb_ext = sb1("tb_ext", [C + 1, 1])
        tg_col = sb1("tg_col", [C, 1])
        qw = sb1("qw", [D, D])
        qb_row = sb1("qb_row", [1, D])
        g_col = sb1("g_col", [D, 1])
        b_col = sb1("b_col", [D, 1])
        k_rows = sb1("k_rows", [C + 1, GT, 4, ROWS])
        k_arr = sb1("k_arr", [C, GT, 4 * ROWS])
        q_rows = sb1("q_rows", [D, GT, 4, ROWS])
        q_arr = sb1("q_arr", [D, GT, 4 * ROWS])
        qb_rows = sb1("qb_rows", [1, GT, 4, ROWS])
        one = sb1("one", [1, 1])
        v_arr = sb1("v_arr", [C, D])
        tb_bc = sb1("tb_bc", [C + 1, P])
        kq_bias = sb1("kq_bias", [P, 2 * GT])
        v_bias = sb1("v_bias", [P, D])
        k_low = sb1("k_low", [P, 1])
        q_low = sb1("q_low", [P, 1])
        of_head = sb1("of_head", [P, 4])
        half = sb1("half", [P, 2, 512], F16)
        whole = sb1("whole", [P, 2, 512])
        k_mix = sb1("k_mix", [P, 2, 512], F16)
        v1 = sb1("v1", [P, NT, D])
        v_stage = sb1("v_stage", [P, QT, H1, ROWS])
        cstats = sb1("cstats", [P, NT, 6])
        cmv = sb1("cmv", [P, NT, 2])
        cvar = sb1("cvar", [P, NT])
        crstd = sb1("crstd", [P, NT])
        ld4 = sem("ld4")
        ldw6 = sem("ldw6")
        ld4c = sem("ld4c")
        w4, w4b, stc, mvc, vec, rsc, rsx, vex, zc_ready, z2_ready = (
            sem(n) for n in ("w4", "w4b", "stc", "mvc", "vec", "rsc", "rsx", "vex", "zc_ready", "z2_ready"))
        bias_done, bias_ready, misc_done, misc_read, kq_done, kq_read, half_ready, kq_mixed, k_masked = (
            sem(n) for n in ("bias_done", "bias_ready", "misc_done", "misc_read", "kq_done", "kq_read", "half_ready",
                             "kq_mixed", "k_masked"))
        LOADS4 = 8
        UNITS_K = GT * (N // 512)

        with nc.Block() as block:
            @block.sync
            def _(sp):
                sp.dma_start(ctx_n, ctx_tok).then_inc(ld4c, 16)
                with nc.allow_non_contiguous_dma(reason="a number per partition"):
                    for dst, src in ((kw_ext[0:C, :], l1_kw), (kw_ext[C:C + 1, :], l1_kb.unsqueeze(0)),
                                     (vw_ext[0:C, :], l1_vw), (vw_ext[C:C + 1, :], l1_vb.unsqueeze(0)),
                                     (tb_ext[0:C, :], l1_tb.unsqueeze(1)), (tg_col[:, :], l1_tg.unsqueeze(1)),
                                     (qw[:, :], l1_qw), (qb_row[:, :], l1_qb.unsqueeze(0)),
                                     (g_col[:, :], l1_g.unsqueeze(1)), (b_col[:, :], l1_b.unsqueeze(1))):
                        sp.dma_start(dst, src).then_inc(ld4, 16)
                for side, src in ((0, f1_wg), (1, f1_wu)):
                    for i in range(FT):
                        sp.dma_start(gu_raw[0:height[i], side, i, :], src[P * i:P * i + height[i], :]).then_inc(ldw6, 16)
                sp.dma_start(wd_raw[:, :], f1_wd).then_inc(ldw6, 16)

            @block.gpsimd
            def _(pool):
                pool.wait_ge(vex, 1)
                nc.gpsimd.tensor_tensor(rstd[:, :], var_eps[:, :], minus_half[:, :], ALU.pow).then_inc(rsx, 1)
                pool.wait_ge(vec, 1)
                nc.gpsimd.tensor_tensor(crstd[:, :], cvar[:, :], minus_half[:, :], ALU.pow).then_inc(rsc, 1)

            @block.vector
            def _(dve):
                for t in range(NT):
                    nc.vector.bn_aggr(mv[:, t, :], stats[:, t, :]).then_inc(mv2, 1)
                dve.wait_ge(mv2, NT)
                nc.vector.tensor_scalar(var_eps[:, :], mv[:, :, 1], LN_EPS, None, ALU.add).then_inc(vex, 1)
                for m in (k_rows[:, :, :, :], q_rows[:, :, :, :], qb_rows[:, :, :, :], v_stage[:, :, :, :],
                          of_head[:, :]):
                    nc.vector.memset(m, 0.0).then_inc(w4b, 1)
                nc.vector.memset(tb_ext[C:C + 1, :], 1.0).then_inc(w4, 1)
                nc.vector.memset(one[:, :], 1.0).then_inc(w4, 1)
                dve.wait_ge(w4b, 5)
                nc.vector.memset(v_stage[:, :, :, DH1:DH1 + 1], 1.0).then_inc(w4, 1)
                nc.vector.memset(k_rows[C:C + 1, :, :, SHIFT_ROW:SHIFT_ROW + 1], 1.0).then_inc(w4, 1)
                for j in range(4):
                    nc.vector.memset(of_head[ROWS * j:ROWS * j + ROWS, j:j + 1], 1.0).then_inc(w4, 1)
                heads = ident[:, :].rearrange("p (j r) -> p j r", r=ROWS)
                nc.vector.tensor_reduce(q_low[:, :], heads[:, :, DH1:2 * DH1], AX.XY, ALU.add, negate=True).then_inc(w4, 1)
                nc.vector.tensor_reduce(k_low[:, :], heads[:, :, 2 * DH1:3 * DH1], AX.XY, ALU.add,
                                        negate=True).then_inc(w4, 1)
                dve.wait_ge(ld4, 160)
                for r in range(3):
                    w = slice(DH1 * r, DH1 * r + DH1)
                    for dst, src in ((k_rows, kw_ext), (q_rows, qw), (qb_rows, qb_row)):
                        nc.vector.tensor_copy(dst[:, :, :, w], src[:, :].rearrange("p (g j d) -> p g j d", g=GT, j=4))\
                            .then_inc(w4, 1)
                dve.wait_ge(w4, 10 + 9)
                nc.vector.tensor_scalar(k_arr[:, :, :], k_rows[0:C, :, :, :].rearrange("p g j r -> p g (j r)"),
                                        tg_col[:, 0:1], None, ALU.mult).then_inc(w4, 1)
                nc.vector.tensor_scalar(q_arr[:, :, :], q_rows[:, :, :, :].rearrange("p g j r -> p g (j r)"),
                                        g_col[:, 0:1], None, ALU.mult).then_inc(w4, 1)
                nc.vector.tensor_scalar(v_arr[:, :], vw_ext[0:C, :], tg_col[:, 0:1], None, ALU.mult).then_inc(w4, 1)
                nc.vector.tensor_copy(tb_bc[:, :], tb_ext[:, 0:1].to_broadcast([C + 1, P])).then_inc(w4, 1)
                dve.wait_ge(ld4c, 16)
                for t in range(NT):
                    nc.vector.bn_stats(cstats[:, t, :], ctx_n[:, t, :]).then_inc(stc, 1)
                for t in range(NT):
                    dve.wait_ge(stc, t + 1)
                    nc.vector.bn_aggr(cmv[:, t, :], cstats[:, t, :]).then_inc(mvc, 1)
                dve.wait_ge(mvc, NT)
                nc.vector.tensor_scalar(cvar[:, :], cmv[:, :, 1], LN_EPS, None, ALU.add).then_inc(vec, 1)
                dve.wait_ge(rsx, 1)
                for t in range(NT):
                    nc.vector.tensor_scalar(z2[:, t, :], xres[:, t, :], mv[:, t, 0:1], rstd[:, t:t + 1],
                                            ALU.subtract, ALU.mult).then_inc(z2_ready, 1)
                dve.wait_ge(rsc, 1)
                for t in range(NT):
                    nc.vector.tensor_scalar(ctx_n[:, t, :], ctx_n[:, t, :], cmv[:, t, 0:1], crstd[:, t:t + 1],
                                            ALU.subtract, ALU.mult).then_inc(zc_ready, 1)
                dve.wait_ge(bias_done, 1)
                nc.vector.tensor_copy(kq_bias[:, :], banks[4][:, 0:2 * GT]).then_inc(bias_ready, 1)
                nc.vector.tensor_copy(v_bias[:, :], banks[4][:, P:2 * P]).then_inc(bias_ready, 1)
                for m in range(NT // 4):
                    dve.wait_ge(misc_done, m + 1)
                    nc.vector.tensor_copy(z2_t[:, 512 * m:512 * m + 512], banks[5 + m % 3][:, :]).then_inc(misc_read, 1)
                for m in range(NT // 4):
                    n = NT // 4 + m
                    dve.wait_ge(misc_done, n + 1)
                    nc.vector.tensor_copy(zc_t[:, 512 * m:512 * m + 512], banks[5 + n % 3][0:C, :]).then_inc(misc_read, 1)
                dve.wait_ge(bias_ready, 2)
                for m in range(NT // 4):
                    n = 2 * (NT // 4) + m
                    dve.wait_ge(misc_done, n + 1)
                    nc.vector.tensor_tensor(v1[:, 4 * m:4 * m + 4, :],
                                            banks[5 + n % 3][:, :].rearrange("p (t d) -> p t d", t=4),
                                            v_bias[:, :].unsqueeze(1).to_broadcast([P, 4, D]), ALU.add).then_inc(misc_read, 1)

                def keys(c):
                    for g in range(GT):
                        dve.wait_ge(half_ready, c * GT + (g + 1))
                        wait(dve, k_masked, 4 * (c * GT + g - 1))
                        nc.vector.scalar_tensor_tensor(k_mix[:, g % 2, :], half[:, g % 2, :], k_low[:, 0:1],
                                                       whole[:, g % 2, :], ALU.mult, ALU.add).then_inc(kq_mixed, 1)
                        dve.wait_ge(kq_mixed, c * GT + (g + 1))
                        for j in range(4):
                            nc.vector.tensor_scalar(k_mask[:, j, g, bass.ds(c * 512, 512)], k_mix[:, g % 2, :],
                                                    of_head[:, j:j + 1], None, ALU.mult).then_inc(k_masked, 1)

                keys(0)
                with dve.Fori(1, N // 512) as c:
                    keys(c)
                with dve.Fori(0, N // 512) as c:
                    for g in range(GT):
                        dve.wait_ge(half_ready, c * GT + (UNITS_K + g + 1))
                        nc.vector.scalar_tensor_tensor(q_mix[:, g, bass.ds(c * 512, 512)], half[:, g % 2, :],
                                                       q_low[:, 0:1], whole[:, g % 2, :], ALU.mult,
                                                       ALU.add).then_inc(kq_mixed, 1)

            @block.scalar
            def _(act):
                act.wait_ge(bias_ready, 1)

                def units(c, first, side):
                    for g in range(GT):
                        n = c * GT + (first + g)
                        act.wait_ge(kq_done, n + 1)
                        wait(act, kq_mixed, n - 1)
                        bias = kq_bias[:, GT * side + g:GT * side + g + 1]
                        nc.scalar.activation(whole[:, g % 2, :], banks[g % 4][:, :], ACT.Identity, bias=bias)\
                            .then_inc(kq_read, 1)
                        nc.scalar.activation(half[:, g % 2, :], banks[g % 4][:, :], ACT.Identity, bias=bias)\
                            .then_inc(half_ready, 1)
                units(0, 0, 0)
                with act.Fori(1, N // 512) as c:
                    units(c, 0, 0)
                with act.Fori(0, N // 512) as c:
                    units(c, UNITS_K, 1)

            @block.tensor
            def _(pe):
                pe.wait_ge(w4, 10 + 9 + 4)
                for g in range(GT):
                    nc.tensor.matmul(banks[4][:, g:g + 1], k_rows[:, g, :, :].rearrange("p j r -> p (j r)"),
                                     tb_ext[:, :], start=True, stop=True)
                for g in range(GT):
                    nc.tensor.matmul(banks[4][:, GT + g:GT + g + 1], q_rows[:, g, :, :].rearrange("p j r -> p (j r)"),
                                     b_col[:, :], start=True, stop=False)
                    nc.tensor.matmul(banks[4][:, GT + g:GT + g + 1], qb_rows[:, g, :, :].rearrange("p j r -> p (j r)"),
                                     one[:, :], start=False, stop=True)
                nc.tensor.matmul(banks[4][:, P:2 * P], tb_bc[:, :], vw_ext[:, :], start=True, stop=True)\
                    .then_inc(bias_done, 1)
                pe.wait_ge(z2_ready, NT)
                for m in range(NT // 4):
                    wait(pe, misc_read, m - 2)
                    for j in range(4):
                        last = nc.tensor.transpose(banks[5 + m % 3][:, P * j:P * j + P], z2[:, 4 * m + j, :], ident[:, :])
                    last.then_inc(misc_done, 1)
                pe.wait_ge(zc_ready, NT)
                for m in range(NT // 4):
                    n = NT // 4 + m
                    wait(pe, misc_read, n - 2)
                    for j in range(4):
                        last = nc.tensor.transpose(banks[5 + n % 3][0:C, P * j:P * j + P], ctx_n[:, 4 * m + j, :],
                                                   ident[:, :])
                    last.then_inc(misc_done, 1)
                pe.wait_ge(misc_read, 2 * (NT // 4))
                for m in range(NT // 4):
                    n = 2 * (NT // 4) + m
                    for j in range(4):
                        t = 4 * m + j
                        last = nc.tensor.matmul(banks[5 + n % 3][:, P * j:P * j + P], zc_t[:, P * t:P * t + P],
                                                v_arr[:, :], start=True, stop=True)
                        if j == 0 and m == 3:
                            pass
                    last.then_inc(misc_done, 1)
                    if m < NT // 4 - 1:
                        wait(pe, misc_read, n - 1)

                def units(c, first, weights, moving):
                    for g in range(GT):
                        wait(pe, half_ready, c * GT + (first + g - 3))
                        nc.tensor.matmul(banks[g % 4][:, :], weights[:, g, :], moving[:, bass.ds(c * 512, 512)],
                                         start=True, stop=True).then_inc(kq_done, 1)
                units(0, 0, k_arr, zc_t)
                with pe.Fori(1, N // 512) as c:
                    units(c, 0, k_arr, zc_t)
                with pe.Fori(0, N // 512) as c:
                    units(c, UNITS_K, q_arr, z2_t)

        wd_diag = temp_v(D)
        ones = temp_v(P)
        w6, st3 = sem("w6"), sem("st3")
        kept = at
        RING1 = 4
        p1 = temp_v(RING1 * QT * S).rearrange("p (r n) -> p r n", r=RING1)
        neg_max1 = sb1("neg_max1", [P, 2, 4 * QT])
        neg_max1_t = sb1("neg_max1_t", [4 * QT, 2, P], F16)
        y_sb = temp_v(2 * S).rearrange("p (r n) -> p r n", r=2)
        y_inv = sb1("y_inv", [P, 2, QT, 4])
        y_norm = sb1("y_norm", [P, 2, QT, 4, DH1])
        score_bank, max_bank, y_bank, shift_bank, yt_bank = banks[0:2], banks[2:4], banks[4:6], banks[6], banks[7]
        LEAD_MAX, LEAD_SHIFT, LAG_PV, LAG_Y, LAG_YT, LAG_FINISH = 10, 6, 3, 7, 9, 10
        SCALE1 = float(DH1) ** -0.5
        max1_done, max1_read, shift1_done, shift1_read, scores1_done, p1_ready, staged, pv1_done = (
            sem(n) for n in ("max1_done", "max1_read", "shift1_done", "shift1_read", "scores1_done", "p1_ready",
                             "staged", "pv1_done"))
        y1_read, y1t_done, y1_inverted, y1t_read, x3_ready = (
            sem(n) for n in ("y1_read", "y1t_done", "y1_inverted", "y1t_read", "x3_ready"))
        shift1_row = [sem("shift1_row_even"), sem("shift1_row_odd")]

        PEELED = 14

        def steps1(eng, step):
            for s in range(-LEAD_MAX, PEELED):
                step(0, s)
            with eng.Fori(0, B - 2) as b:
                for s in range(PEELED, PEELED + H1):
                    step(b, s)
            for s in range(PEELED, 2 * H1 + LAG_FINISH + 2):
                step(B - 2, s)

        def work_out(eng, values, places):
            for v in values:
                eng.compute_val(v)
            for ap in places:
                eng.lower_ap(ap)

        def group(b, s):
            return b * GT + s // 4

        with nc.Block() as block:
            @block.tensor
            def _(pe):
                def maxima(b, s):
                    g, j = (s // 4) % GT, s % 4
                    wait(pe, max1_read, count(b, s) - 1)
                    for q in range(QT):
                        last = nc.tensor.matmul(max_bank[s % 2][:, S * q:S * q + S],
                                                q_mix[:, g, bass.ds((b + s // H1) * S + P * q, P)],
                                                k_mask[:, j, g, bass.ds((b + s // H1) * S, S)], start=True, stop=True)
                    last.then_inc(max1_done, 1)

                def shift(b, s):
                    pe.wait_ge(max1_read, count(b, s) + 4)
                    wait(pe, shift1_read, group(b, s))
                    nc.tensor.transpose(shift_bank[0:4 * QT, 0:P], neg_max1[:, (s // 4) % 2, :],
                                        ident[:, :]).then_inc(shift1_done, 1)

                def scores(b, s):
                    g, j = (s // 4) % GT, s % 4
                    if j == 0:
                        pe.wait_ge(shift1_row[(s // 4) % 2], b * 32 + 16 * (s // 8 + 1))
                    wait(pe, p1_ready, count(b, s) - 1)
                    for k in range(QT):
                        last = nc.tensor.matmul(score_bank[s % 2][:, S * k:S * k + S],
                                                k_mask[:, j, g, bass.ds((b + s // H1) * S + P * k, P)],
                                                q_mix[:, g, bass.ds((b + s // H1) * S, S)], start=True, stop=True)
                    last.then_inc(scores1_done, 1)

                def values(b, s):
                    g, j = s // 4, s % 4
                    if j == 0:
                        wait(pe, y1_read, group(b, s) - 1)
                        pe.wait_ge(staged, b * GT + (g + 1))
                    if not there(b, s + LAG_PV):
                        pe.wait_ge(p1_ready, count(b, s) + 1)
                    for k in range(QT):
                        last = nc.tensor.matmul(y_bank[g % 2][ROWS * j:ROWS * j + ROWS, 0:S], v_stage[:, k, s % H1, :],
                                                p1[:, s % RING1, S * k:S * k + S], start=(k == 0), stop=(k == QT - 1))
                    last.then_inc(pv1_done, 1)

                def back(b, s):
                    g = s // 4
                    pe.wait_ge(y1_read, b * GT + (g + 1))
                    wait(pe, y1t_read, group(b, s))
                    for q in range(QT):
                        last = nc.tensor.transpose(yt_bank[:, P * q:P * q + P], y_sb[:, g % 2, P * q:P * q + P],
                                                   ident[:, :])
                    last.then_inc(y1t_done, 1)

                def max_query(b, s, q):
                    return q_mix[:, (s // 4) % GT, bass.ds((b + s // H1) * S + P * q, P)]

                def max_keys(b, s):
                    return k_mask[:, s % 4, (s // 4) % GT, bass.ds((b + s // H1) * S, S)]

                def score_keys(b, s, k):
                    return k_mask[:, s % 4, (s // 4) % GT, bass.ds((b + s // H1) * S + P * k, P)]

                def score_queries(b, s):
                    return q_mix[:, (s // 4) % GT, bass.ds((b + s // H1) * S, S)]

                def step(b, s):
                    if not isinstance(b, int):
                        work_out(pe, (count(b, s) - 1, count(b, s + LEAD_MAX) - 1),
                                 (max_query(b, s + LEAD_MAX, 0), max_query(b, s + LEAD_MAX, 1), max_keys(b, s + LEAD_MAX),
                                  score_keys(b, s, 0), score_keys(b, s, 1), score_queries(b, s)))
                    if there(b, s):
                        scores(b, s)
                    if there(b, s + LEAD_MAX):
                        maxima(b, s + LEAD_MAX)
                    if (s + LEAD_SHIFT) % 4 == 0 and there(b, s + LEAD_SHIFT):
                        shift(b, s + LEAD_SHIFT)
                    if there(b, s - LAG_PV):
                        values(b, s - LAG_PV)
                    if (s - LAG_YT) % 4 == 0 and there(b, s - LAG_YT):
                        back(b, s - LAG_YT)
                steps1(pe, step)

            @block.scalar
            def _(act):
                def step(b, s):
                    if there(b, s):
                        act.wait_ge(scores1_done, count(b, s) + 1)
                        wait(act, pv1_done, count(b, s) + 1 - RING1)
                        nc.scalar.activation(p1[:, s % RING1, :], score_bank[s % 2][:, :], ACT.Exp,
                                             scale=SCALE1).then_inc(p1_ready, 1)
                    u = s - LAG_Y
                    if u % 4 == 0 and there(b, u):
                        act.wait_ge(pv1_done, count(b, u) + 4)
                        wait(act, y1t_done, group(b, u) - 1)
                        nc.scalar.activation(y_sb[:, (u // 4) % 2, :], y_bank[(u // 4) % 2][:, 0:S],
                                             ACT.Copy).then_inc(y1_read, 1)
                steps1(act, step)

            @block.vector
            def _(dve):
                def weight_scales():
                    nc.vector.memset(ones[:, :], 1.0).then_inc(w6, 1)
                    dve.wait_ge(ldw6, 112)
                    for side in range(2):
                        for i in range(FT):
                            p = height[i]
                            nc.vector.tensor_reduce(gu_max[0:p, side, i:i + 1], gu_raw[0:p, side, i, :], AX.X, ALU.max,
                                                    apply_absolute_value=True).then_inc(w6, 1)
                    nc.vector.tensor_reduce(wd_max[:, :], wd_raw[:, :], AX.X, ALU.max, apply_absolute_value=True).then_inc(w6, 1)
                    dve.wait_ge(w6, 8)
                    for i in range(FT):
                        p = height[i]
                        nc.vector.tensor_scalar(gu_scale[0:p, :, i], gu_max[0:p, :, i], 1.0 / QMAX, None, ALU.mult).then_inc(w6, 1)
                    nc.vector.tensor_scalar(wd_scale[:, :], wd_max[:, :], 1.0 / QMAX, None, ALU.mult).then_inc(w6, 1)
                    dve.wait_ge(w6, 12)
                    for i in range(FT):
                        p = height[i]
                        nc.vector.reciprocal(gu_inv[0:p, :, i], gu_scale[0:p, :, i]).then_inc(w6, 1)
                    nc.vector.reciprocal(wd_inv[:, :], wd_scale[:, :]).then_inc(w6, 1)
                    nc.vector.tensor_scalar(wd_diag[:, :], ident[:, :], wd_scale[:, 0:1], None, ALU.mult).then_inc(w6, 1)

                def max_of(b, s):
                    g, j = (s // 4) % 2, s % 4
                    dve.wait_ge(max1_done, count(b, s) + 1)
                    if j == 0:
                        wait(dve, shift1_done, group(b, s) - 1)
                    nc.vector.tensor_reduce(neg_max1[:, g, QT * j:QT * j + QT],
                                            max_bank[s % 2][:, :].rearrange("p (q k) -> p q k", q=QT),
                                            AX.X, ALU.max, negate=True).then_inc(max1_read, 1)

                def shift_out(b, s):
                    g = (s // 4) % 2
                    dve.wait_ge(shift1_done, b * GT + (s // 4 + 1))
                    wait(dve, shift1_row[g], b * 32 + 16 * (s // 8))
                    nc.vector.tensor_copy(neg_max1_t[:, g, :], shift_bank[0:4 * QT, 0:P]).then_inc(shift1_read, 1)

                def finish(b, s):
                    g = (s // 4) % 2
                    y = yt_bank[:, 0:QT * P].rearrange("p (q j r) -> p q j r", q=QT, j=4)
                    dve.wait_ge(y1t_done, b * GT + (s // 4 + 1))
                    nc.vector.reciprocal(y_inv[:, g, :, :], y[:, :, :, DH1]).then_inc(y1_inverted, 1)
                    dve.wait_ge(y1_inverted, b * GT + (s // 4 + 1))
                    wait(dve, x3_ready, group(b, s) - 1)
                    nc.vector.tensor_tensor(y_norm[:, g, :, :, :], y[:, :, :, 0:DH1],
                                            y_inv[:, g, :, :].unsqueeze(3).to_broadcast([P, QT, 4, DH1]),
                                            ALU.mult).then_inc(y1t_read, 1)

                def step(b, s):
                    if there(b, s + LEAD_MAX):
                        max_of(b, s + LEAD_MAX)
                    if isinstance(b, int) and count(b, s) == -1:
                        weight_scales()
                    u = s + LEAD_SHIFT - 1
                    if u % 4 == 0 and there(b, u):
                        shift_out(b, u)
                    u = s - LAG_FINISH
                    if u % 4 == 0 and there(b, u):
                        finish(b, u)
                    u = s - LAG_FINISH - 1
                    if u % H1 == H1 - 4 and there(b, u):
                        dve.wait_ge(x3_ready, b * GT + (u // 4 + 1))
                        for q in range(QT):
                            t = bass.ds((b + u // H1) * QT + q, 1)
                            nc.vector.bn_stats(stats[:, t, :], xres[:, t, :]).then_inc(st3, 1)
                steps1(dve, step)

            @block.gpsimd
            def _(pool):
                def on_grid(n):
                    def put(dst, inv):
                        if n == 0:
                            return nc.gpsimd.tensor_scalar(dst, dst, inv, MAGIC, ALU.mult, ALU.add)
                        if n == 1:
                            return nc.gpsimd.tensor_scalar(dst, dst, MAGIC + QMAX, MAGIC - QMAX - 1.0, ALU.min, ALU.max)
                        return nc.gpsimd.tensor_scalar(dst, dst, MAGIC, None, ALU.subtract)
                    pool.wait_ge(w6, 17 + 7 * n)
                    for side in range(2):
                        for i in range(FT):
                            p = height[i]
                            put(gu_raw[0:p, side, i, :], gu_inv[0:p, side, i:i + 1]).then_inc(w6, 1)
                    put(wd_raw[:, :], wd_inv[:, 0:1]).then_inc(w6, 1)

                def step(b, s):
                    u = s + LEAD_SHIFT
                    if u % 4 == 0 and there(b, u):
                        h = u % H1
                        wait(pool, pv1_done, count(b, u) + 4 - H1)
                        nc.gpsimd.tensor_copy(v_stage[:, :, h:h + 4, 0:DH1],
                                              v1[:, bass.ds((b + u // H1) * QT, QT), DH1 * h:DH1 * h + 4 * DH1]
                                              .rearrange("p t (h d) -> p t h d", h=4)).then_inc(staged, 1)
                    if isinstance(b, int) and count(b, s) in (0, 4, 8):
                        on_grid(s // 4)
                    u = s - LAG_FINISH
                    if u % 4 == 0 and there(b, u):
                        h = u % H1
                        pool.wait_ge(y1t_read, b * GT + (u // 4 + 1))
                        rows = xres[:, bass.ds((b + u // H1) * QT, QT), DH1 * h:DH1 * h + 4 * DH1]
                        nc.gpsimd.tensor_tensor(rows, rows, y_norm[:, (u // 4) % 2, :, :, :]
                                                .rearrange("p q j d -> p q (j d)"), ALU.add).then_inc(x3_ready, 1)
                steps1(pool, step)

            @block.sync
            def _(sp):
                def step(b, s):
                    u = s + LEAD_SHIFT
                    if u % 4 == 0 and there(b, u):
                        g = (u // 4) % 2
                        sp.wait_ge(shift1_read, b * GT + (u // 4 + 1))
                        sp.dma_start(q_mix[SHIFT_ROW:P:ROWS, (u // 4) % GT, bass.ds((b + u // H1) * S, S)],
                                     neg_max1_t[:, g, :]).then_inc(shift1_row[g], 16)
                steps1(sp, step)
        scratch.close()

        scratch = ExitStack()
        CH = N // 512
        at = kept
        z3 = temp_v(N).rearrange("p (t d) -> p t d", t=NT)
        grid = temp_v(N)
        gated = temp_v(512 * 2).rearrange("p (r n) -> p r n", r=2)
        hidden = arena_o[:, 0:FT * N].rearrange("p (i n) -> p i n", i=FT)
        hidden_q = arena_o[:, FT * N:FT * N + FT * N // 2].bitcast(BF16).rearrange("p (i n) -> p i n", i=FT)
        gu_t = sb1("gu_t", [D, 2, FT * P], BF16)
        wd_t = sb1("wd_t", [P, FT, D], BF16)
        x_q = zt_halves[:, 0:N].bitcast(BF16)
        wd_row = sb1("wd_row", [P, D])
        clips = sb1("clips", [P, 2])
        clip_sig = sb1("clip_sig", [P, 2])
        x_max = sb1("x_max", [P, 1])
        x_all = sb1("x_all", [P, 1])
        x_scale = sb1("x_scale", [P, 1])
        x_inv = sb1("x_inv", [P, 1])
        gu_cols = sb1("gu_cols", [P, 2, FT])
        h_max = sb1("h_max", [P, FT * CH])
        h_top = sb1("h_top", [P, 1])
        h_all = sb1("h_all", [P, 1])
        h_scale = sb1("h_scale", [P, 1])
        h_inv = sb1("h_inv", [P, 1])
        y_part = sb1("y_part", [P, 2, 4, D])
        h_cleared, ld6, mv3, ve3, rs3, wt_done, wt_read, z3_ready, clip_ready, x_chain = (
            sem(n) for n in ("h_cleared", "ld6", "mv3", "ve3", "rs3", "wt_done", "wt_read", "z3_ready", "clip_ready",
                             "x_chain"))
        x_reduced, z3t_done, grid_ready, xq_ready, gu_done, gated_ready, hidden_ready, h_maxed, h_reduced = (
            sem(n) for n in ("x_reduced", "z3t_done", "grid_ready", "xq_ready", "gu_done", "gated_ready",
                             "hidden_ready", "h_maxed", "h_reduced"))
        h_grid, hq_ready, y3_done, y3_read, out_ready, stored, h_chain = (
            sem(n) for n in ("h_grid", "hq_ready", "y3_done", "y3_read", "out_ready", "stored", "h_chain"))
        UNITS_H = FT * CH

        with nc.Block() as block:
            @block.sync
            def _(sp):
                sp.dma_start(clips[:, 0:1], f1_cx.partition_broadcast(P)).then_inc(ld6, 16)
                sp.dma_start(clips[:, 1:2], f1_cd.partition_broadcast(P)).then_inc(ld6, 16)
                for c in range(CH):
                    sp.wait_ge(out_ready, c + 1)
                    sp.dma_start(out[:, 4 * c:4 * c + 4, :], xres[:, 4 * c:4 * c + 4, :]).then_inc(stored, 16)
                sp.wait_ge(stored, 16 * CH)

            @block.gpsimd
            def _(pool):
                pool.wait_ge(ve3, 1)
                nc.gpsimd.tensor_tensor(rstd[:, :], var_eps[:, :], minus_half[:, :], ALU.pow).then_inc(rs3, 1)
                pool.wait_ge(x_chain, 1)
                nc.gpsimd.partition_all_reduce(x_all[:, :], x_max[:, :], P, bass.bass_isa.ReduceOp.max).then_inc(x_reduced, 1)
                pool.wait_ge(h_chain, 1)
                nc.gpsimd.partition_all_reduce(h_all[:, :], h_top[:, :], P, bass.bass_isa.ReduceOp.max).then_inc(h_reduced, 1)

            @block.scalar
            def _(act):
                act.wait_ge(ld6, 32)
                nc.scalar.activation(clip_sig[:, :], clips[:, :], ACT.Sigmoid).then_inc(clip_ready, 1)
                for n in range(CH):
                    act.wait_ge(grid_ready, 2 * n + 2)
                    nc.scalar.activation(x_q[:, 512 * n:512 * n + 512], grid[:, 512 * n:512 * n + 512], ACT.Copy,
                                         bias=-MAGIC).then_inc(xq_ready, 1)
                act.wait_ge(x_chain, 5)
                for n in range(UNITS_H):
                    i = n // CH
                    p = height[i]
                    act.wait_ge(gu_done, n + 1)
                    wait(act, hidden_ready, n - 1)
                    nc.scalar.activation(gated[0:p, n % 2, :], banks[4 + 2 * (n % 2)][0:p, :], ACT.Silu,
                                         scale=gu_cols[0:p, 0, i:i + 1]).then_inc(gated_ready, 1)
                for n in range(UNITS_H):
                    i, w = n // CH, slice(512 * (n % CH), 512 * (n % CH) + 512)
                    p = height[i]
                    act.wait_ge(h_grid, 2 * n + 2)
                    nc.scalar.activation(hidden_q[0:p, i, w], hidden[0:p, i, w], ACT.Copy, bias=-MAGIC).then_inc(hq_ready, 1)

            @block.vector
            def _(dve):
                for t in range(NT):
                    nc.vector.bn_aggr(mv[:, t, :], stats[:, t, :]).then_inc(mv3, 1)
                nc.vector.memset(h_max[:, :], 0.0).then_inc(h_cleared, 1)
                dve.wait_ge(mv3, NT)
                nc.vector.tensor_scalar(var_eps[:, :], mv[:, :, 1], LN_EPS, None, ALU.add).then_inc(ve3, 1)
                for side in range(2):
                    dve.wait_ge(wt_done, side + 1)
                    nc.vector.tensor_copy(gu_t[:, side, 0:FF], banks[side][:, 0:FF]).then_inc(wt_read, 1)
                dve.wait_ge(wt_done, 3)
                for i in range(FT):
                    p = height[i]
                    nc.vector.tensor_copy(wd_t[0:p, i, :], banks[2][0:p, D * i:D * i + D]).then_inc(wt_read, 1)
                dve.wait_ge(rs3, 1)
                for t in range(NT):
                    nc.vector.tensor_scalar(z3[:, t, :], xres[:, t, :], mv[:, t, 0:1], rstd[:, t:t + 1],
                                            ALU.subtract, ALU.mult).then_inc(z3_ready, 1)
                dve.wait_ge(z3_ready, NT)
                nc.vector.tensor_reduce(x_max[:, :], z3[:, :, :], AX.XY, ALU.max, apply_absolute_value=True).then_inc(x_chain, 1)
                dve.wait_ge(x_reduced, 1)
                dve.wait_ge(clip_ready, 1)
                nc.vector.tensor_scalar(x_scale[:, :], x_all[:, :], clip_sig[:, 0:1], 1.0 / QMAX, ALU.mult, ALU.mult)\
                    .then_inc(x_chain, 1)
                dve.wait_ge(x_chain, 2)
                nc.vector.reciprocal(x_inv[:, :], x_scale[:, :]).then_inc(x_chain, 1)
                nc.vector.tensor_scalar(gu_cols[:, :, 0:FT - 1], gu_scale[:, :, 0:FT - 1], x_scale[:, 0:1], None,
                                        ALU.mult).then_inc(x_chain, 1)
                p = height[FT - 1]
                nc.vector.tensor_scalar(gu_cols[0:p, :, FT - 1], gu_scale[0:p, :, FT - 1], x_scale[0:p, 0:1], None,
                                        ALU.mult).then_inc(x_chain, 1)
                dve.wait_ge(x_chain, 5)
                for n in range(CH):
                    dve.wait_ge(z3t_done, n + 1)
                    w = grid[:, 512 * n:512 * n + 512]
                    nc.vector.tensor_scalar(w, banks[4 + n][:, :], x_inv[:, 0:1], MAGIC, ALU.mult, ALU.add).then_inc(grid_ready, 1)
                    dve.wait_ge(grid_ready, 2 * n + 1)
                    nc.vector.tensor_scalar(w, w, MAGIC + QMAX, MAGIC - QMAX - 1.0, ALU.min, ALU.max).then_inc(grid_ready, 1)
                dve.wait_ge(h_cleared, 1)
                for n in range(UNITS_H):
                    i, w = n // CH, slice(512 * (n % CH), 512 * (n % CH) + 512)
                    p = height[i]
                    dve.wait_ge(gated_ready, n + 1)
                    nc.vector.scalar_tensor_tensor(hidden[0:p, i, w], banks[5 + 2 * (n % 2)][0:p, :],
                                                   gu_cols[0:p, 1, i:i + 1], gated[0:p, n % 2, :], ALU.mult,
                                                   ALU.mult).then_inc(hidden_ready, 1)
                    dve.wait_ge(hidden_ready, n + 1)
                    nc.vector.tensor_reduce(h_max[0:p, n:n + 1], hidden[0:p, i, w], AX.X, ALU.max,
                                            apply_absolute_value=True).then_inc(h_maxed, 1)
                dve.wait_ge(h_maxed, UNITS_H)
                nc.vector.tensor_reduce(h_top[:, :], h_max[:, :], AX.X, ALU.max).then_inc(h_chain, 1)
                dve.wait_ge(h_reduced, 1)
                nc.vector.tensor_scalar(h_scale[:, :], h_all[:, :], clip_sig[:, 1:2], 1.0 / QMAX, ALU.mult, ALU.mult)\
                    .then_inc(h_chain, 1)
                dve.wait_ge(h_chain, 2)
                nc.vector.reciprocal(h_inv[:, :], h_scale[:, :]).then_inc(h_chain, 1)
                dve.wait_ge(wt_done, 4)
                nc.vector.tensor_scalar(wd_row[:, :], banks[3][:, 0:D], h_scale[:, 0:1], None, ALU.mult).then_inc(h_chain, 1)
                dve.wait_ge(h_chain, 4)
                for n in range(UNITS_H):
                    i, w = n // CH, slice(512 * (n % CH), 512 * (n % CH) + 512)
                    h = hidden[0:height[i], i, w]
                    nc.vector.tensor_scalar(h, h, h_inv[0:height[i], 0:1], MAGIC, ALU.mult, ALU.add).then_inc(h_grid, 1)
                    dve.wait_ge(h_grid, 2 * n + 1)
                    nc.vector.tensor_scalar(h, h, MAGIC + QMAX, MAGIC - QMAX - 1.0, ALU.min, ALU.max).then_inc(h_grid, 1)
                for c in range(CH):
                    dve.wait_ge(y3_done, c + 1)
                    nc.vector.tensor_tensor(y_part[:, c % 2, :, :], banks[4 + c][:, :].rearrange("p (t d) -> p t d", t=4),
                                            wd_row[:, :].unsqueeze(1).to_broadcast([P, 4, D]), ALU.mult).then_inc(y3_read, 1)
                    dve.wait_ge(y3_read, c + 1)
                    nc.vector.tensor_tensor(xres[:, 4 * c:4 * c + 4, :], xres[:, 4 * c:4 * c + 4, :], y_part[:, c % 2, :, :],
                                            ALU.add).then_inc(out_ready, 1)

            @block.tensor
            def _(pe):
                for side in range(2):
                    for i in range(FT):
                        p = height[i]
                        last = nc.tensor.transpose(banks[side][:, P * i:P * i + p], gu_raw[0:p, side, i, :], ident[0:p, 0:p])
                    last.then_inc(wt_done, 1)
                for i in range(FT):
                    p = height[i]
                    last = nc.tensor.transpose(banks[2][0:p, D * i:D * i + D], wd_raw[:, P * i:P * i + p], ident[:, :])
                last.then_inc(wt_done, 1)
                nc.tensor.matmul(banks[3][:, 0:D], ones[:, :], wd_diag[:, :], start=True, stop=True).then_inc(wt_done, 1)
                pe.wait_ge(wt_read, 2 + FT)
                pe.wait_ge(z3_ready, NT)
                for n in range(CH):
                    for j in range(4):
                        last = nc.tensor.transpose(banks[4 + n][:, P * j:P * j + P], z3[:, 4 * n + j, :], ident[:, :])
                    last.then_inc(z3t_done, 1)
                for n in range(UNITS_H):
                    i, c = n // CH, n % CH
                    p = height[i]
                    pe.wait_ge(xq_ready, CH)
                    wait(pe, hidden_ready, n - 1)
                    nc.tensor.matmul(banks[4 + 2 * (n % 2)][0:p, :], gu_t[:, 0, P * i:P * i + p],
                                     x_q[:, 512 * c:512 * c + 512], start=True, stop=True)
                    nc.tensor.matmul(banks[5 + 2 * (n % 2)][0:p, :], gu_t[:, 1, P * i:P * i + p],
                                     x_q[:, 512 * c:512 * c + 512], start=True, stop=True).then_inc(gu_done, 1)
                for c in range(CH):
                    for j in range(4):
                        t = 4 * c + j
                        for i in range(FT):
                            p = height[i]
                            pe.wait_ge(hq_ready, CH * i + c + 1)
                            last = nc.tensor.matmul(banks[4 + c][:, P * j:P * j + P], hidden_q[0:p, i, P * t:P * t + P],
                                                    wd_t[0:p, i, :], start=(i == 0), stop=(i == FT - 1))
                    last.then_inc(y3_done, 1)
        scratch.close()


def laid_out(inputs):
    import numpy as _np
    a = {k: _np.ascontiguousarray(v) for k, v in inputs.items()}

    def tiles(m):
        return _np.ascontiguousarray(m.reshape(-1, P, m.shape[-1]).transpose(1, 0, 2))

    def heads_t(w):
        return _np.ascontiguousarray(w.reshape(w.shape[0], H0, DH0).transpose(2, 1, 0))

    return {
        "x": tiles(a["x"].reshape(N, D)),
        "ctx_tok": tiles(a["ctx_768"].reshape(N, C)),
        "ctx_t": _np.ascontiguousarray(a["ctx_768"].reshape(N, C).T),
        "l0_wq_t": heads_t(a["L0_xattn_Wq"]),
        "l0_wk_t": heads_t(a["L0_xattn_Wk"]),
        "l0_wv": a["L0_xattn_Wv"],
        "l0_wo": tiles(a["L0_xattn_Wo"]),
        "l0_bo": a["L0_xattn_bo"],
        "f0_wg": a["L0_ffn_Wg"],
        "f0_w1": tiles(a["L0_ffn_W1"].reshape(-1, D)),
        "f0_b1": _np.ascontiguousarray(a["L0_ffn_b1"].reshape(-1, P).T),
        "f0_wo_t": tiles(_np.ascontiguousarray(a["L0_ffn_Wo"].T)),
        "f0_bo": a["L0_ffn_bo"],
        "l1_qw": a["L1_xattn_q_w"], "l1_qb": a["L1_xattn_q_b"],
        "l1_kw": a["L1_xattn_k_w"], "l1_kb": a["L1_xattn_k_b"],
        "l1_vw": a["L1_xattn_v_w"], "l1_vb": a["L1_xattn_v_b"],
        "l1_g": a["L1_xattn_ln_g"], "l1_b": a["L1_xattn_ln_b"],
        "l1_tg": a["L1_xattn_tln_g"], "l1_tb": a["L1_xattn_tln_b"],
        "f1_cx": a["L1_ffn_clip_x"], "f1_cd": a["L1_ffn_clip_down"],
        "f1_wg": a["L1_ffn_w_gate"], "f1_wu": a["L1_ffn_w_up"], "f1_wd": a["L1_ffn_w_down"],
    }


def kernel(**inputs):
    import numpy as _np
    import concourse.bacc as _bacc
    from concourse import mybir as _mybir
    from concourse.bass_utils import run_bass_kernel_spmd as _run

    nc = _bacc.Bacc("TRN2", target_bir_lowering=False, num_devices=1)
    arrays, args = {}, {}
    for name, a in laid_out(inputs).items():
        arrays[f"in_{name}"] = a
        args[name] = nc.dram_tensor(f"in_{name}", a.shape, _mybir.dt.from_np(a.dtype), kind="ExternalInput").ap()
    out = nc.dram_tensor("out", (P, NT, D), F32, kind="ExternalOutput").ap()
    cross_ffn_network(nc, out=out, **args)
    r = _run(nc, [arrays], core_ids=[0])
    return _np.ascontiguousarray(r.results[0]["out"].transpose(1, 0, 2)).reshape(B, S, D)
```

```python
from contextlib import ExitStack

import concourse.bass as bass
from concourse import mybir

F32 = mybir.dt.float32
F16 = mybir.dt.float16
BF16 = mybir.dt.bfloat16
ALU = mybir.AluOpType
ACT = mybir.ActivationFunctionType
AX = mybir.AxisListType

P = 128
B = 8
S = 256
QT = S // P
NT = B * QT
N = B * S
D = 128
C = 96
H0 = 16
DH0 = 64
E = 8
HF = 256
HG = H0 // 4
H1 = 16
DH1 = D // H1
FF = 352
LN_EPS = 1e-5
W_SCALE = 64.0
MAGIC = 12582912.0
QMAX = 127.0
FT = -(-FF // P)
U = B * H0


def wait(eng, semaphore, value):
    if not isinstance(value, int) or value > 0:
        eng.wait_ge(semaphore, value)


def cross_ffn_network(nc, x, ctx_tok, ctx_t, l0_wq_t, l0_wk_t, l0_wv, l0_wo, l0_bo, f0_wg, f0_w1, f0_b1,
                      f0_wo_t, f0_bo, l1_qw, l1_qb, l1_kw, l1_kb, l1_vw, l1_vb, l1_g, l1_b, l1_tg, l1_tb,
                      f1_cx, f1_cd, f1_wg, f1_wu, f1_wd, out):
    with ExitStack() as ctx:
        def sb(name, shape, dt=F32):
            return ctx.enter_context(nc.sbuf_tensor(name, shape, dt))

        def sem(name):
            return ctx.enter_context(nc.semaphore(name))

        banks = [ctx.enter_context(nc.psum_tensor(f"bank{i}", [P, 512], F32)) for i in range(8)]

        height = [min(P, FF - P * i) for i in range(FT)]

        xres = sb("xres", [P, NT, D])
        ident = sb("ident", [P, P])
        ctx_halves = sb("ctx_halves", [P, 2 * N], F16)
        ctx_hi, ctx_lo = ctx_halves[:, 0:N], ctx_halves[:, N:2 * N]
        zt_halves = sb("zt_halves", [P, 2 * N], F16)
        zt_hi, zt_lo = zt_halves[:, 0:N], zt_halves[:, N:2 * N]
        m_hi = sb("m_hi", [P, H0, C], F16)
        m_lo = sb("m_lo", [P, H0, C], F16)
        bo_bc = sb("bo_bc", [P, D])
        wo = sb("wo", [P, H0 // 2, D])
        stats = sb("stats", [P, NT, 6])
        mv = sb("mv", [P, NT, 2])
        var_eps = sb("var_eps", [P, NT])
        rstd = sb("rstd", [P, NT])
        minus_half = sb("minus_half", [P, NT])
        eps_add = sb("eps_add", [P, NT])
        gate = sb("gate", [P, NT, E])
        fbo_bc = sb("fbo_bc", [P, D])
        fwo_t = sb("fwo_t", [P, HF // P, D])
        gu_max = sb("gu_max", [P, 2, FT])
        gu_scale = sb("gu_scale", [P, 2, FT])
        gu_inv = sb("gu_inv", [P, 2, FT])
        wd_max = sb("wd_max", [D, 1])
        wd_scale = sb("wd_scale", [D, 1])
        wd_inv = sb("wd_inv", [D, 1])
        arena_v = sb("arena_v", [P, NT * H0 * (2 * DH0 + 1)], F16)
        arena_o = sb("arena_o", [P, NT * H0 * DH0])
        v_hi = arena_v[:, 0:NT * H0 * (DH0 + 1)].rearrange("p (t h d) -> p t h d", t=NT, h=H0)
        v_lo = arena_v[:, NT * H0 * (DH0 + 1):].rearrange("p (t h d) -> p t h d", t=NT, h=H0)
        o_all = arena_o[:, :].rearrange("p (t h d) -> p t h d", t=NT, h=H0)

        at = 0

        def temp(width):
            nonlocal at
            at += width
            return arena_o[:, at - width:at]

        wq_t = temp(H0 * P).rearrange("p (h d) -> p h d", h=H0)
        wk_t = temp(H0 * P).rearrange("p (h c) -> p h c", h=H0)
        ctx_raw = temp(N)
        wv_raw = temp(H0 * DH0)
        z0 = temp(NT * D).rearrange("p (t d) -> p t d", t=NT)
        wv_hi = temp(H0 * DH0 // 2).bitcast(F16)
        wv_lo = temp(H0 * DH0 // 2).bitcast(F16)

        ld_x, ld_ctx, ld_wq, ld_wk, ld_wv, ld_wo = (sem(f"ld_{n}") for n in ("x", "ctx", "wq", "wk", "wv", "wo"))
        pads, idents, consts = sem("pads"), sem("idents"), sem("consts")
        st0, mv0, ve0, rs0, z0_ready = (sem(n) for n in ("st0", "mv0", "ve0", "rs0", "z0_ready"))
        ctx_hi_ready, ctx_lo_ready, wv_hi_ready, wv_lo_ready = (
            sem(n) for n in ("ctx_hi_ready", "ctx_lo_ready", "wv_hi_ready", "wv_lo_ready"))
        p0_mm, p0_hi, p0_lo = sem("p0_mm"), sem("p0_hi"), sem("p0_lo")
        NM = H0 // 4
        NV = NT * 2
        Z_AT = NM + NV
        HH = H0 // 2

        with nc.Block() as block:
            @block.sync
            def _(sp):
                sp.dma_start(xres[:, :, :], x).then_inc(ld_x, 16)
                sp.dma_start(ctx_raw[0:C, :], ctx_t).then_inc(ld_ctx, 16)
                sp.dma_start(wv_raw[0:C, :], l0_wv).then_inc(ld_wv, 16)
                sp.dma_start(wq_t[0:DH0, :, :], l0_wq_t).then_inc(ld_wq, 16)
                sp.dma_start(wk_t[0:DH0, :, 0:C], l0_wk_t).then_inc(ld_wk, 16)
                sp.dma_start(wo[:, :, :], l0_wo).then_inc(ld_wo, 16)
                sp.dma_start(bo_bc[:, :], l0_bo.partition_broadcast(P)).then_inc(ld_wo, 16)

            @block.gpsimd
            def _(pool):
                nc.gpsimd.memset(minus_half[:, :], -0.5).then_inc(consts, 1)
                nc.gpsimd.memset(ident[:, :], 0.0).then_inc(idents, 1)
                pool.wait_ge(idents, 1)
                nc.gpsimd.affine_select(out=ident[:, :], in_=ident[:, :], compare_op=ALU.not_equal, fill=1.0,
                                        base=0, pattern=[[-1, P]], channel_multiplier=1).then_inc(idents, 1)
                pool.wait_ge(ve0, 1)
                pool.wait_ge(consts, 1)
                nc.gpsimd.tensor_tensor(rstd[:, :], var_eps[:, :], minus_half[:, :], ALU.pow).then_inc(rs0, 1)
                pool.wait_ge(z0_ready, NT)
                pool.wait_ge(ld_wo, 32)
                nc.gpsimd.tensor_tensor(xres[:, :, :], xres[:, :, :],
                                        bo_bc[:, :].unsqueeze(1).to_broadcast([P, NT, D]),
                                        ALU.add)

            @block.scalar
            def _(act):
                act.wait_ge(ld_ctx, 16)
                nc.scalar.activation(ctx_hi[0:C, :], ctx_raw[0:C, :], ACT.Copy).then_inc(ctx_hi_ready, 1)
                act.wait_ge(ld_wv, 16)
                nc.scalar.activation(wv_hi[0:C, :], wv_raw[0:C, :], ACT.Copy).then_inc(wv_hi_ready, 1)
                for n in range(NM):
                    act.wait_ge(p0_mm, n + 1)
                    nc.scalar.activation(m_hi[:, 4 * n:4 * n + 4, :],
                                         banks[n % 8][:, :].rearrange("p (h c) -> p h c", h=4)[:, :, 0:C],
                                         ACT.Copy).then_inc(p0_hi, 1)

                def value_halves(k):
                    for j in range(8):
                        act.wait_ge(p0_mm, k * 8 + (NM + j + 1))
                        nc.scalar.activation(v_hi[:, k * 4 + j // 2, HH * (j % 2):HH * (j % 2) + HH, 0:DH0],
                                             banks[(NM + j) % 8][:, :].rearrange("p (h d) -> p h d", h=HH),
                                             ACT.Copy).then_inc(p0_hi, 1)
                with act.Fori(0, NV // 8) as k:
                    value_halves(k)
                for n in range(NT // 4):
                    act.wait_ge(p0_mm, Z_AT + n + 1)
                    nc.scalar.activation(zt_hi[:, 512 * n:512 * n + 512], banks[(Z_AT + n) % 8][:, :],
                                         ACT.Copy).then_inc(p0_hi, 1)

            @block.vector
            def _(dve):
                nc.vector.memset(wq_t[DH0:P, :, :], 0.0).then_inc(pads, 1)
                nc.vector.memset(wk_t[DH0:P, :, :], 0.0).then_inc(pads, 1)
                nc.vector.memset(wk_t[0:DH0, :, C:P], 0.0).then_inc(pads, 1)
                nc.vector.memset(ctx_hi[C:C + 1, :], 1.0)
                nc.vector.memset(v_hi[:, :, :, DH0:DH0 + 1], 1.0)
                dve.wait_ge(ld_x, 16)
                for t in range(NT):
                    nc.vector.bn_stats(stats[:, t, :], xres[:, t, :]).then_inc(st0, 1)
                for t in range(NT):
                    dve.wait_ge(st0, t + 1)
                    nc.vector.bn_aggr(mv[:, t, :], stats[:, t, :]).then_inc(mv0, 1)
                dve.wait_ge(mv0, NT)
                nc.vector.tensor_scalar(var_eps[:, :], mv[:, :, 1], LN_EPS, None, ALU.add).then_inc(ve0, 1)
                dve.wait_ge(ctx_hi_ready, 1)
                nc.vector.tensor_tensor(ctx_lo[0:C, :], ctx_raw[0:C, :], ctx_hi[0:C, :],
                                        ALU.subtract).then_inc(ctx_lo_ready, 1)
                dve.wait_ge(wv_hi_ready, 1)
                nc.vector.tensor_tensor(wv_lo[0:C, :], wv_raw[0:C, :], wv_hi[0:C, :],
                                        ALU.subtract).then_inc(wv_lo_ready, 1)
                dve.wait_ge(rs0, 1)
                for t in range(NT):
                    nc.vector.tensor_scalar(z0[:, t, :], xres[:, t, :], mv[:, t, 0:1], rstd[:, t:t + 1],
                                            ALU.subtract, ALU.mult).then_inc(z0_ready, 1)
                for n in range(NM):
                    dve.wait_ge(p0_hi, n + 1)
                    nc.vector.tensor_tensor(m_lo[:, 4 * n:4 * n + 4, :],
                                            banks[n % 8][:, :].rearrange("p (h c) -> p h c", h=4)[:, :, 0:C],
                                            m_hi[:, 4 * n:4 * n + 4, :], ALU.subtract).then_inc(p0_lo, 1)
                with dve.Fori(0, NV // 8) as k:
                    for j in range(8):
                        heads = slice(HH * (j % 2), HH * (j % 2) + HH)
                        dve.wait_ge(p0_hi, k * 8 + (NM + j + 1))
                        nc.vector.tensor_tensor(v_lo[:, k * 4 + j // 2, heads, :],
                                                banks[(NM + j) % 8][:, :].rearrange("p (h d) -> p h d", h=HH),
                                                v_hi[:, k * 4 + j // 2, heads, 0:DH0],
                                                ALU.subtract).then_inc(p0_lo, 1)
                for n in range(NT // 4):
                    dve.wait_ge(p0_hi, Z_AT + n + 1)
                    nc.vector.tensor_tensor(zt_lo[:, 512 * n:512 * n + 512], banks[(Z_AT + n) % 8][:, :],
                                            zt_hi[:, 512 * n:512 * n + 512], ALU.subtract).then_inc(p0_lo, 1)

            @block.tensor
            def _(pe):
                pe.wait_ge(ld_wq, 16)
                pe.wait_ge(ld_wk, 16)
                pe.wait_ge(pads, 3)
                for h in range(H0):
                    last = nc.tensor.matmul(banks[h // 4][:, P * (h % 4):P * (h % 4) + P],
                                            wq_t[:, h, :], wk_t[:, h, :], start=True, stop=True)
                    if h % 4 == 3:
                        last.then_inc(p0_mm, 1)
                pe.wait_ge(ctx_lo_ready, 1)
                pe.wait_ge(wv_lo_ready, 1)

                def values(k):
                    for j in range(8):
                        wait(pe, p0_lo, k * 8 + (NM + j - 7))
                        tokens = bass.ds(k * 512 + (j // 2) * P, P)
                        heads = slice(512 * (j % 2), 512 * (j % 2) + 512)
                        bank = banks[(NM + j) % 8]
                        nc.tensor.matmul(bank[:, :], ctx_hi[0:C, tokens], wv_hi[0:C, heads], start=True, stop=False)
                        nc.tensor.matmul(bank[:, :], ctx_lo[0:C, tokens], wv_hi[0:C, heads], start=False, stop=False)
                        nc.tensor.matmul(bank[:, :], ctx_hi[0:C, tokens], wv_lo[0:C, heads], start=False,
                                         stop=True).then_inc(p0_mm, 1)
                values(0)
                with pe.Fori(1, NV // 8) as k:
                    values(k)
                pe.wait_ge(idents, 2)
                pe.wait_ge(z0_ready, NT)
                for n in range(NT // 4):
                    wait(pe, p0_lo, Z_AT + n - 7)
                    for j in range(4):
                        last = nc.tensor.transpose(banks[(Z_AT + n) % 8][:, P * j:P * j + P], z0[:, 4 * n + j, :],
                                                   ident[:, :])
                    last.then_inc(p0_mm, 1)

        scratch = ExitStack()

        def sb1(name, shape, dt=F32):
            return scratch.enter_context(nc.sbuf_tensor(name, shape, dt))

        RING = 4
        t_hi = sb1("t_hi", [P, H0, S], F16)
        t_lo = sb1("t_lo", [P, H0, S], F16)
        p32 = sb1("p32", [P, 2, QT * S])
        p_hi = sb1("p_hi", [P, RING, QT * S], F16)
        p_lo = sb1("p_lo", [P, RING, QT * S], F16)
        neg_max = sb1("neg_max", [P, 2, 4 * QT])
        neg_max_t = sb1("neg_max_t", [4 * QT, 2, P], F16)
        rsum = sb1("rsum", [P, 2, QT, 2])
        t_bank, max_bank, score_bank, o_bank = banks[0:2], banks[2:4], banks[4:6], banks[6:8]
        SHIFT_AT = 384
        LEAD_T, LEAD_MAX, LEAD_SHIFT = 12, 10, 5
        LAG_PV = 2
        SCALE0 = DH0 ** -0.5

        t_done, t_hi_ready, t_lo_ready, max_done, max_read = (
            sem(n) for n in ("t_done", "t_hi_ready", "t_lo_ready", "max_done", "max_read"))
        shift_in_psum, shift_read, scores_done, p32_ready, lo_ready, pv_done, sum_inverted, o_read = (
            sem(n) for n in ("shift_in_psum", "shift_read", "scores_done", "p32_ready", "lo_ready",
                             "pv_done", "sum_inverted", "o_read"))
        shift_row = [sem("shift_row_even"), sem("shift_row_odd")]

        def steps(eng, step):
            for s in range(-LEAD_T, 4):
                step(0, s)
            with eng.Fori(0, B - 1) as b:
                for s in range(4, 4 + H0):
                    step(b, s)
            for s in range(4, H0 + 5):
                step(B - 1, s)

        def there(b, s):
            return not isinstance(b, int) or 0 <= H0 * b + s < U

        def count(b, s):
            return b * H0 + s

        with nc.Block() as block:
            @block.tensor
            def _(pe):
                def make_t(b, s):
                    if s % 2 == 0:
                        wait(pe, t_lo_ready, count(b, s) // 2 - 1 if isinstance(b, int) else b * 8 + (s // 2 - 1))
                    tokens = bass.ds((b + s // H0) * S, S)
                    h = s % H0
                    dst = t_bank[(s // 2) % 2][0:C, S * (s % 2):S * (s % 2) + S]
                    nc.tensor.matmul(dst, m_hi[:, h, :], zt_hi[:, tokens], start=True, stop=False)
                    nc.tensor.matmul(dst, m_hi[:, h, :], zt_lo[:, tokens], start=False, stop=False)
                    nc.tensor.matmul(dst, m_lo[:, h, :], zt_hi[:, tokens], start=False, stop=True).then_inc(t_done, 1)

                def maxima(b, s):
                    pe.wait_ge(t_hi_ready, b * 8 + (s // 2 + 1))
                    wait(pe, max_read, count(b, s) - 1)
                    keys = bass.ds((b + s // H0) * S, S)
                    for q in range(QT):
                        last = nc.tensor.matmul(max_bank[s % 2][:, S * q:S * q + S],
                                                t_hi[0:C, s % H0, P * q:P * q + P], ctx_hi[0:C, keys],
                                                start=True, stop=True)
                    last.then_inc(max_done, 1)

                def shift(b, s):
                    pe.wait_ge(max_read, count(b, s) + 4)
                    wait(pe, shift_read, b * 4 + s // 4)
                    nc.tensor.transpose(o_bank[0][0:4 * QT, SHIFT_AT:SHIFT_AT + P], neg_max[:, (s // 4) % 2, :],
                                        ident[:, :]).then_inc(shift_in_psum, 1)

                def scores(b, s):
                    if s % 4 == 0:
                        pe.wait_ge(shift_row[(s // 4) % 2], b * 32 + 16 * (s // 8 + 1))
                    wait(pe, p32_ready, count(b, s) - 1)
                    h = s % H0
                    if s % 2 == 0:
                        pe.wait_ge(t_lo_ready, b * 8 + (s // 2 + 1))
                    for k in range(QT):
                        dst = score_bank[s % 2][:, S * k:S * k + S]
                        keys = bass.ds((b + s // H0) * S + P * k, P)
                        nc.tensor.matmul(dst, ctx_hi[0:C + 1, keys], t_hi[0:C + 1, h, :], start=True, stop=False)
                        nc.tensor.matmul(dst, ctx_hi[0:C, keys], t_lo[0:C, h, :], start=False, stop=False)
                        last = nc.tensor.matmul(dst, ctx_lo[0:C, keys], t_hi[0:C, h, :], start=False, stop=True)
                    last.then_inc(scores_done, 1)

                def values(b, s):
                    r, h, left = s % RING, s % H0, s % 2
                    if s % 2 == 0:
                        wait(pe, o_read, (count(b, s) // 2 - 1) if isinstance(b, int) else b * 8 + (s // 2 - 1))
                    pe.wait_ge(lo_ready, count(b, s) + 1)
                    for q in range(QT):
                        c0 = (DH0 + 1) * (2 * q + left)
                        dst = o_bank[(s // 2) % 2][:, c0:c0 + DH0 + 1]
                        for k in range(QT):
                            tile = b * QT + (s // H0 * QT + k)
                            w = slice(S * k + P * q, S * k + P * q + P)
                            nc.tensor.matmul(dst, p_hi[:, r, w], v_hi[:, tile, h, :], start=(k == 0), stop=False)
                            nc.tensor.matmul(dst[:, 0:DH0], p_hi[:, r, w], v_lo[:, tile, h, :], start=False, stop=False)
                            last = nc.tensor.matmul(dst, p_lo[:, r, w], v_hi[:, tile, h, :], start=False,
                                                    stop=(k == QT - 1))
                    last.then_inc(pv_done, 1)

                def step(b, s):
                    if there(b, s):
                        scores(b, s)
                    if there(b, s + LEAD_T):
                        make_t(b, s + LEAD_T)
                    if there(b, s + LEAD_MAX):
                        maxima(b, s + LEAD_MAX)
                    if (s + LEAD_SHIFT) % 4 == 0 and there(b, s + LEAD_SHIFT):
                        shift(b, s + LEAD_SHIFT)
                    if there(b, s - LAG_PV):
                        values(b, s - LAG_PV)
                steps(pe, step)

            @block.scalar
            def _(act):
                def exps(b, s):
                    r = s % 2
                    act.wait_ge(scores_done, count(b, s) + 1)
                    wait(act, pv_done, count(b, s) + 1 - RING)
                    nc.scalar.activation(p_hi[:, s % RING, :], score_bank[r][:, :], ACT.Exp, scale=SCALE0)
                    wait(act, lo_ready, count(b, s) - 1)
                    nc.scalar.activation(p32[:, r, :], score_bank[r][:, :], ACT.Exp, scale=SCALE0).then_inc(p32_ready, 1)

                def t_halves(b, s):
                    act.wait_ge(t_done, count(b, s) + 1)
                    wait(act, scores_done, count(b, s) + 1 - H0)
                    h = (s - 1) % H0
                    nc.scalar.activation(t_hi[0:C, h:h + 2, :],
                                         t_bank[(s // 2) % 2][0:C, :].rearrange("p (h q) -> p h q", h=2),
                                         ACT.Copy).then_inc(t_hi_ready, 1)

                def step(b, s):
                    if there(b, s):
                        exps(b, s)
                    if s % 2 == 1 and there(b, s + LEAD_T):
                        t_halves(b, s + LEAD_T)
                steps(act, step)

            @block.gpsimd
            def _(pool):
                def step(b, s):
                    if there(b, s):
                        r = s % RING
                        pool.wait_ge(p32_ready, count(b, s) + 1)
                        wait(pool, pv_done, count(b, s) + 1 - RING)
                        nc.gpsimd.tensor_tensor(p_lo[:, r, :], p32[:, s % 2, :], p_hi[:, r, :],
                                                ALU.subtract).then_inc(lo_ready, 1)
                steps(pool, step)

            @block.vector
            def _(dve):
                def t_rest(b, s):
                    pair = b * 8 + ((s - 1) // 2)
                    h = (s - 1) % H0
                    dve.wait_ge(t_hi_ready, pair + 1)
                    nc.vector.tensor_tensor(t_lo[0:C, h:h + 2, :],
                                            t_bank[(s // 2) % 2][0:C, :].rearrange("p (h q) -> p h q", h=2),
                                            t_hi[0:C, h:h + 2, :], ALU.subtract).then_inc(t_lo_ready, 1)

                def max_of(b, s):
                    g, j = (s // 4) % 2, s % 4
                    dve.wait_ge(max_done, count(b, s) + 1)
                    if j == 0:
                        wait(dve, shift_in_psum, (count(b, s) // 4 - 1) if isinstance(b, int) else b * 4 + (s // 4 - 1))
                    nc.vector.tensor_reduce(neg_max[:, g, QT * j:QT * j + QT],
                                            max_bank[s % 2][:, :].rearrange("p (q k) -> p q k", q=QT),
                                            AX.X, ALU.max, negate=True).then_inc(max_read, 1)

                def shift_out(b, s):
                    g = (s // 4) % 2
                    dve.wait_ge(shift_in_psum, b * 4 + (s // 4 + 1))
                    before = b * 32 + 16 * (s // 8)
                    wait(dve, shift_row[g], before)
                    nc.vector.tensor_copy(neg_max_t[:, g, :], o_bank[0][0:4 * QT, SHIFT_AT:SHIFT_AT + P])\
                        .then_inc(shift_read, 1)

                def output(b, s):
                    pair = b * 8 + (s // 2)
                    g, h = (s // 2) % 2, (s - 1) % H0
                    dve.wait_ge(pv_done, count(b, s) + 1)
                    o = o_bank[g][:, 0:QT * 2 * (DH0 + 1)].rearrange("p (q h d) -> p q h d", q=QT, h=2)
                    nc.vector.reciprocal(rsum[:, g, :, :], o[:, :, :, DH0]).then_inc(sum_inverted, 1)
                    dve.wait_ge(sum_inverted, pair + 1)
                    nc.vector.tensor_tensor(o_all[:, bass.ds((b + s // H0) * QT, QT), h:h + 2, :], o[:, :, :, 0:DH0],
                                            rsum[:, g, :, :].unsqueeze(3).to_broadcast([P, QT, 2, DH0]),
                                            ALU.mult).then_inc(o_read, 1)

                def step(b, s):
                    if s % 2 == 1 and there(b, s + LEAD_T):
                        t_rest(b, s + LEAD_T)
                    if there(b, s + LEAD_MAX):
                        max_of(b, s + LEAD_MAX)
                    if (s + LEAD_SHIFT) % 4 == 0 and there(b, s + LEAD_SHIFT):
                        if there(b, s - LAG_PV):
                            dve.wait_ge(pv_done, count(b, s - LAG_PV) + 1)
                        shift_out(b, s + LEAD_SHIFT)
                    if (s - LAG_PV) % 2 == 1 and there(b, s - LAG_PV):
                        output(b, s - LAG_PV)
                steps(dve, step)

            @block.sync
            def _(sp):
                def step(b, s):
                    if (s + LEAD_SHIFT) % 4 == 0 and there(b, s + LEAD_SHIFT):
                        u = s + LEAD_SHIFT
                        g, h = (u // 4) % 2, u % H0
                        sp.wait_ge(shift_read, b * 4 + (u // 4 + 1))
                        sp.dma_start(t_hi[C:C + 1, h:h + 4, :], neg_max_t[:, g, :]).then_inc(shift_row[g], 16)
                steps(sp, step)

        scratch.close()

        layer1 = ExitStack()
        scratch = ExitStack()
        at = 0

        def sb2(name, shape, dt=F32):
            return layer1.enter_context(nc.sbuf_tensor(name, shape, dt))

        def temp_v(width):
            nonlocal at
            at += width
            return arena_v[:, 2 * (at - width):2 * at].bitcast(F32)

        w1_raw = temp_v(E * HG * D).rearrange("p (r d) -> p r d", d=D)
        w1t_hi = temp_v(E * 2 * HF // 2).bitcast(F16)
        w1t_lo = temp_v(E * 2 * HF // 2).bitcast(F16)
        NR = E * 2 * HF // P
        ctx_n = temp_v(NT * C).rearrange("p (t c) -> p t c", t=NT)
        zc_t = temp_v(N)[0:C + 1, :]
        gu_raw = temp_v(2 * FT * D).rearrange("p (s i d) -> p s i d", s=2, i=FT)
        wd_raw = temp_v(FF)
        wd_diag = temp_v(D)
        ones = temp_v(P)
        GT = H1 // 4
        ROWS = 32
        SHIFT_ROW = 3 * DH1
        kw_ext = sb2("kw_ext", [C + 1, D])
        vw_ext = sb2("vw_ext", [C + 1, D])
        tb_ext = sb2("tb_ext", [C + 1, 1])
        tg_col = sb2("tg_col", [C, 1])
        qw = sb2("qw", [D, D])
        qb_row = sb2("qb_row", [1, D])
        g_col = sb2("g_col", [D, 1])
        b_col = sb2("b_col", [D, 1])
        k_rows = sb2("k_rows", [C + 1, GT, 4, ROWS])
        k_arr = sb2("k_arr", [C + 1, GT, 4 * ROWS])
        q_rows = sb2("q_rows", [D, GT, 4, ROWS])
        q_arr = sb2("q_arr", [D, GT, 4 * ROWS])
        qb_rows = sb2("qb_rows", [1, GT, 4, ROWS])
        one = sb2("one", [1, 1])
        v_arr = sb2("v_arr", [C + 1, D])
        q_bias = sb2("q_bias", [P, GT])
        k_low = sb2("k_low", [P, 1])
        q_low = sb2("q_low", [P, 1])
        zero = sb2("zero", [P, 1])
        v1 = sb2("v1", [P, NT, D])
        v_stage = sb2("v_stage", [P, QT, H1, ROWS])
        cstats = sb1("cstats", [P, NT, 6])
        cmv = sb1("cmv", [P, NT, 2])
        cvar = sb1("cvar", [P, NT])
        crstd = sb1("crstd", [P, NT])
        ld4, ld4c, ldw6 = sem("ld4"), sem("ld4c"), sem("ldw6")
        rows_zero, rows_ones, zc_ones, rows_filled, gains_in = (
            sem(n) for n in ("rows_zero", "rows_ones", "zc_ones", "rows_filled", "gains_in"))
        stc, mvc, vec, rsc, zc_ready, bias_done, bias_read, zct_done, zct_read, v1_done, v1_read = (
            sem(n) for n in ("stc", "mvc", "vec", "rsc", "zc_ready", "bias_done", "bias_read", "zct_done", "zct_read",
                             "v1_done", "v1_read"))
        o_t = sb1("o_t", [P, 2, H0 // 2, P])
        z1 = sb1("z1", [P, 2, D])
        b1_cols = sb1("b1_cols", [P, NR])
        wg_raw = sb1("wg_raw", [E, D])
        wg_shift = sb1("wg_shift", [E, D])
        wgt_hi = sb1("wgt_hi", [P, E], F16)
        wgt_lo = sb1("wgt_lo", [P, E], F16)
        logit_max = sb1("logit_max", [P, NT])
        prob = sb1("prob", [P, NT, E])
        over, over_eq = (temp_v(NT * E * E).rearrange("p (t e o) -> p t e o", t=NT, e=E) for _ in range(2))
        later = sb1("later", [P, E, E])
        earlier = sb1("earlier", [P, E, E])
        rank = sb1("rank", [P, NT, E])
        esum = sb1("esum", [P, NT])
        einv = sb1("einv", [P, NT])
        csum = sb1("csum", [P, NT])
        o_front, o_back, side_bank, y_bank, z_bank, g_bank = banks[0], banks[1], banks[2:4], banks[4:6], banks[6], banks[7]
        ld_w1, ld_wg, ld_b1, ld_f0 = sem("ld_w1"), sem("ld_wg"), sem("ld_b1"), sem("ld_f0")
        o_t_done, o_front_read, o_back_read, y1_done, x1_ready = (
            sem(n) for n in ("o_t_done", "o_front_read", "o_back_read", "y1_done", "x1_ready"))
        st1, mv1, ve1, rs1, z1_ready, z1t_done, z1_hi_ready, z1_lo_ready = (
            sem(n) for n in ("st1", "mv1", "ve1", "rs1", "z1_ready", "z1t_done", "z1_hi_ready", "z1_lo_ready"))
        wg_shifted, wgt_done, wgt_hi_ready, wgt_lo_ready, gates_done = (
            sem(n) for n in ("wg_shifted", "wgt_done", "wgt_hi_ready", "wgt_lo_ready", "gates_done"))
        w1_shifted, w1_bias, w1t_done, w1t_hi_ready, w1t_lo_ready = (
            sem(n) for n in ("w1_shifted", "w1_bias", "w1t_done", "w1t_hi_ready", "w1t_lo_ready"))
        masks_set, route, prob_ready = sem("masks_set"), sem("route"), sem("prob_ready")
        LAG_PROJECT, LAG_Z, LAG_ZT, LAG_GATE = 1, 2, 3, 4
        LAST = NT + LAG_GATE
        W1_AT, BIAS_AT, ZC_AT, V_AT = 5, 7, 10, 14
        W1_UNITS = NR // 4

        with nc.Block() as block:
            @block.sync
            def _(sp):
                sp.dma_start(wg_raw[:, :], f0_wg).then_inc(ld_wg, 16)
                sp.dma_start(b1_cols[:, :], f0_b1).then_inc(ld_b1, 16)
                sp.dma_start(ctx_n, ctx_tok).then_inc(ld4c, 16)
                with nc.allow_non_contiguous_dma(reason="a number per partition"):
                    for dst, src in ((kw_ext[0:C, :], l1_kw), (kw_ext[C:C + 1, :], l1_kb.unsqueeze(0)),
                                     (vw_ext[0:C, :], l1_vw), (vw_ext[C:C + 1, :], l1_vb.unsqueeze(0)),
                                     (tb_ext[0:C, :], l1_tb.unsqueeze(1)), (tg_col[:, :], l1_tg.unsqueeze(1)),
                                     (qw[:, :], l1_qw), (qb_row[:, :], l1_qb.unsqueeze(0)),
                                     (g_col[:, :], l1_g.unsqueeze(1)), (b_col[:, :], l1_b.unsqueeze(1))):
                        sp.dma_start(dst, src).then_inc(ld4, 16)
                sp.dma_start(w1_raw, f0_w1).then_inc(ld_w1, 16)
                sp.dma_start(fwo_t[:, :, :], f0_wo_t).then_inc(ld_f0, 16)
                sp.dma_start(fbo_bc[:, :], f0_bo.partition_broadcast(P)).then_inc(ld_f0, 16)
                for side, src in ((0, f1_wg), (1, f1_wu)):
                    for i in range(FT):
                        sp.dma_start(gu_raw[0:height[i], side, i, :], src[P * i:P * i + height[i], :]).then_inc(ldw6, 16)
                sp.dma_start(wd_raw[:, :], f1_wd).then_inc(ldw6, 16)

            @block.tensor
            def _(pe):
                for i in range(LAST):
                    t = i
                    if t < NT:
                        wait(pe, o_front_read, t)
                        wait(pe, o_back_read, t)
                        for c in range(H0 // 2):
                            last = nc.tensor.transpose((o_front, o_back)[c // 4][:, P * (c % 4):P * (c % 4) + P],
                                                       arena_o[:, (t * 8 + c) * P:(t * 8 + c) * P + P], ident[:, :])
                        last.then_inc(o_t_done, 1)
                    if i == LAG_PROJECT:
                        pe.wait_ge(wg_shifted, 2)
                        nc.tensor.transpose(z_bank[:, 0:E], wg_shift[:, :], ident[0:E, 0:E]).then_inc(wgt_done, 1)
                    if 0 <= i - W1_AT < W1_UNITS:
                        n = i - W1_AT
                        pe.wait_ge(w1_bias, n + 1)
                        wait(pe, w1t_lo_ready, n)
                        for j in range(4):
                            last = nc.tensor.transpose(side_bank[0][:, P * j:P * j + P], w1_raw[:, 4 * n + j, :],
                                                       ident[:, :])
                        last.then_inc(w1t_done, 1)
                    t = i - LAG_PROJECT
                    if 0 <= t < NT:
                        pe.wait_ge(o_front_read, t + 1)
                        pe.wait_ge(o_back_read, t + 1)
                        wait(pe, x1_ready, t - 1)
                        for c in range(H0 // 2):
                            last = nc.tensor.matmul(y_bank[t % 2][:, 0:D], o_t[:, t % 2, c, :], wo[:, c, :],
                                                    start=(c == 0), stop=(c == H0 // 2 - 1))
                        last.then_inc(y1_done, 1)
                    t = i - LAG_ZT
                    if 0 <= t < NT:
                        pe.wait_ge(z1_ready, t + 1)
                        pe.wait_ge(wgt_lo_ready, 1)
                        wait(pe, z1_lo_ready, t)
                        nc.tensor.transpose(z_bank[:, 0:P], z1[:, t % 2, :], ident[:, :]).then_inc(z1t_done, 1)
                    t = i - LAG_GATE
                    if 0 <= t < NT:
                        pe.wait_ge(z1_lo_ready, t + 1)
                        tokens = slice(P * t, P * t + P)
                        nc.tensor.matmul(g_bank[:, E * t:E * t + E], zt_hi[:, tokens], wgt_hi[:, :], start=True, stop=False)
                        nc.tensor.matmul(g_bank[:, E * t:E * t + E], zt_lo[:, tokens], wgt_hi[:, :], start=False, stop=False)
                        nc.tensor.matmul(g_bank[:, E * t:E * t + E], zt_hi[:, tokens], wgt_lo[:, :], start=False,
                                         stop=True).then_inc(gates_done, 1)
                    if i == BIAS_AT:
                        bank = side_bank[1]
                        pe.wait_ge(rows_filled, 9)
                        pe.wait_ge(rows_ones, 3)
                        for g in range(GT):
                            nc.tensor.matmul(bank[:, g:g + 1], q_rows[:, g, :, :].rearrange("p j r -> p (j r)"),
                                             b_col[:, :], start=True, stop=False)
                            nc.tensor.matmul(bank[:, g:g + 1], qb_rows[:, g, :, :].rearrange("p j r -> p (j r)"),
                                             one[:, :], start=False, stop=True)
                        nc.tensor.matmul(bank[C:C + 1, P:2 * P], tb_ext[:, :], vw_ext[:, :], start=True, stop=True)\
                            .then_inc(bias_done, 1)
                    if i == BIAS_AT + 1:
                        pe.wait_ge(bias_read, 2)
                        nc.tensor.matmul(side_bank[1][C:C + 1, :], tb_ext[:, :],
                                         k_rows[:, :, :, :].rearrange("p g j r -> p (g j r)"), start=True,
                                         stop=True).then_inc(bias_done, 1)
                    if 0 <= i - ZC_AT < NT // 4:
                        n = i - ZC_AT
                        pe.wait_ge(zc_ready, 4 * n + 4)
                        if n == 0:
                            pe.wait_ge(bias_read, 3)
                        wait(pe, zct_read, n)
                        for j in range(4):
                            last = nc.tensor.transpose(side_bank[1][0:C, P * j:P * j + P],
                                                       ctx_n[:, 4 * n + j, :], ident[:, :])
                        last.then_inc(zct_done, 1)
                    if 0 <= i - V_AT < NT // 4:
                        n = i - V_AT
                        pe.wait_ge(zct_read, NT // 4)
                        wait(pe, v1_read, n)
                        if n == 0:
                            pe.wait_ge(gains_in, 3)
                            pe.wait_ge(zc_ones, 1)
                        for j in range(4):
                            t = 4 * n + j
                            last = nc.tensor.matmul(side_bank[1][:, P * j:P * j + P],
                                                    zc_t[:, P * t:P * t + P], v_arr[:, :], start=True, stop=True)
                        last.then_inc(v1_done, 1)

            @block.scalar
            def _(act):
                for i in range(LAST):
                    t = i
                    if t < NT:
                        act.wait_ge(o_t_done, t + 1)
                        wait(act, y1_done, t - 1)
                        nc.scalar.activation(o_t[:, t % 2, 0:4, :], o_front[:, :].rearrange("p (c q) -> p c q", c=4),
                                             ACT.Copy).then_inc(o_front_read, 1)
                    if i == LAG_PROJECT:
                        act.wait_ge(wgt_done, 1)
                        nc.scalar.activation(wgt_hi[:, :], z_bank[:, 0:E], ACT.Copy, scale=W_SCALE).then_inc(wgt_hi_ready, 1)
                    t = i - LAG_ZT
                    if 0 <= t < NT:
                        act.wait_ge(z1t_done, t + 1)
                        nc.scalar.activation(zt_hi[:, P * t:P * t + P], z_bank[:, 0:P], ACT.Copy).then_inc(z1_hi_ready, 1)
                    if 0 <= i - W1_AT < W1_UNITS:
                        n = i - W1_AT
                        act.wait_ge(w1t_done, n + 1)
                        nc.scalar.activation(w1t_hi[:, 512 * n:512 * n + 512], side_bank[0][:, :], ACT.Copy,
                                             scale=W_SCALE).then_inc(w1t_hi_ready, 1)
                    if i in (3, 4, 5):
                        act.wait_ge(ld4, 160)
                        act.wait_ge(rows_zero, 4)
                        w = slice(DH1 * (i - 3), DH1 * (i - 3) + DH1)
                        for dst, src in ((k_rows, kw_ext), (q_rows, qw), (qb_rows, qb_row)):
                            nc.scalar.activation(dst[:, :, :, w], src[:, :].rearrange("p (g j d) -> p g j d", g=GT, j=4),
                                                 ACT.Copy).then_inc(rows_filled, 1)
                    if i == BIAS_AT:
                        act.wait_ge(bias_done, 1)
                        nc.scalar.activation(q_bias[:, :], side_bank[1][:, 0:GT], ACT.Copy).then_inc(bias_read, 1)
                        nc.scalar.activation(v_arr[C:C + 1, :], side_bank[1][C:C + 1, P:2 * P],
                                             ACT.Copy).then_inc(bias_read, 1)
                    if i == BIAS_AT + 1:
                        act.wait_ge(bias_done, 2)
                        nc.scalar.activation(k_arr[C:C + 1, :, :].rearrange("p g r -> p (g r)"),
                                             side_bank[1][C:C + 1, :], ACT.Copy).then_inc(bias_read, 1)
                    if 0 <= i - ZC_AT < NT // 4:
                        n = i - ZC_AT
                        act.wait_ge(zct_done, n + 1)
                        nc.scalar.activation(zc_t[0:C, 512 * n:512 * n + 512], side_bank[1][0:C, :],
                                             ACT.Copy).then_inc(zct_read, 1)
                    if 0 <= i - V_AT < NT // 4:
                        n = i - V_AT
                        act.wait_ge(v1_done, n + 1)
                        nc.scalar.activation(v1[:, 4 * n:4 * n + 4, :],
                                             side_bank[1][:, :].rearrange("p (t d) -> p t d", t=4),
                                             ACT.Copy).then_inc(v1_read, 1)
                act.wait_ge(route, 2)
                nc.scalar.activation(prob[:, :, :], prob[:, :, :], ACT.Exp, scale=1.0 / W_SCALE).then_inc(prob_ready, 1)

            @block.gpsimd
            def _(pool):
                for m in (k_rows[:, :, :, :], q_rows[:, :, :, :], qb_rows[:, :, :, :], v_stage[:, :, :, :]):
                    nc.gpsimd.memset(m, 0.0).then_inc(rows_zero, 1)
                pool.wait_ge(rows_zero, 4)
                nc.gpsimd.memset(zc_t[C:C + 1, :], 1.0).then_inc(zc_ones, 1)
                pool.wait_ge(zc_ones, 1)
                nc.gpsimd.memset(later[:, :, :], 1.0).then_inc(masks_set, 1)
                nc.gpsimd.memset(earlier[:, :, :], 1.0).then_inc(masks_set, 1)
                pool.wait_ge(masks_set, 2)
                nc.gpsimd.affine_select(out=later[:, :, :], in_=later[:, :, :], compare_op=ALU.is_ge, fill=0.0,
                                        base=0, pattern=[[-1, E], [1, E]], channel_multiplier=0).then_inc(masks_set, 1)
                nc.gpsimd.affine_select(out=earlier[:, :, :], in_=earlier[:, :, :], compare_op=ALU.is_gt, fill=0.0,
                                        base=0, pattern=[[1, E], [-1, E]], channel_multiplier=0).then_inc(masks_set, 1)
                for t in range(NT):
                    n = t - W1_AT + 2
                    if 0 <= n < W1_UNITS:
                        pool.wait_ge(ld_w1, 16)
                        rows = slice(4 * n, 4 * n + 4)
                        nc.gpsimd.tensor_tensor(w1_raw[:, rows, 0:D - 1], w1_raw[:, rows, 0:D - 1],
                                                w1_raw[:, rows, D - 1:D].to_broadcast([P, 4, D - 1]),
                                                ALU.subtract).then_inc(w1_shifted, 1)
                    pool.wait_ge(mv1, t + 1)
                    nc.gpsimd.tensor_scalar(var_eps[:, t:t + 1], mv[:, t, 1:2], LN_EPS, None, ALU.add).then_inc(ve1, 1)
                    pool.wait_ge(ve1, t + 1)
                    nc.gpsimd.tensor_tensor(rstd[:, t:t + 1], var_eps[:, t:t + 1], minus_half[:, t:t + 1],
                                            ALU.pow).then_inc(rs1, 1)
                    if t == 7:
                        pool.wait_ge(vec, 1)
                        nc.gpsimd.tensor_tensor(crstd[:, :], cvar[:, :], minus_half[:, :], ALU.pow).then_inc(rsc, 1)

            @block.vector
            def _(dve):
                nc.vector.memset(z1[:, :, D - 1:D], 1.0)
                for i in range(LAST):
                    t = i
                    if t < NT:
                        dve.wait_ge(o_t_done, t + 1)
                        wait(dve, y1_done, t - 1)
                        nc.vector.tensor_copy(o_t[:, t % 2, 4:8, :], o_back[:, :].rearrange("p (c q) -> p c q", c=4))\
                            .then_inc(o_back_read, 1)
                    if i == 0:
                        dve.wait_ge(ld_wg, 16)
                        nc.vector.tensor_scalar(wg_shift[:, :], wg_raw[:, :], wg_raw[:, D - 1:D], None,
                                                ALU.subtract).then_inc(wg_shifted, 1)
                        dve.wait_ge(wg_shifted, 1)
                        nc.vector.memset(wg_shift[:, D - 1:D], 0.0).then_inc(wg_shifted, 1)
                    if i == LAG_PROJECT:
                        dve.wait_ge(wgt_hi_ready, 1)
                        nc.vector.scalar_tensor_tensor(wgt_lo[:, :], z_bank[:, 0:E], W_SCALE, wgt_hi[:, :], ALU.mult,
                                                       ALU.subtract).then_inc(wgt_lo_ready, 1)
                    t = i - LAG_PROJECT
                    if 0 <= t < NT:
                        dve.wait_ge(y1_done, t + 1)
                        nc.vector.tensor_tensor(xres[:, t, :], y_bank[t % 2][:, 0:D], xres[:, t, :],
                                                ALU.add).then_inc(x1_ready, 1)
                        dve.wait_ge(x1_ready, t + 1)
                        nc.vector.bn_stats(stats[:, t, :], xres[:, t, :]).then_inc(st1, 1)
                        dve.wait_ge(st1, t + 1)
                        nc.vector.bn_aggr(mv[:, t, :], stats[:, t, :]).then_inc(mv1, 1)
                    t = i - LAG_Z
                    if 0 <= t < NT:
                        dve.wait_ge(rs1, t + 1)
                        wait(dve, z1t_done, t - 1)
                        nc.vector.tensor_scalar(z1[:, t % 2, 0:D - 1], xres[:, t, 0:D - 1], mv[:, t, 0:1],
                                                rstd[:, t:t + 1], ALU.subtract, ALU.mult).then_inc(z1_ready, 1)
                    t = i - LAG_ZT
                    if 0 <= t < NT:
                        dve.wait_ge(z1_hi_ready, t + 1)
                        nc.vector.tensor_tensor(zt_lo[:, P * t:P * t + P], z_bank[:, 0:P], zt_hi[:, P * t:P * t + P],
                                                ALU.subtract).then_inc(z1_lo_ready, 1)
                    n = i - W1_AT + 1
                    if 0 <= n < W1_UNITS:
                        dve.wait_ge(w1_shifted, n + 1)
                        dve.wait_ge(ld_b1, 16)
                        nc.vector.tensor_copy(w1_raw[:, 4 * n:4 * n + 4, D - 1], b1_cols[:, 4 * n:4 * n + 4])\
                            .then_inc(w1_bias, 1)
                    if 0 <= i - W1_AT < W1_UNITS:
                        n = i - W1_AT
                        dve.wait_ge(w1t_hi_ready, n + 1)
                        nc.vector.scalar_tensor_tensor(w1t_lo[:, 512 * n:512 * n + 512], side_bank[0][:, :], W_SCALE,
                                                       w1t_hi[:, 512 * n:512 * n + 512], ALU.mult,
                                                       ALU.subtract).then_inc(w1t_lo_ready, 1)
                    if i == 1:
                        nc.vector.memset(tb_ext[C:C + 1, :], 1.0).then_inc(rows_ones, 1)
                        nc.vector.memset(zero[:, :], 0.0)
                        nc.vector.memset(one[:, :], 1.0).then_inc(rows_ones, 1)
                        dve.wait_ge(rows_zero, 4)
                        nc.vector.memset(k_rows[C:C + 1, :, :, SHIFT_ROW:SHIFT_ROW + 1], 1.0).then_inc(rows_ones, 1)
                        nc.vector.memset(v_stage[:, :, :, DH1:DH1 + 1], 1.0)
                    if i == 0:
                        heads = ident[:, :].rearrange("p (j r) -> p j r", r=ROWS)
                        nc.vector.tensor_reduce(q_low[:, :], heads[:, :, DH1:2 * DH1], AX.XY, ALU.add,
                                                negate=True)
                        nc.vector.tensor_reduce(k_low[:, :], heads[:, :, 2 * DH1:3 * DH1], AX.XY, ALU.add,
                                                negate=True)
                    if 3 <= i < 7:
                        dve.wait_ge(ld4c, 16)
                        for t in range(4 * i - 12, 4 * i - 8):
                            nc.vector.bn_stats(cstats[:, t, :], ctx_n[:, t, :]).then_inc(stc, 1)
                    if i == 7:
                        dve.wait_ge(stc, NT)
                        for t in range(NT):
                            nc.vector.bn_aggr(cmv[:, t, :], cstats[:, t, :]).then_inc(mvc, 1)
                        dve.wait_ge(mvc, NT)
                        nc.vector.tensor_scalar(cvar[:, :], cmv[:, :, 1], LN_EPS, None, ALU.add).then_inc(vec, 1)
                    if i == 6:
                        dve.wait_ge(rows_filled, 9)
                        nc.vector.tensor_scalar(k_arr[0:C, :, :], k_rows[0:C, :, :, :].rearrange("p g j r -> p g (j r)"),
                                                tg_col[:, 0:1], None, ALU.mult).then_inc(gains_in, 1)
                        nc.vector.tensor_scalar(q_arr[:, :, :], q_rows[:, :, :, :].rearrange("p g j r -> p g (j r)"),
                                                g_col[:, 0:1], None, ALU.mult).then_inc(gains_in, 1)
                        nc.vector.tensor_scalar(v_arr[0:C, :], vw_ext[0:C, :], tg_col[:, 0:1], None,
                                                ALU.mult).then_inc(gains_in, 1)
                    if ZC_AT - 1 <= i < ZC_AT + 3:
                        dve.wait_ge(rsc, 1)
                        for t in range(4 * (i - ZC_AT) + 4, 4 * (i - ZC_AT) + 8):
                            nc.vector.tensor_scalar(ctx_n[:, t, :], ctx_n[:, t, :], cmv[:, t, 0:1], crstd[:, t:t + 1],
                                                    ALU.subtract, ALU.mult).then_inc(zc_ready, 1)
                dve.wait_ge(gates_done, NT)
                logits = g_bank[:, 0:NT * E].rearrange("p (t e) -> p t e", e=E)
                nc.vector.tensor_reduce(logit_max[:, :], logits, AX.X, ALU.max).then_inc(route, 1)
                dve.wait_ge(route, 1)
                nc.vector.tensor_tensor(prob[:, :, :], logits, logit_max[:, :].unsqueeze(2).to_broadcast([P, NT, E]),
                                        ALU.subtract).then_inc(route, 1)
                dve.wait_ge(prob_ready, 1)
                nc.vector.tensor_reduce(esum[:, :], prob[:, :, :], AX.X, ALU.add).then_inc(route, 1)
                dve.wait_ge(route, 3)
                nc.vector.reciprocal(einv[:, :], esum[:, :]).then_inc(route, 1)
                dve.wait_ge(route, 4)
                nc.vector.tensor_tensor(prob[:, :, :], prob[:, :, :],
                                        einv[:, :].unsqueeze(2).to_broadcast([P, NT, E]), ALU.mult).then_inc(route, 1)
                dve.wait_ge(route, 5)
                dve.wait_ge(masks_set, 4)
                other = prob[:, :, :].unsqueeze(2).to_broadcast([P, NT, E, E])
                own = prob[:, :, :].unsqueeze(3).to_broadcast([P, NT, E, E])
                nc.vector.tensor_tensor(over[:, :, :, :], other, own, ALU.is_gt).then_inc(route, 1)
                nc.vector.tensor_tensor(over_eq[:, :, :, :], other, own, ALU.is_ge).then_inc(route, 1)
                dve.wait_ge(route, 7)
                nc.vector.tensor_tensor(over[:, :, :, :], over[:, :, :, :],
                                        later[:, :, :].unsqueeze(1).to_broadcast([P, NT, E, E]), ALU.mult).then_inc(route, 1)
                nc.vector.tensor_tensor(over_eq[:, :, :, :], over_eq[:, :, :, :],
                                        earlier[:, :, :].unsqueeze(1).to_broadcast([P, NT, E, E]), ALU.mult).then_inc(route, 1)
                dve.wait_ge(route, 9)
                nc.vector.tensor_tensor(over[:, :, :, :], over[:, :, :, :], over_eq[:, :, :, :], ALU.add).then_inc(route, 1)
                dve.wait_ge(route, 10)
                nc.vector.tensor_reduce(rank[:, :, :], over[:, :, :, :], AX.X, ALU.add).then_inc(route, 1)
                dve.wait_ge(route, 11)
                nc.vector.scalar_tensor_tensor(prob[:, :, :], rank[:, :, :], 1.5, prob[:, :, :], ALU.is_lt,
                                               ALU.mult).then_inc(route, 1)
                dve.wait_ge(route, 12)
                nc.vector.tensor_reduce(esum[:, :], prob[:, :, :], AX.X, ALU.add).then_inc(route, 1)
                dve.wait_ge(route, 13)
                nc.vector.tensor_scalar(csum[:, :], esum[:, :], 1e-9, None, ALU.add).then_inc(route, 1)
                dve.wait_ge(route, 14)
                nc.vector.reciprocal(einv[:, :], csum[:, :]).then_inc(route, 1)
                dve.wait_ge(route, 15)
                nc.vector.tensor_tensor(csum[:, :], esum[:, :], einv[:, :], ALU.mult).then_inc(route, 1)
                nc.vector.tensor_scalar(einv[:, :], einv[:, :], 1.0 / W_SCALE, None, ALU.mult).then_inc(route, 1)
                dve.wait_ge(route, 17)
                nc.vector.tensor_tensor(gate[:, :, :], prob[:, :, :],
                                        einv[:, :].unsqueeze(2).to_broadcast([P, NT, E]), ALU.mult).then_inc(route, 1)
                dve.wait_ge(ld_f0, 32)
                for t in range(NT):
                    last = nc.vector.scalar_tensor_tensor(xres[:, t, :], fbo_bc[:, :], csum[:, t:t + 1], xres[:, t, :],
                                                          ALU.mult, ALU.add)
                    last.then_inc(route, 1)

        scratch.close()

        scratch = ExitStack()
        sig = sb1("sig", [P, 2, HF])
        glu = sb1("glu", [P, 4, HF])
        mix = sb1("mix", [P, 2, HF])
        mix_t = sb1("mix_t", [P, 2, HF // P, P])
        k_half = sb1("k_half", [P, 2, 2, S], F16)
        k_mix = sb1("k_mix", [P, 2, 2, S], F16)
        k_zeros = arena_o[:, :].rearrange("p (j g n) -> p j g n", j=4, g=GT)
        k_mask = arena_o[:, :].bitcast(F16).rearrange("p (j g n) -> p j g n", j=4, g=GT)
        k_done, k_half_ready, k_mixed, k_zeroed = (sem(n) for n in ("k_done", "k_half_ready", "k_mixed", "k_zeroed"))
        k_placed = [sem("k_placed_even"), sem("k_placed_odd")]
        AT_ZERO = 0
        AT_KEYS = 1
        h_bank, mt_bank, k_bank, y2_bank = banks[0:4], banks[4], banks[5], banks[6:8]
        h_done, sig_ready, glu_ready, mixed, mix_t_done, mix_t_read, y2_done, x2_ready, mv2 = (
            sem(n) for n in ("h_done", "sig_ready", "glu_ready", "mixed", "mix_t_done", "mix_t_read", "y2_done",
                             "x2_ready", "mv2"))
        MIXES = E - 1
        AT_TRANSPOSE, AT_COPY, AT_PROJECT = 3, 4, 6

        def work_out(eng, values, places):
            for v in values:
                eng.compute_val(v)
            for ap in places:
                eng.lower_ap(ap)

        def tiles_of(eng, tile):
            tile(0, 0)
            tile(0, 1)
            with eng.Fori(0, NT // 2 - 1) as k:
                tile(k, 2)
                tile(k, 3)
            tile(NT // 2, 0)

        with nc.Block() as block:
            @block.tensor
            def _(pe):
                def tile(k, r):
                    final = isinstance(k, int) and 2 * k + r == NT
                    before = not (isinstance(k, int) and 2 * k + r == 0)
                    for e in range(E):
                        if not final:
                            tokens = bass.ds((k * 2 + r) * P, P)
                            bank = h_bank[e % 4]
                            wait(pe, glu_ready, k * (2 * E) + (r * E + e - 3))
                            w = slice(2 * HF * e, 2 * HF * e + 2 * HF)
                            nc.tensor.matmul(bank[:, :], zt_hi[:, tokens], w1t_hi[:, w], start=True, stop=False)
                            nc.tensor.matmul(bank[:, :], zt_lo[:, tokens], w1t_hi[:, w], start=False, stop=False)
                            nc.tensor.matmul(bank[:, :], zt_hi[:, tokens], w1t_lo[:, w], start=False,
                                             stop=True).then_inc(h_done, 1)
                        if not final and e == AT_KEYS:
                            wait(pe, k_mixed, k * 2 + r)
                            for g in range(2):
                                last = nc.tensor.matmul(k_bank[:, S * g:S * g + S], k_arr[:, 2 * (r % 2) + g, :],
                                                        zc_t[:, bass.ds((k + r // 2) * S, S)], start=True, stop=True)
                            last.then_inc(k_done, 1)
                        if before and e == AT_TRANSPOSE:
                            pe.wait_ge(mixed, k * (2 * MIXES) + r * MIXES)
                            wait(pe, mix_t_read, k * 2 + (r - 1))
                            for c in range(HF // P):
                                last = nc.tensor.transpose(mt_bank[:, P * c:P * c + P],
                                                           mix[:, (r - 1) % 2, P * c:P * c + P], ident[:, :])
                            last.then_inc(mix_t_done, 1)
                        if before and e == AT_PROJECT:
                            pe.wait_ge(mix_t_read, k * 2 + r)
                            wait(pe, x2_ready, k * 2 + (r - 2))
                            for c in range(HF // P):
                                last = nc.tensor.matmul(y2_bank[(r - 1) % 2][:, 0:D], mix_t[:, (r - 1) % 2, c, :],
                                                        fwo_t[:, c, :], start=(c == 0), stop=(c == HF // P - 1))
                            last.then_inc(y2_done, 1)
                tiles_of(pe, tile)

            @block.scalar
            def _(act):
                def tile(k, r):
                    final = isinstance(k, int) and 2 * k + r == NT
                    before = not (isinstance(k, int) and 2 * k + r == 0)
                    for e in range(E):
                        if not final:
                            act.wait_ge(h_done, k * (2 * E) + (r * E + e + 1))
                            wait(act, glu_ready, k * (2 * E) + (r * E + e - 1))
                            nc.scalar.activation(sig[:, e % 2, :], h_bank[e % 4][:, HF:2 * HF], ACT.Sigmoid,
                                                 scale=1.0 / W_SCALE).then_inc(sig_ready, 1)
                        if not final and e == AT_KEYS:
                            act.wait_ge(k_done, k * 2 + (r + 1))
                            wait(act, k_mixed, k * 2 + (r - 1))
                            nc.scalar.activation(k_half[:, r % 2, :, :], k_bank[:, :].rearrange("p (g n) -> p g n", g=2),
                                                 ACT.Copy).then_inc(k_half_ready, 1)
                        if not final and e == AT_ZERO:
                            g = 2 * (r % 2)
                            nc.scalar.activation(k_zeros[:, :, g:g + 2, bass.ds((k + r // 2) * (S // 2), S // 2)],
                                                 zero[:, 0:1].unsqueeze(2).unsqueeze(3).to_broadcast([P, 4, 2, S // 2]),
                                                 ACT.Copy).then_inc(k_zeroed, 1)
                        if before and e == AT_COPY:
                            act.wait_ge(mix_t_done, k * 2 + r)
                            nc.scalar.activation(mix_t[:, (r - 1) % 2, :, :],
                                                 mt_bank[:, 0:HF].rearrange("p (c q) -> p c q", q=P),
                                                 ACT.Copy).then_inc(mix_t_read, 1)
                tiles_of(act, tile)

            @block.vector
            def _(dve):
                def tile(k, r):
                    final = isinstance(k, int) and 2 * k + r == NT
                    before = not (isinstance(k, int) and 2 * k + r == 0)
                    for e in range(E):
                        if not final:
                            dve.wait_ge(sig_ready, k * (2 * E) + (r * E + e + 1))
                            if e >= 4:
                                dve.wait_ge(mixed, k * (2 * MIXES) + (r * MIXES + max(e - 4, 1)))
                            elif before:
                                dve.wait_ge(mixed, k * (2 * MIXES) + ((r - 1) * MIXES + e + 4))
                            nc.vector.scalar_tensor_tensor(glu[:, e % 4, :], sig[:, e % 2, :],
                                                           gate[:, bass.ds(k * 2 + r, 1), e:e + 1].rearrange("p a b -> p (a b)"),
                                                           h_bank[e % 4][:, 0:HF], ALU.mult,
                                                           ALU.mult).then_inc(glu_ready, 1)
                        if not final and e == AT_KEYS:
                            dve.wait_ge(k_half_ready, k * 2 + (r + 1))
                            wait(dve, k_placed[r % 2], k * 64 + r // 2 * 64)
                            nc.vector.scalar_tensor_tensor(k_mix[:, r % 2, :, :], k_half[:, r % 2, :, :], k_low[:, 0:1],
                                                           k_bank[:, :].rearrange("p (g n) -> p g n", g=2), ALU.mult,
                                                           ALU.add).then_inc(k_mixed, 1)
                    if before:
                        prev = bass.ds(k * 2 + (r - 1), 1)
                        dve.wait_ge(y2_done, k * 2 + r)
                        nc.vector.tensor_tensor(xres[:, prev, :], y2_bank[(r - 1) % 2][:, 0:D].unsqueeze(1),
                                                xres[:, prev, :], ALU.add).then_inc(x2_ready, 1)
                        dve.wait_ge(x2_ready, k * 2 + r)
                        nc.vector.bn_stats(stats[:, prev, :], xres[:, prev, :])
                tiles_of(dve, tile)

            @block.gpsimd
            def _(pool):
                def tile(k, r):
                    if isinstance(k, int) and 2 * k + r == NT:
                        return
                    for e in range(1, E):
                        pool.wait_ge(glu_ready, k * (2 * E) + (r * E + e + 1))
                        if e == 1:
                            if not isinstance(k, int) or 2 * k + r >= 2:
                                wait(pool, mix_t_done, k * 2 + (r - 1))
                        else:
                            pool.wait_ge(mixed, k * (2 * MIXES) + (r * MIXES + e - 1))
                        nc.gpsimd.tensor_tensor(mix[:, r % 2, :], glu[:, 0, :] if e == 1 else mix[:, r % 2, :],
                                                glu[:, e % 4, :], ALU.add).then_inc(mixed, 1)
                tiles_of(pool, tile)

            @block.sync
            def _(sp):
                def tile(k, r):
                    if isinstance(k, int) and 2 * k + r == NT:
                        return
                    g = 2 * (r % 2)
                    places = [k_mask[ROWS * j:ROWS * j + ROWS, j, g:g + 2, bass.ds((k + r // 2) * S, S)] for j in range(4)]
                    if not isinstance(k, int):
                        work_out(sp, (k * 2 + (r + 1),), places)
                    sp.wait_ge(k_zeroed, k * 2 + (r + 1))
                    sp.wait_ge(k_mixed, k * 2 + (r + 1))
                    for j, place in enumerate(places):
                        sp.dma_start(place, k_mix[ROWS * j:ROWS * j + ROWS, r % 2, :, :]).then_inc(k_placed[r % 2], 16)
                tiles_of(sp, tile)
                for placed in k_placed:
                    sp.wait_ge(placed, 64 * NT // 2)
        scratch.close()

        scratch = ExitStack()
        q_mix = arena_v[:, 0:GT * N].rearrange("p (g n) -> p g n", g=GT)
        z2 = ctx_halves[:, :].bitcast(F32).rearrange("p (t d) -> p t d", t=NT)
        z2_t = zt_halves[:, :].bitcast(F32)
        q_half = sb1("q_half", [P, 2, 512], F16)
        q_whole = sb1("q_whole", [P, 2, 512])
        rsx, vex, z2_ready, z2t_done, z2t_read, q_done, q_half_ready, q_mixed = (
            sem(n) for n in ("rsx", "vex", "z2_ready", "z2t_done", "z2t_read", "q_done", "q_half_ready",
                             "q_mixed"))
        CHUNKS = N // 512

        with nc.Block() as block:
            @block.gpsimd
            def _(pool):
                for c in range(CHUNKS):
                    t = slice(4 * c, 4 * c + 4)
                    pool.wait_ge(vex, 1)
                    nc.gpsimd.tensor_tensor(rstd[:, t], var_eps[:, t], minus_half[:, t], ALU.pow).then_inc(rsx, 1)

            @block.vector
            def _(dve):
                for t in range(NT):
                    nc.vector.bn_aggr(mv[:, t, :], stats[:, t, :]).then_inc(mv2, 1)
                dve.wait_ge(mv2, NT)
                nc.vector.tensor_scalar(var_eps[:, :], mv[:, :, 1], LN_EPS, None, ALU.add).then_inc(vex, 1)
                for c in range(CHUNKS):
                    dve.wait_ge(rsx, c + 1)
                    for t in range(4 * c, 4 * c + 4):
                        nc.vector.tensor_scalar(z2[:, t, :], xres[:, t, :], mv[:, t, 0:1], rstd[:, t:t + 1],
                                                ALU.subtract, ALU.mult).then_inc(z2_ready, 1)
                    dve.wait_ge(z2t_done, c + 1)
                    nc.vector.tensor_copy(z2_t[:, 512 * c:512 * c + 512], banks[4 + c][:, :]).then_inc(z2t_read, 1)

                def queries(c):
                    for g in range(GT):
                        dve.wait_ge(q_half_ready, c * GT + (g + 1))
                        nc.vector.scalar_tensor_tensor(q_mix[:, g, bass.ds(c * 512, 512)], q_half[:, g % 2, :],
                                                       q_low[:, 0:1], q_whole[:, g % 2, :], ALU.mult,
                                                       ALU.add).then_inc(q_mixed, 1)
                with dve.Fori(0, CHUNKS) as c:
                    queries(c)

            @block.scalar
            def _(act):
                def queries(c):
                    for g in range(GT):
                        act.wait_ge(q_done, c * GT + (g + 1))
                        wait(act, q_mixed, c * GT + (g - 1))
                        nc.scalar.activation(q_whole[:, g % 2, :], banks[g % 4][:, :], ACT.Identity,
                                             bias=q_bias[:, g:g + 1])
                        nc.scalar.activation(q_half[:, g % 2, :], banks[g % 4][:, :], ACT.Identity,
                                             bias=q_bias[:, g:g + 1]).then_inc(q_half_ready, 1)
                queries(0)
                with act.Fori(1, CHUNKS) as c:
                    queries(c)

            @block.tensor
            def _(pe):
                for c in range(CHUNKS):
                    pe.wait_ge(z2_ready, 4 * c + 4)
                    for j in range(4):
                        last = nc.tensor.transpose(banks[4 + c][:, P * j:P * j + P], z2[:, 4 * c + j, :], ident[:, :])
                    last.then_inc(z2t_done, 1)

                def queries(c):
                    pe.wait_ge(z2t_read, c + 1)
                    for g in range(GT):
                        wait(pe, q_half_ready, c * GT + (g - 3))
                        nc.tensor.matmul(banks[g % 4][:, :], q_arr[:, g, :], z2_t[:, bass.ds(c * 512, 512)],
                                         start=True, stop=True).then_inc(q_done, 1)
                queries(0)
                with pe.Fori(1, CHUNKS) as c:
                    queries(c)
        scratch.close()

        scratch = ExitStack()
        w6 = sem("w6")
        RING1 = 4
        at = GT * N // 2
        p1 = temp_v(RING1 * QT * S).rearrange("p (r n) -> p r n", r=RING1)
        neg_max1 = sb1("neg_max1", [P, 2, 4 * QT])
        neg_max1_t = sb1("neg_max1_t", [4 * QT, 2, P], F16)
        y_sb = temp_v(2 * S).rearrange("p (r n) -> p r n", r=2)
        y_inv = sb1("y_inv", [P, 2, QT, 4])
        y_norm = sb1("y_norm", [P, 2, QT, 4, DH1])
        score_bank, max_bank, y_bank, shift_bank, yt_bank = banks[0:2], banks[2:4], banks[4:6], banks[6], banks[7]
        LEAD_MAX, LEAD_SHIFT, LAG_PV, LAG_Y, LAG_YT, LAG_FINISH = 10, 6, 3, 7, 9, 10
        SCALE1 = float(DH1) ** -0.5
        max1_done, max1_read, shift1_done, shift1_read, scores1_done, p1_ready, staged, pv1_done = (
            sem(n) for n in ("max1_done", "max1_read", "shift1_done", "shift1_read", "scores1_done", "p1_ready",
                             "staged", "pv1_done"))
        y1_read, y1t_done, y1_inverted, y1t_read, x3_ready = (
            sem(n) for n in ("y1_read", "y1t_done", "y1_inverted", "y1t_read", "x3_ready"))
        shift1_row = [sem("shift1_row_even"), sem("shift1_row_odd")]

        PEELED = 14

        def steps1(eng, step):
            for s in range(-LEAD_MAX, PEELED):
                step(0, s)
            with eng.Fori(0, B - 2) as b:
                for s in range(PEELED, PEELED + H1):
                    step(b, s)
            for s in range(PEELED, 2 * H1 + LAG_FINISH + 2):
                step(B - 2, s)

        def group(b, s):
            return b * GT + s // 4

        with nc.Block() as block:
            @block.tensor
            def _(pe):
                def maxima(b, s):
                    g, j = (s // 4) % GT, s % 4
                    wait(pe, max1_read, count(b, s) - 1)
                    for q in range(QT):
                        last = nc.tensor.matmul(max_bank[s % 2][:, S * q:S * q + S],
                                                q_mix[:, g, bass.ds((b + s // H1) * S + P * q, P)],
                                                k_mask[:, j, g, bass.ds((b + s // H1) * S, S)], start=True, stop=True)
                    last.then_inc(max1_done, 1)

                def shift(b, s):
                    pe.wait_ge(max1_read, count(b, s) + 4)
                    wait(pe, shift1_read, group(b, s))
                    nc.tensor.transpose(shift_bank[0:4 * QT, 0:P], neg_max1[:, (s // 4) % 2, :],
                                        ident[:, :]).then_inc(shift1_done, 1)

                def scores(b, s):
                    g, j = (s // 4) % GT, s % 4
                    if j == 0:
                        pe.wait_ge(shift1_row[(s // 4) % 2], b * 32 + 16 * (s // 8 + 1))
                    wait(pe, p1_ready, count(b, s) - 1)
                    for k in range(QT):
                        last = nc.tensor.matmul(score_bank[s % 2][:, S * k:S * k + S],
                                                k_mask[:, j, g, bass.ds((b + s // H1) * S + P * k, P)],
                                                q_mix[:, g, bass.ds((b + s // H1) * S, S)], start=True, stop=True)
                    last.then_inc(scores1_done, 1)

                def values(b, s):
                    g, j = s // 4, s % 4
                    if j == 0:
                        wait(pe, y1_read, group(b, s) - 1)
                        pe.wait_ge(staged, b * GT + (g + 1))
                    if not there(b, s + LAG_PV):
                        pe.wait_ge(p1_ready, count(b, s) + 1)
                    for k in range(QT):
                        last = nc.tensor.matmul(y_bank[g % 2][ROWS * j:ROWS * j + ROWS, 0:S], v_stage[:, k, s % H1, :],
                                                p1[:, s % RING1, S * k:S * k + S], start=(k == 0), stop=(k == QT - 1))
                    last.then_inc(pv1_done, 1)

                def back(b, s):
                    g = s // 4
                    pe.wait_ge(y1_read, b * GT + (g + 1))
                    wait(pe, y1t_read, group(b, s))
                    for q in range(QT):
                        last = nc.tensor.transpose(yt_bank[:, P * q:P * q + P], y_sb[:, g % 2, P * q:P * q + P],
                                                   ident[:, :])
                    last.then_inc(y1t_done, 1)

                def max_query(b, s, q):
                    return q_mix[:, (s // 4) % GT, bass.ds((b + s // H1) * S + P * q, P)]

                def max_keys(b, s):
                    return k_mask[:, s % 4, (s // 4) % GT, bass.ds((b + s // H1) * S, S)]

                def score_keys(b, s, k):
                    return k_mask[:, s % 4, (s // 4) % GT, bass.ds((b + s // H1) * S + P * k, P)]

                def score_queries(b, s):
                    return q_mix[:, (s // 4) % GT, bass.ds((b + s // H1) * S, S)]

                def step(b, s):
                    if not isinstance(b, int):
                        work_out(pe, (count(b, s) - 1, count(b, s + LEAD_MAX) - 1),
                                 (max_query(b, s + LEAD_MAX, 0), max_query(b, s + LEAD_MAX, 1), max_keys(b, s + LEAD_MAX),
                                  score_keys(b, s, 0), score_keys(b, s, 1), score_queries(b, s)))
                    if there(b, s):
                        scores(b, s)
                    if there(b, s + LEAD_MAX):
                        maxima(b, s + LEAD_MAX)
                    if (s + LEAD_SHIFT) % 4 == 0 and there(b, s + LEAD_SHIFT):
                        shift(b, s + LEAD_SHIFT)
                    if there(b, s - LAG_PV):
                        values(b, s - LAG_PV)
                    if (s - LAG_YT) % 4 == 0 and there(b, s - LAG_YT):
                        back(b, s - LAG_YT)
                steps1(pe, step)

            @block.scalar
            def _(act):
                def step(b, s):
                    if there(b, s):
                        act.wait_ge(scores1_done, count(b, s) + 1)
                        wait(act, pv1_done, count(b, s) + 1 - RING1)
                        nc.scalar.activation(p1[:, s % RING1, :], score_bank[s % 2][:, :], ACT.Exp,
                                             scale=SCALE1).then_inc(p1_ready, 1)
                    u = s - LAG_Y
                    if u % 4 == 0 and there(b, u):
                        act.wait_ge(pv1_done, count(b, u) + 4)
                        wait(act, y1t_done, group(b, u) - 1)
                        nc.scalar.activation(y_sb[:, (u // 4) % 2, :], y_bank[(u // 4) % 2][:, 0:S],
                                             ACT.Copy).then_inc(y1_read, 1)
                steps1(act, step)

            @block.vector
            def _(dve):
                def weight_scales():
                    nc.vector.memset(ones[:, :], 1.0).then_inc(w6, 1)
                    dve.wait_ge(ldw6, 112)
                    for side in range(2):
                        for i in range(FT):
                            p = height[i]
                            nc.vector.tensor_reduce(gu_max[0:p, side, i:i + 1], gu_raw[0:p, side, i, :], AX.X, ALU.max,
                                                    apply_absolute_value=True).then_inc(w6, 1)
                    nc.vector.tensor_reduce(wd_max[:, :], wd_raw[:, :], AX.X, ALU.max, apply_absolute_value=True).then_inc(w6, 1)
                    dve.wait_ge(w6, 8)
                    for i in range(FT):
                        p = height[i]
                        nc.vector.tensor_scalar(gu_scale[0:p, :, i], gu_max[0:p, :, i], 1.0 / QMAX, None, ALU.mult).then_inc(w6, 1)
                    nc.vector.tensor_scalar(wd_scale[:, :], wd_max[:, :], 1.0 / QMAX, None, ALU.mult).then_inc(w6, 1)
                    dve.wait_ge(w6, 12)
                    for i in range(FT):
                        p = height[i]
                        nc.vector.reciprocal(gu_inv[0:p, :, i], gu_scale[0:p, :, i]).then_inc(w6, 1)
                    nc.vector.reciprocal(wd_inv[:, :], wd_scale[:, :]).then_inc(w6, 1)
                    nc.vector.tensor_scalar(wd_diag[:, :], ident[:, :], wd_scale[:, 0:1], None, ALU.mult).then_inc(w6, 1)

                def max_of(b, s):
                    g, j = (s // 4) % 2, s % 4
                    dve.wait_ge(max1_done, count(b, s) + 1)
                    if j == 0:
                        wait(dve, shift1_done, group(b, s) - 1)
                    nc.vector.tensor_reduce(neg_max1[:, g, QT * j:QT * j + QT],
                                            max_bank[s % 2][:, :].rearrange("p (q k) -> p q k", q=QT),
                                            AX.X, ALU.max, negate=True).then_inc(max1_read, 1)

                def shift_out(b, s):
                    g = (s // 4) % 2
                    dve.wait_ge(shift1_done, b * GT + (s // 4 + 1))
                    wait(dve, shift1_row[g], b * 32 + 16 * (s // 8))
                    nc.vector.tensor_copy(neg_max1_t[:, g, :], shift_bank[0:4 * QT, 0:P]).then_inc(shift1_read, 1)

                def finish(b, s):
                    g = (s // 4) % 2
                    y = yt_bank[:, 0:QT * P].rearrange("p (q j r) -> p q j r", q=QT, j=4)
                    dve.wait_ge(y1t_done, b * GT + (s // 4 + 1))
                    nc.vector.reciprocal(y_inv[:, g, :, :], y[:, :, :, DH1]).then_inc(y1_inverted, 1)
                    dve.wait_ge(y1_inverted, b * GT + (s // 4 + 1))
                    wait(dve, x3_ready, group(b, s) - 1)
                    nc.vector.tensor_tensor(y_norm[:, g, :, :, :], y[:, :, :, 0:DH1],
                                            y_inv[:, g, :, :].unsqueeze(3).to_broadcast([P, QT, 4, DH1]),
                                            ALU.mult).then_inc(y1t_read, 1)

                def step(b, s):
                    if there(b, s + LEAD_MAX):
                        max_of(b, s + LEAD_MAX)
                    if isinstance(b, int) and count(b, s) == -1:
                        weight_scales()
                    u = s + LEAD_SHIFT - 1
                    if u % 4 == 0 and there(b, u):
                        shift_out(b, u)
                    u = s - LAG_FINISH
                    if u % 4 == 0 and there(b, u):
                        finish(b, u)
                    u = s - LAG_FINISH - 1
                    if u % H1 == H1 - 4 and there(b, u):
                        dve.wait_ge(x3_ready, b * GT + (u // 4 + 1))
                        for q in range(QT):
                            t = bass.ds((b + u // H1) * QT + q, 1)
                            nc.vector.bn_stats(stats[:, t, :], xres[:, t, :])
                steps1(dve, step)

            @block.gpsimd
            def _(pool):
                def on_grid(n):
                    def put(dst, inv):
                        if n == 0:
                            return nc.gpsimd.tensor_scalar(dst, dst, inv, MAGIC, ALU.mult, ALU.add)
                        if n == 1:
                            return nc.gpsimd.tensor_scalar(dst, dst, MAGIC + QMAX, MAGIC - QMAX - 1.0, ALU.min, ALU.max)
                        return nc.gpsimd.tensor_scalar(dst, dst, MAGIC, None, ALU.subtract)
                    pool.wait_ge(w6, 17 + 7 * n)
                    for side in range(2):
                        for i in range(FT):
                            p = height[i]
                            put(gu_raw[0:p, side, i, :], gu_inv[0:p, side, i:i + 1]).then_inc(w6, 1)
                    put(wd_raw[:, :], wd_inv[:, 0:1]).then_inc(w6, 1)

                def step(b, s):
                    u = s + LEAD_SHIFT
                    if u % 4 == 0 and there(b, u):
                        h = u % H1
                        wait(pool, pv1_done, count(b, u) + 4 - H1)
                        nc.gpsimd.tensor_copy(v_stage[:, :, h:h + 4, 0:DH1],
                                              v1[:, bass.ds((b + u // H1) * QT, QT), DH1 * h:DH1 * h + 4 * DH1]
                                              .rearrange("p t (h d) -> p t h d", h=4)).then_inc(staged, 1)
                    if isinstance(b, int) and count(b, s) in (0, 4, 8):
                        on_grid(s // 4)
                    u = s - LAG_FINISH
                    if u % 4 == 0 and there(b, u):
                        h = u % H1
                        pool.wait_ge(y1t_read, b * GT + (u // 4 + 1))
                        rows = xres[:, bass.ds((b + u // H1) * QT, QT), DH1 * h:DH1 * h + 4 * DH1]
                        nc.gpsimd.tensor_tensor(rows, rows, y_norm[:, (u // 4) % 2, :, :, :]
                                                .rearrange("p q j d -> p q (j d)"), ALU.add).then_inc(x3_ready, 1)
                steps1(pool, step)

            @block.sync
            def _(sp):
                def step(b, s):
                    u = s + LEAD_SHIFT
                    if u % 4 == 0 and there(b, u):
                        g = (u // 4) % 2
                        sp.wait_ge(shift1_read, b * GT + (u // 4 + 1))
                        sp.dma_start(q_mix[SHIFT_ROW:P:ROWS, (u // 4) % GT, bass.ds((b + u // H1) * S, S)],
                                     neg_max1_t[:, g, :]).then_inc(shift1_row[g], 16)
                steps1(sp, step)
        scratch.close()
        layer1.close()

        scratch = ExitStack()
        CH = N // 512
        at = 0
        z3 = temp_v(N).rearrange("p (t d) -> p t d", t=NT)
        grid = temp_v(N)
        gated = temp_v(512 * 2).rearrange("p (r n) -> p r n", r=2)
        hidden = arena_o[:, 0:FT * N].rearrange("p (i n) -> p i n", i=FT)
        hidden_q = arena_o[:, FT * N:FT * N + FT * N // 2].bitcast(BF16).rearrange("p (i n) -> p i n", i=FT)
        gu_t = sb1("gu_t", [D, 2, FT * P], BF16)
        wd_t = sb1("wd_t", [P, FT, D], BF16)
        x_q = zt_halves[:, 0:N].bitcast(BF16)
        wd_row = sb1("wd_row", [P, D])
        clips = sb1("clips", [P, 2])
        clip_sig = sb1("clip_sig", [P, 2])
        x_max = sb1("x_max", [P, 1])
        x_all = sb1("x_all", [P, 1])
        x_scale = sb1("x_scale", [P, 1])
        x_inv = sb1("x_inv", [P, 1])
        gu_cols = sb1("gu_cols", [P, 2, FT])
        h_max = sb1("h_max", [P, FT * CH])
        h_top = sb1("h_top", [P, 1])
        h_all = sb1("h_all", [P, 1])
        h_scale = sb1("h_scale", [P, 1])
        h_inv = sb1("h_inv", [P, 1])
        y_part = sb1("y_part", [P, 2, 4, D])
        h_cleared, ld6, mv3, ve3, rs3, wt_done, wt_read, z3_ready, clip_ready, x_chain = (
            sem(n) for n in ("h_cleared", "ld6", "mv3", "ve3", "rs3", "wt_done", "wt_read", "z3_ready", "clip_ready",
                             "x_chain"))
        x_reduced, z3t_done, grid_ready, xq_ready, gu_done, gated_ready, hidden_ready, h_maxed, h_reduced = (
            sem(n) for n in ("x_reduced", "z3t_done", "grid_ready", "xq_ready", "gu_done", "gated_ready",
                             "hidden_ready", "h_maxed", "h_reduced"))
        h_grid, hq_ready, y3_done, y3_read, out_ready, stored, h_chain = (
            sem(n) for n in ("h_grid", "hq_ready", "y3_done", "y3_read", "out_ready", "stored", "h_chain"))
        UNITS_H = FT * CH

        with nc.Block() as block:
            @block.sync
            def _(sp):
                sp.dma_start(clips[:, 0:1], f1_cx.partition_broadcast(P)).then_inc(ld6, 16)
                sp.dma_start(clips[:, 1:2], f1_cd.partition_broadcast(P)).then_inc(ld6, 16)
                for c in range(CH):
                    sp.wait_ge(out_ready, c + 1)
                    sp.dma_start(out[:, 4 * c:4 * c + 4, :], xres[:, 4 * c:4 * c + 4, :]).then_inc(stored, 16)
                sp.wait_ge(stored, 16 * CH)

            @block.gpsimd
            def _(pool):
                pool.wait_ge(ve3, 1)
                nc.gpsimd.tensor_tensor(rstd[:, :], var_eps[:, :], minus_half[:, :], ALU.pow).then_inc(rs3, 1)
                pool.wait_ge(x_chain, 1)
                nc.gpsimd.partition_all_reduce(x_all[:, :], x_max[:, :], P, bass.bass_isa.ReduceOp.max).then_inc(x_reduced, 1)
                pool.wait_ge(h_chain, 1)
                nc.gpsimd.partition_all_reduce(h_all[:, :], h_top[:, :], P, bass.bass_isa.ReduceOp.max).then_inc(h_reduced, 1)

            @block.scalar
            def _(act):
                act.wait_ge(ld6, 32)
                nc.scalar.activation(clip_sig[:, :], clips[:, :], ACT.Sigmoid).then_inc(clip_ready, 1)
                for n in range(CH):
                    act.wait_ge(grid_ready, 2 * n + 2)
                    nc.scalar.activation(x_q[:, 512 * n:512 * n + 512], grid[:, 512 * n:512 * n + 512], ACT.Copy,
                                         bias=-MAGIC).then_inc(xq_ready, 1)
                act.wait_ge(x_chain, 5)
                for n in range(UNITS_H):
                    i = n // CH
                    p = height[i]
                    act.wait_ge(gu_done, n + 1)
                    wait(act, hidden_ready, n - 1)
                    nc.scalar.activation(gated[0:p, n % 2, :], banks[4 + 2 * (n % 2)][0:p, :], ACT.Silu,
                                         scale=gu_cols[0:p, 0, i:i + 1]).then_inc(gated_ready, 1)
                for n in range(UNITS_H):
                    i, w = n // CH, slice(512 * (n % CH), 512 * (n % CH) + 512)
                    p = height[i]
                    act.wait_ge(h_grid, 2 * n + 2)
                    nc.scalar.activation(hidden_q[0:p, i, w], hidden[0:p, i, w], ACT.Copy, bias=-MAGIC).then_inc(hq_ready, 1)

            @block.vector
            def _(dve):
                for t in range(NT):
                    nc.vector.bn_aggr(mv[:, t, :], stats[:, t, :]).then_inc(mv3, 1)
                nc.vector.memset(h_max[:, :], 0.0).then_inc(h_cleared, 1)
                dve.wait_ge(mv3, NT)
                nc.vector.tensor_scalar(var_eps[:, :], mv[:, :, 1], LN_EPS, None, ALU.add).then_inc(ve3, 1)
                for side in range(2):
                    dve.wait_ge(wt_done, side + 1)
                    nc.vector.tensor_copy(gu_t[:, side, 0:FF], banks[side][:, 0:FF]).then_inc(wt_read, 1)
                dve.wait_ge(wt_done, 3)
                for i in range(FT):
                    p = height[i]
                    nc.vector.tensor_copy(wd_t[0:p, i, :], banks[2][0:p, D * i:D * i + D]).then_inc(wt_read, 1)
                dve.wait_ge(rs3, 1)
                for t in range(NT):
                    nc.vector.tensor_scalar(z3[:, t, :], xres[:, t, :], mv[:, t, 0:1], rstd[:, t:t + 1],
                                            ALU.subtract, ALU.mult).then_inc(z3_ready, 1)
                dve.wait_ge(z3_ready, NT)
                nc.vector.tensor_reduce(x_max[:, :], z3[:, :, :], AX.XY, ALU.max, apply_absolute_value=True).then_inc(x_chain, 1)
                dve.wait_ge(x_reduced, 1)
                dve.wait_ge(clip_ready, 1)
                nc.vector.tensor_scalar(x_scale[:, :], x_all[:, :], clip_sig[:, 0:1], 1.0 / QMAX, ALU.mult, ALU.mult)\
                    .then_inc(x_chain, 1)
                dve.wait_ge(x_chain, 2)
                nc.vector.reciprocal(x_inv[:, :], x_scale[:, :]).then_inc(x_chain, 1)
                nc.vector.tensor_scalar(gu_cols[:, :, 0:FT - 1], gu_scale[:, :, 0:FT - 1], x_scale[:, 0:1], None,
                                        ALU.mult).then_inc(x_chain, 1)
                p = height[FT - 1]
                nc.vector.tensor_scalar(gu_cols[0:p, :, FT - 1], gu_scale[0:p, :, FT - 1], x_scale[0:p, 0:1], None,
                                        ALU.mult).then_inc(x_chain, 1)
                dve.wait_ge(x_chain, 5)
                for n in range(CH):
                    dve.wait_ge(z3t_done, n + 1)
                    w = grid[:, 512 * n:512 * n + 512]
                    nc.vector.tensor_scalar(w, banks[4 + n][:, :], x_inv[:, 0:1], MAGIC, ALU.mult, ALU.add).then_inc(grid_ready, 1)
                    dve.wait_ge(grid_ready, 2 * n + 1)
                    nc.vector.tensor_scalar(w, w, MAGIC + QMAX, MAGIC - QMAX - 1.0, ALU.min, ALU.max).then_inc(grid_ready, 1)
                dve.wait_ge(h_cleared, 1)
                for n in range(UNITS_H):
                    i, w = n // CH, slice(512 * (n % CH), 512 * (n % CH) + 512)
                    p = height[i]
                    dve.wait_ge(gated_ready, n + 1)
                    nc.vector.scalar_tensor_tensor(hidden[0:p, i, w], banks[5 + 2 * (n % 2)][0:p, :],
                                                   gu_cols[0:p, 1, i:i + 1], gated[0:p, n % 2, :], ALU.mult,
                                                   ALU.mult).then_inc(hidden_ready, 1)
                    dve.wait_ge(hidden_ready, n + 1)
                    nc.vector.tensor_reduce(h_max[0:p, n:n + 1], hidden[0:p, i, w], AX.X, ALU.max,
                                            apply_absolute_value=True).then_inc(h_maxed, 1)
                dve.wait_ge(h_maxed, UNITS_H)
                nc.vector.tensor_reduce(h_top[:, :], h_max[:, :], AX.X, ALU.max).then_inc(h_chain, 1)
                dve.wait_ge(h_reduced, 1)
                nc.vector.tensor_scalar(h_scale[:, :], h_all[:, :], clip_sig[:, 1:2], 1.0 / QMAX, ALU.mult, ALU.mult)\
                    .then_inc(h_chain, 1)
                dve.wait_ge(h_chain, 2)
                nc.vector.reciprocal(h_inv[:, :], h_scale[:, :]).then_inc(h_chain, 1)
                dve.wait_ge(wt_done, 4)
                nc.vector.tensor_scalar(wd_row[:, :], banks[3][:, 0:D], h_scale[:, 0:1], None, ALU.mult).then_inc(h_chain, 1)
                dve.wait_ge(h_chain, 4)
                for n in range(UNITS_H):
                    i, w = n // CH, slice(512 * (n % CH), 512 * (n % CH) + 512)
                    h = hidden[0:height[i], i, w]
                    nc.vector.tensor_scalar(h, h, h_inv[0:height[i], 0:1], MAGIC, ALU.mult, ALU.add).then_inc(h_grid, 1)
                    dve.wait_ge(h_grid, 2 * n + 1)
                    nc.vector.tensor_scalar(h, h, MAGIC + QMAX, MAGIC - QMAX - 1.0, ALU.min, ALU.max).then_inc(h_grid, 1)
                for c in range(CH):
                    dve.wait_ge(y3_done, c + 1)
                    nc.vector.tensor_tensor(y_part[:, c % 2, :, :], banks[4 + c][:, :].rearrange("p (t d) -> p t d", t=4),
                                            wd_row[:, :].unsqueeze(1).to_broadcast([P, 4, D]), ALU.mult).then_inc(y3_read, 1)
                    dve.wait_ge(y3_read, c + 1)
                    nc.vector.tensor_tensor(xres[:, 4 * c:4 * c + 4, :], xres[:, 4 * c:4 * c + 4, :], y_part[:, c % 2, :, :],
                                            ALU.add).then_inc(out_ready, 1)

            @block.tensor
            def _(pe):
                for side in range(2):
                    for i in range(FT):
                        p = height[i]
                        last = nc.tensor.transpose(banks[side][:, P * i:P * i + p], gu_raw[0:p, side, i, :], ident[0:p, 0:p])
                    last.then_inc(wt_done, 1)
                for i in range(FT):
                    p = height[i]
                    last = nc.tensor.transpose(banks[2][0:p, D * i:D * i + D], wd_raw[:, P * i:P * i + p], ident[:, :])
                last.then_inc(wt_done, 1)
                nc.tensor.matmul(banks[3][:, 0:D], ones[:, :], wd_diag[:, :], start=True, stop=True).then_inc(wt_done, 1)
                pe.wait_ge(wt_read, 2 + FT)
                pe.wait_ge(z3_ready, NT)
                for n in range(CH):
                    for j in range(4):
                        last = nc.tensor.transpose(banks[4 + n][:, P * j:P * j + P], z3[:, 4 * n + j, :], ident[:, :])
                    last.then_inc(z3t_done, 1)
                for n in range(UNITS_H):
                    i, c = n // CH, n % CH
                    p = height[i]
                    pe.wait_ge(xq_ready, CH)
                    wait(pe, hidden_ready, n - 1)
                    nc.tensor.matmul(banks[4 + 2 * (n % 2)][0:p, :], gu_t[:, 0, P * i:P * i + p],
                                     x_q[:, 512 * c:512 * c + 512], start=True, stop=True)
                    nc.tensor.matmul(banks[5 + 2 * (n % 2)][0:p, :], gu_t[:, 1, P * i:P * i + p],
                                     x_q[:, 512 * c:512 * c + 512], start=True, stop=True).then_inc(gu_done, 1)
                for c in range(CH):
                    for j in range(4):
                        t = 4 * c + j
                        for i in range(FT):
                            p = height[i]
                            pe.wait_ge(hq_ready, CH * i + c + 1)
                            last = nc.tensor.matmul(banks[4 + c][:, P * j:P * j + P], hidden_q[0:p, i, P * t:P * t + P],
                                                    wd_t[0:p, i, :], start=(i == 0), stop=(i == FT - 1))
                    last.then_inc(y3_done, 1)
        scratch.close()


def laid_out(inputs):
    import numpy as _np
    a = {k: _np.ascontiguousarray(v) for k, v in inputs.items()}

    def tiles(m):
        return _np.ascontiguousarray(m.reshape(-1, P, m.shape[-1]).transpose(1, 0, 2))

    def heads_t(w):
        return _np.ascontiguousarray(w.reshape(w.shape[0], H0, DH0).transpose(2, 1, 0))

    return {
        "x": tiles(a["x"].reshape(N, D)),
        "ctx_tok": tiles(a["ctx_768"].reshape(N, C)),
        "ctx_t": _np.ascontiguousarray(a["ctx_768"].reshape(N, C).T),
        "l0_wq_t": heads_t(a["L0_xattn_Wq"]),
        "l0_wk_t": heads_t(a["L0_xattn_Wk"]),
        "l0_wv": a["L0_xattn_Wv"],
        "l0_wo": tiles(a["L0_xattn_Wo"]),
        "l0_bo": a["L0_xattn_bo"],
        "f0_wg": a["L0_ffn_Wg"],
        "f0_w1": tiles(a["L0_ffn_W1"].reshape(-1, D)),
        "f0_b1": _np.ascontiguousarray(a["L0_ffn_b1"].reshape(-1, P).T),
        "f0_wo_t": tiles(_np.ascontiguousarray(a["L0_ffn_Wo"].T)),
        "f0_bo": a["L0_ffn_bo"],
        "l1_qw": a["L1_xattn_q_w"], "l1_qb": a["L1_xattn_q_b"],
        "l1_kw": a["L1_xattn_k_w"], "l1_kb": a["L1_xattn_k_b"],
        "l1_vw": a["L1_xattn_v_w"], "l1_vb": a["L1_xattn_v_b"],
        "l1_g": a["L1_xattn_ln_g"], "l1_b": a["L1_xattn_ln_b"],
        "l1_tg": a["L1_xattn_tln_g"], "l1_tb": a["L1_xattn_tln_b"],
        "f1_cx": a["L1_ffn_clip_x"], "f1_cd": a["L1_ffn_clip_down"],
        "f1_wg": a["L1_ffn_w_gate"], "f1_wu": a["L1_ffn_w_up"], "f1_wd": a["L1_ffn_w_down"],
    }


def kernel(**inputs):
    import numpy as _np
    import concourse.bacc as _bacc
    from concourse import mybir as _mybir
    from concourse.bass_utils import run_bass_kernel_spmd as _run

    nc = _bacc.Bacc("TRN2", target_bir_lowering=False, num_devices=1)
    arrays, args = {}, {}
    for name, a in laid_out(inputs).items():
        arrays[f"in_{name}"] = a
        args[name] = nc.dram_tensor(f"in_{name}", a.shape, _mybir.dt.from_np(a.dtype), kind="ExternalInput").ap()
    out = nc.dram_tensor("out", (P, NT, D), F32, kind="ExternalOutput").ap()
    cross_ffn_network(nc, out=out, **args)
    r = _run(nc, [arrays], core_ids=[0])
    return _np.ascontiguousarray(r.results[0]["out"].transpose(1, 0, 2)).reshape(B, S, D)
```

```python
from contextlib import ExitStack

import concourse.bass as bass
from concourse import mybir

F32 = mybir.dt.float32
F16 = mybir.dt.float16
BF16 = mybir.dt.bfloat16
ALU = mybir.AluOpType
ACT = mybir.ActivationFunctionType
AX = mybir.AxisListType

P = 128
B = 8
S = 256
QT = S // P
NT = B * QT
N = B * S
D = 128
C = 96
H0 = 16
DH0 = 64
E = 8
HF = 256
HG = H0 // 4
H1 = 16
DH1 = D // H1
FF = 352
LN_EPS = 1e-5
W_SCALE = 64.0
MAGIC = 12582912.0
QMAX = 127.0
FT = -(-FF // P)
U = B * H0


def wait(eng, semaphore, value):
    if not isinstance(value, int) or value > 0:
        eng.wait_ge(semaphore, value)


def work_out(eng, values, places):
    for v in values:
        eng.compute_val(v)
    for ap in places:
        eng.lower_ap(ap)


def cross_ffn_network(nc, x, ctx_tok, ctx_t, l0_wq_t, l0_wk_t, l0_wv, l0_wo, l0_bo, f0_wg, f0_w1, f0_b1,
                      f0_wo_t, f0_bo, l1_qw, l1_qb, l1_kw, l1_kb, l1_vw, l1_vb, l1_g, l1_b, l1_tg, l1_tb,
                      f1_cx, f1_cd, f1_wg, f1_wu, f1_wd, out):
    with ExitStack() as ctx:
        def sb(name, shape, dt=F32):
            return ctx.enter_context(nc.sbuf_tensor(name, shape, dt))

        def sem(name):
            return ctx.enter_context(nc.semaphore(name))

        banks = [ctx.enter_context(nc.psum_tensor(f"bank{i}", [P, 512], F32)) for i in range(8)]

        height = [min(P, FF - P * i) for i in range(FT)]

        xres = sb("xres", [P, NT, D])
        ident = sb("ident", [P, P])
        ctx_halves = sb("ctx_halves", [P, 2 * N], F16)
        ctx_hi, ctx_lo = ctx_halves[:, 0:N], ctx_halves[:, N:2 * N]
        zt_halves = sb("zt_halves", [P, 2 * N], F16)
        zt_hi, zt_lo = zt_halves[:, 0:N], zt_halves[:, N:2 * N]
        m_hi = sb("m_hi", [P, H0, C], F16)
        m_lo = sb("m_lo", [P, H0, C], F16)
        bo_bc = sb("bo_bc", [P, D])
        wo = sb("wo", [P, H0 // 2, D])
        stats = sb("stats", [P, NT, 6])
        mv = sb("mv", [P, NT, 2])
        var_eps = sb("var_eps", [P, NT])
        rstd = sb("rstd", [P, NT])
        minus_half = sb("minus_half", [P, NT])
        eps_add = sb("eps_add", [P, NT])
        gate = sb("gate", [P, NT, E])
        fbo_bc = sb("fbo_bc", [P, D])
        fwo_t = sb("fwo_t", [P, HF // P, D])
        gu_max = sb("gu_max", [P, 2, FT])
        gu_scale = sb("gu_scale", [P, 2, FT])
        gu_inv = sb("gu_inv", [P, 2, FT])
        wd_max = sb("wd_max", [D, 1])
        wd_scale = sb("wd_scale", [D, 1])
        wd_inv = sb("wd_inv", [D, 1])
        arena_v = sb("arena_v", [P, NT * H0 * (2 * DH0 + 1)], F16)
        arena_o = sb("arena_o", [P, NT * H0 * DH0])
        v_hi = arena_v[:, 0:NT * H0 * (DH0 + 1)].rearrange("p (t h d) -> p t h d", t=NT, h=H0)
        v_lo = arena_v[:, NT * H0 * (DH0 + 1):].rearrange("p (t h d) -> p t h d", t=NT, h=H0)
        o_all = arena_o[:, :].rearrange("p (t h d) -> p t h d", t=NT, h=H0)

        at = 0

        def temp(width):
            nonlocal at
            at += width
            return arena_o[:, at - width:at]

        wq_t = temp(H0 * P).rearrange("p (h d) -> p h d", h=H0)
        wk_t = temp(H0 * P).rearrange("p (h c) -> p h c", h=H0)
        ctx_raw = temp(N)
        wv_raw = temp(H0 * DH0)
        z0 = temp(NT * D).rearrange("p (t d) -> p t d", t=NT)
        wv_hi = temp(H0 * DH0 // 2).bitcast(F16)
        wv_lo = temp(H0 * DH0 // 2).bitcast(F16)

        ld_x, ld_ctx, ld_wq, ld_wk, ld_wv, ld_wo = (sem(f"ld_{n}") for n in ("x", "ctx", "wq", "wk", "wv", "wo"))
        pads, fills = sem("pads"), sem("fills")
        st0, mv0, ve0, rs0, z0_ready = (sem(n) for n in ("st0", "mv0", "ve0", "rs0", "z0_ready"))
        ctx_hi_ready, ctx_lo_ready, wv_hi_ready, wv_lo_ready = (
            sem(n) for n in ("ctx_hi_ready", "ctx_lo_ready", "wv_hi_ready", "wv_lo_ready"))
        p0_mm, p0_hi, p0_lo = sem("p0_mm"), sem("p0_hi"), sem("p0_lo")
        NM = H0 // 4
        NV = NT * 2
        Z_AT = NM + NV
        HH = H0 // 2

        with nc.Block() as block:
            @block.sync
            def _(sp):
                sp.dma_start(ctx_raw[0:C, :], ctx_t).then_inc(ld_ctx, 16)
                sp.dma_start(wq_t[0:DH0, :, :], l0_wq_t).then_inc(ld_wq, 16)
                sp.dma_start(wk_t[0:DH0, :, 0:C], l0_wk_t).then_inc(ld_wk, 16)
                sp.dma_start(wv_raw[0:C, :], l0_wv).then_inc(ld_wv, 16)
                sp.dma_start(xres[:, :, :], x).then_inc(ld_x, 16)
                sp.dma_start(wo[:, :, :], l0_wo).then_inc(ld_wo, 16)
                sp.dma_start(bo_bc[:, :], l0_bo.partition_broadcast(P)).then_inc(ld_wo, 16)

            @block.gpsimd
            def _(pool):
                nc.gpsimd.memset(wk_t[DH0:P, :, :], 0.0).then_inc(fills, 1)
                pool.wait_ge(fills, 1)
                nc.gpsimd.memset(ident[:, :], 0.0).then_inc(fills, 1)
                pool.wait_ge(fills, 2)
                nc.gpsimd.affine_select(out=ident[:, :], in_=ident[:, :], compare_op=ALU.not_equal, fill=1.0,
                                        base=0, pattern=[[-1, P]], channel_multiplier=1).then_inc(fills, 1)
                pool.wait_ge(fills, 3)
                nc.gpsimd.memset(ctx_hi[C:C + 1, :], 1.0).then_inc(fills, 1)
                pool.wait_ge(fills, 4)
                nc.gpsimd.memset(v_hi[:, :, :, DH0:DH0 + 1], 1.0).then_inc(fills, 1)
                nc.gpsimd.memset(minus_half[:, :], -0.5).then_inc(fills, 1)
                pool.wait_ge(ve0, 1)
                pool.wait_ge(fills, 6)
                nc.gpsimd.tensor_tensor(rstd[:, :], var_eps[:, :], minus_half[:, :], ALU.pow).then_inc(rs0, 1)
                nc.gpsimd.tensor_tensor(z0[:, :, :], xres[:, :, :], mv[:, :, 0:1].to_broadcast([P, NT, D]),
                                        ALU.subtract).then_inc(z0_ready, 1)
                pool.wait_ge(rs0, 1)
                pool.wait_ge(z0_ready, 1)
                nc.gpsimd.tensor_tensor(z0[:, :, :], z0[:, :, :], rstd[:, :].unsqueeze(2).to_broadcast([P, NT, D]),
                                        ALU.mult).then_inc(z0_ready, 1)
                pool.wait_ge(ld_wo, 32)
                nc.gpsimd.tensor_tensor(xres[:, :, :], xres[:, :, :],
                                        bo_bc[:, :].unsqueeze(1).to_broadcast([P, NT, D]),
                                        ALU.add)

            @block.scalar
            def _(act):
                act.wait_ge(ld_ctx, 16)
                for n in range(N // 512):
                    w = slice(512 * n, 512 * n + 512)
                    nc.scalar.activation(ctx_hi[0:C, w], ctx_raw[0:C, w], ACT.Copy).then_inc(ctx_hi_ready, 1)
                act.wait_ge(ld_wv, 16)
                nc.scalar.activation(wv_hi[0:C, :], wv_raw[0:C, :], ACT.Copy).then_inc(wv_hi_ready, 1)
                for n in range(NM):
                    act.wait_ge(p0_mm, n + 1)
                    nc.scalar.activation(m_hi[:, 4 * n:4 * n + 4, :],
                                         banks[n % 8][:, :].rearrange("p (h c) -> p h c", h=4)[:, :, 0:C],
                                         ACT.Copy).then_inc(p0_hi, 1)

                def value_halves(k):
                    for j in range(8):
                        act.wait_ge(p0_mm, k * 8 + (NM + j + 1))
                        nc.scalar.activation(v_hi[:, k * 4 + j // 2, HH * (j % 2):HH * (j % 2) + HH, 0:DH0],
                                             banks[(NM + j) % 8][:, :].rearrange("p (h d) -> p h d", h=HH),
                                             ACT.Copy).then_inc(p0_hi, 1)
                with act.Fori(0, NV // 8) as k:
                    value_halves(k)
                for n in range(NT // 4):
                    act.wait_ge(p0_mm, Z_AT + n + 1)
                    nc.scalar.activation(zt_hi[:, 512 * n:512 * n + 512], banks[(Z_AT + n) % 8][:, :],
                                         ACT.Copy).then_inc(p0_hi, 1)

            @block.vector
            def _(dve):
                nc.vector.memset(wq_t[DH0:P, :, :], 0.0).then_inc(pads, 1)
                nc.vector.memset(wk_t[0:DH0, :, C:P], 0.0).then_inc(pads, 1)
                for n in range(N // 512):
                    w = slice(512 * n, 512 * n + 512)
                    dve.wait_ge(ctx_hi_ready, n + 1)
                    nc.vector.tensor_tensor(ctx_lo[0:C, w], ctx_raw[0:C, w], ctx_hi[0:C, w],
                                            ALU.subtract).then_inc(ctx_lo_ready, 1)
                dve.wait_ge(wv_hi_ready, 1)
                nc.vector.tensor_tensor(wv_lo[0:C, :], wv_raw[0:C, :], wv_hi[0:C, :],
                                        ALU.subtract).then_inc(wv_lo_ready, 1)
                dve.wait_ge(ld_x, 16)
                for t in range(NT):
                    nc.vector.bn_stats(stats[:, t, :], xres[:, t, :]).then_inc(st0, 1)
                for t in range(NT):
                    dve.wait_ge(st0, t + 1)
                    nc.vector.bn_aggr(mv[:, t, :], stats[:, t, :]).then_inc(mv0, 1)
                dve.wait_ge(mv0, NT)
                nc.vector.tensor_scalar(var_eps[:, :], mv[:, :, 1], LN_EPS, None, ALU.add).then_inc(ve0, 1)
                for n in range(NM):
                    dve.wait_ge(p0_hi, n + 1)
                    nc.vector.tensor_tensor(m_lo[:, 4 * n:4 * n + 4, :],
                                            banks[n % 8][:, :].rearrange("p (h c) -> p h c", h=4)[:, :, 0:C],
                                            m_hi[:, 4 * n:4 * n + 4, :], ALU.subtract).then_inc(p0_lo, 1)
                with dve.Fori(0, NV // 8) as k:
                    for j in range(8):
                        heads = slice(HH * (j % 2), HH * (j % 2) + HH)
                        dve.wait_ge(p0_hi, k * 8 + (NM + j + 1))
                        nc.vector.tensor_tensor(v_lo[:, k * 4 + j // 2, heads, :],
                                                banks[(NM + j) % 8][:, :].rearrange("p (h d) -> p h d", h=HH),
                                                v_hi[:, k * 4 + j // 2, heads, 0:DH0],
                                                ALU.subtract).then_inc(p0_lo, 1)
                for n in range(NT // 4):
                    dve.wait_ge(p0_hi, Z_AT + n + 1)
                    nc.vector.tensor_tensor(zt_lo[:, 512 * n:512 * n + 512], banks[(Z_AT + n) % 8][:, :],
                                            zt_hi[:, 512 * n:512 * n + 512], ALU.subtract).then_inc(p0_lo, 1)

            @block.tensor
            def _(pe):
                pe.wait_ge(ld_wq, 16)
                pe.wait_ge(ld_wk, 16)
                pe.wait_ge(pads, 2)
                pe.wait_ge(fills, 1)
                for h in range(H0):
                    last = nc.tensor.matmul(banks[h // 4][:, P * (h % 4):P * (h % 4) + P],
                                            wq_t[:, h, :], wk_t[:, h, :], start=True, stop=True)
                    if h % 4 == 3:
                        last.then_inc(p0_mm, 1)
                pe.wait_ge(ctx_lo_ready, N // 512)
                pe.wait_ge(wv_lo_ready, 1)

                def values(k):
                    for j in range(8):
                        wait(pe, p0_lo, k * 8 + (NM + j - 7))
                        tokens = bass.ds(k * 512 + (j // 2) * P, P)
                        heads = slice(512 * (j % 2), 512 * (j % 2) + 512)
                        bank = banks[(NM + j) % 8]
                        nc.tensor.matmul(bank[:, :], ctx_hi[0:C, tokens], wv_hi[0:C, heads], start=True, stop=False)
                        nc.tensor.matmul(bank[:, :], ctx_lo[0:C, tokens], wv_hi[0:C, heads], start=False, stop=False)
                        nc.tensor.matmul(bank[:, :], ctx_hi[0:C, tokens], wv_lo[0:C, heads], start=False,
                                         stop=True).then_inc(p0_mm, 1)
                values(0)
                with pe.Fori(1, NV // 8) as k:
                    values(k)
                pe.wait_ge(fills, 3)
                pe.wait_ge(z0_ready, 2)
                for n in range(NT // 4):
                    wait(pe, p0_lo, Z_AT + n - 7)
                    for j in range(4):
                        last = nc.tensor.transpose(banks[(Z_AT + n) % 8][:, P * j:P * j + P], z0[:, 4 * n + j, :],
                                                   ident[:, :])
                    last.then_inc(p0_mm, 1)

        scratch = ExitStack()

        def sb1(name, shape, dt=F32):
            return scratch.enter_context(nc.sbuf_tensor(name, shape, dt))

        RING = 4
        t_hi = sb1("t_hi", [P, H0, S], F16)
        t_lo = sb1("t_lo", [P, H0, S], F16)
        p32 = sb1("p32", [P, 2, QT * S])
        p_hi = sb1("p_hi", [P, RING, QT * S], F16)
        p_lo = sb1("p_lo", [P, RING, QT * S], F16)
        neg_max = sb1("neg_max", [P, 2, 4 * QT])
        neg_max_t = sb1("neg_max_t", [4 * QT, 2, P], F16)
        rsum = sb1("rsum", [P, 2, QT, 2])
        t_bank, max_bank, score_bank, o_bank = banks[0:2], banks[2:4], banks[4:6], banks[6:8]
        SHIFT_AT = 384
        LEAD_T, LEAD_MAX, LEAD_SHIFT = 12, 10, 5
        LAG_PV = 2
        SCALE0 = DH0 ** -0.5

        t_done, t_hi_ready, t_lo_ready, max_done, max_read = (
            sem(n) for n in ("t_done", "t_hi_ready", "t_lo_ready", "max_done", "max_read"))
        shift_in_psum, shift_read, scores_done, p32_ready, lo_ready, pv_done, sum_inverted, o_read = (
            sem(n) for n in ("shift_in_psum", "shift_read", "scores_done", "p32_ready", "lo_ready",
                             "pv_done", "sum_inverted", "o_read"))
        shift_row = [sem("shift_row_even"), sem("shift_row_odd")]

        def steps(eng, step):
            for s in range(-LEAD_T, 4):
                step(0, s)
            with eng.Fori(0, B - 1) as b:
                for s in range(4, 4 + H0):
                    step(b, s)
            for s in range(4, H0 + 5):
                step(B - 1, s)

        def there(b, s):
            return not isinstance(b, int) or 0 <= H0 * b + s < U

        def count(b, s):
            return b * H0 + s

        with nc.Block() as block:
            @block.tensor
            def _(pe):
                def make_t(b, s):
                    if s % 2 == 0:
                        wait(pe, t_lo_ready, count(b, s) // 2 - 1 if isinstance(b, int) else b * 8 + (s // 2 - 1))
                    tokens = bass.ds((b + s // H0) * S, S)
                    h = s % H0
                    dst = t_bank[(s // 2) % 2][0:C, S * (s % 2):S * (s % 2) + S]
                    nc.tensor.matmul(dst, m_hi[:, h, :], zt_hi[:, tokens], start=True, stop=False)
                    nc.tensor.matmul(dst, m_hi[:, h, :], zt_lo[:, tokens], start=False, stop=False)
                    nc.tensor.matmul(dst, m_lo[:, h, :], zt_hi[:, tokens], start=False, stop=True).then_inc(t_done, 1)

                def maxima(b, s):
                    pe.wait_ge(t_hi_ready, b * 8 + (s // 2 + 1))
                    wait(pe, max_read, count(b, s) - 1)
                    keys = bass.ds((b + s // H0) * S, S)
                    for q in range(QT):
                        last = nc.tensor.matmul(max_bank[s % 2][:, S * q:S * q + S],
                                                t_hi[0:C, s % H0, P * q:P * q + P], ctx_hi[0:C, keys],
                                                start=True, stop=True)
                    last.then_inc(max_done, 1)

                def shift(b, s):
                    pe.wait_ge(max_read, count(b, s) + 4)
                    wait(pe, shift_read, b * 4 + s // 4)
                    nc.tensor.transpose(o_bank[0][0:4 * QT, SHIFT_AT:SHIFT_AT + P], neg_max[:, (s // 4) % 2, :],
                                        ident[:, :]).then_inc(shift_in_psum, 1)

                def scores(b, s):
                    if s % 4 == 0:
                        pe.wait_ge(shift_row[(s // 4) % 2], b * 32 + 16 * (s // 8 + 1))
                    wait(pe, p32_ready, count(b, s) - 1)
                    h = s % H0
                    if s % 2 == 0:
                        pe.wait_ge(t_lo_ready, b * 8 + (s // 2 + 1))
                    for k in range(QT):
                        dst = score_bank[s % 2][:, S * k:S * k + S]
                        keys = bass.ds((b + s // H0) * S + P * k, P)
                        nc.tensor.matmul(dst, ctx_hi[0:C + 1, keys], t_hi[0:C + 1, h, :], start=True, stop=False)
                        nc.tensor.matmul(dst, ctx_hi[0:C, keys], t_lo[0:C, h, :], start=False, stop=False)
                        last = nc.tensor.matmul(dst, ctx_lo[0:C, keys], t_hi[0:C, h, :], start=False, stop=True)
                    last.then_inc(scores_done, 1)

                def values(b, s):
                    r, h, left = s % RING, s % H0, s % 2
                    if s % 2 == 0:
                        wait(pe, o_read, (count(b, s) // 2 - 1) if isinstance(b, int) else b * 8 + (s // 2 - 1))
                    pe.wait_ge(lo_ready, count(b, s) + 1)
                    for q in range(QT):
                        c0 = (DH0 + 1) * (2 * q + left)
                        dst = o_bank[(s // 2) % 2][:, c0:c0 + DH0 + 1]
                        for k in range(QT):
                            tile = b * QT + (s // H0 * QT + k)
                            w = slice(S * k + P * q, S * k + P * q + P)
                            nc.tensor.matmul(dst, p_hi[:, r, w], v_hi[:, tile, h, :], start=(k == 0), stop=False)
                            nc.tensor.matmul(dst[:, 0:DH0], p_hi[:, r, w], v_lo[:, tile, h, :], start=False, stop=False)
                            last = nc.tensor.matmul(dst, p_lo[:, r, w], v_hi[:, tile, h, :], start=False,
                                                    stop=(k == QT - 1))
                    last.then_inc(pv_done, 1)

                def step(b, s):
                    if not isinstance(b, int):
                        counts = [count(b, s) - 1, count(b, s + LEAD_MAX) - 1, count(b, s - LAG_PV) + 1]
                        if s % 2 == 0:
                            counts += [b * 8 + (s // 2 + 1), b * 8 + ((s + LEAD_T) // 2 - 1)]
                        u = s - LAG_PV
                        tiles = [b * QT + (u // H0 * QT + k) for k in range(QT)]
                        work_out(pe, counts, [v[:, t, u % H0, :] for t in tiles for v in (v_hi, v_lo)])
                    if there(b, s):
                        scores(b, s)
                    if there(b, s + LEAD_T):
                        make_t(b, s + LEAD_T)
                    if there(b, s + LEAD_MAX):
                        maxima(b, s + LEAD_MAX)
                    if (s + LEAD_SHIFT) % 4 == 0 and there(b, s + LEAD_SHIFT):
                        shift(b, s + LEAD_SHIFT)
                    if there(b, s - LAG_PV):
                        values(b, s - LAG_PV)
                steps(pe, step)

            @block.scalar
            def _(act):
                def exps(b, s):
                    r = s % 2
                    act.wait_ge(scores_done, count(b, s) + 1)
                    wait(act, pv_done, count(b, s) + 1 - RING)
                    nc.scalar.activation(p_hi[:, s % RING, :], score_bank[r][:, :], ACT.Exp, scale=SCALE0)
                    wait(act, lo_ready, count(b, s) - 1)
                    nc.scalar.activation(p32[:, r, :], score_bank[r][:, :], ACT.Exp, scale=SCALE0).then_inc(p32_ready, 1)

                def t_halves(b, s):
                    act.wait_ge(t_done, count(b, s) + 1)
                    wait(act, scores_done, count(b, s) + 1 - H0)
                    h = (s - 1) % H0
                    nc.scalar.activation(t_hi[0:C, h:h + 2, :],
                                         t_bank[(s // 2) % 2][0:C, :].rearrange("p (h q) -> p h q", h=2),
                                         ACT.Copy).then_inc(t_hi_ready, 1)

                def step(b, s):
                    if there(b, s):
                        exps(b, s)
                    if s % 2 == 1 and there(b, s + LEAD_T):
                        t_halves(b, s + LEAD_T)
                steps(act, step)

            @block.gpsimd
            def _(pool):
                def step(b, s):
                    if there(b, s):
                        r = s % RING
                        pool.wait_ge(p32_ready, count(b, s) + 1)
                        wait(pool, pv_done, count(b, s) + 1 - RING)
                        nc.gpsimd.tensor_tensor(p_lo[:, r, :], p32[:, s % 2, :], p_hi[:, r, :],
                                                ALU.subtract).then_inc(lo_ready, 1)
                steps(pool, step)

            @block.vector
            def _(dve):
                def t_rest(b, s):
                    pair = b * 8 + ((s - 1) // 2)
                    h = (s - 1) % H0
                    dve.wait_ge(t_hi_ready, pair + 1)
                    nc.vector.tensor_tensor(t_lo[0:C, h:h + 2, :],
                                            t_bank[(s // 2) % 2][0:C, :].rearrange("p (h q) -> p h q", h=2),
                                            t_hi[0:C, h:h + 2, :], ALU.subtract).then_inc(t_lo_ready, 1)

                def max_of(b, s):
                    g, j = (s // 4) % 2, s % 4
                    dve.wait_ge(max_done, count(b, s) + 1)
                    if j == 0:
                        wait(dve, shift_in_psum, (count(b, s) // 4 - 1) if isinstance(b, int) else b * 4 + (s // 4 - 1))
                    nc.vector.tensor_reduce(neg_max[:, g, QT * j:QT * j + QT],
                                            max_bank[s % 2][:, :].rearrange("p (q k) -> p q k", q=QT),
                                            AX.X, ALU.max, negate=True).then_inc(max_read, 1)

                def shift_out(b, s):
                    g = (s // 4) % 2
                    dve.wait_ge(shift_in_psum, b * 4 + (s // 4 + 1))
                    before = b * 32 + 16 * (s // 8)
                    wait(dve, shift_row[g], before)
                    nc.vector.tensor_copy(neg_max_t[:, g, :], o_bank[0][0:4 * QT, SHIFT_AT:SHIFT_AT + P])\
                        .then_inc(shift_read, 1)

                def output(b, s):
                    pair = b * 8 + (s // 2)
                    g, h = (s // 2) % 2, (s - 1) % H0
                    dve.wait_ge(pv_done, count(b, s) + 1)
                    o = o_bank[g][:, 0:QT * 2 * (DH0 + 1)].rearrange("p (q h d) -> p q h d", q=QT, h=2)
                    nc.vector.reciprocal(rsum[:, g, :, :], o[:, :, :, DH0]).then_inc(sum_inverted, 1)
                    dve.wait_ge(sum_inverted, pair + 1)
                    nc.vector.tensor_tensor(o_all[:, bass.ds((b + s // H0) * QT, QT), h:h + 2, :], o[:, :, :, 0:DH0],
                                            rsum[:, g, :, :].unsqueeze(3).to_broadcast([P, QT, 2, DH0]),
                                            ALU.mult).then_inc(o_read, 1)

                def step(b, s):
                    if s % 2 == 1 and there(b, s + LEAD_T):
                        t_rest(b, s + LEAD_T)
                    if there(b, s + LEAD_MAX):
                        max_of(b, s + LEAD_MAX)
                    if (s + LEAD_SHIFT) % 4 == 0 and there(b, s + LEAD_SHIFT):
                        if there(b, s - LAG_PV):
                            dve.wait_ge(pv_done, count(b, s - LAG_PV) + 1)
                        shift_out(b, s + LEAD_SHIFT)
                    if (s - LAG_PV) % 2 == 1 and there(b, s - LAG_PV):
                        output(b, s - LAG_PV)
                steps(dve, step)

            @block.sync
            def _(sp):
                def step(b, s):
                    if (s + LEAD_SHIFT) % 4 == 0 and there(b, s + LEAD_SHIFT):
                        u = s + LEAD_SHIFT
                        g, h = (u // 4) % 2, u % H0
                        sp.wait_ge(shift_read, b * 4 + (u // 4 + 1))
                        sp.dma_start(t_hi[C:C + 1, h:h + 4, :], neg_max_t[:, g, :]).then_inc(shift_row[g], 16)
                steps(sp, step)

        scratch.close()

        layer1 = ExitStack()
        scratch = ExitStack()
        at = 0

        def sb2(name, shape, dt=F32):
            return layer1.enter_context(nc.sbuf_tensor(name, shape, dt))

        def temp_v(width):
            nonlocal at
            at += width
            return arena_v[:, 2 * (at - width):2 * at].bitcast(F32)

        w1_raw = temp_v(E * HG * D).rearrange("p (r d) -> p r d", d=D)
        w1t_hi = temp_v(E * 2 * HF // 2).bitcast(F16)
        w1t_lo = temp_v(E * 2 * HF // 2).bitcast(F16)
        NR = E * 2 * HF // P
        ctx_n = temp_v(NT * C).rearrange("p (t c) -> p t c", t=NT)
        zc_t = temp_v(N)[0:C + 1, :]
        gu_raw = temp_v(2 * FT * D).rearrange("p (s i d) -> p s i d", s=2, i=FT)
        wd_raw = temp_v(FF)
        wd_diag = temp_v(D)
        ones = temp_v(P)
        GT = H1 // 4
        ROWS = 32
        SHIFT_ROW = 3 * DH1
        kw_ext = sb2("kw_ext", [C + 1, D])
        vw_ext = sb2("vw_ext", [C + 1, D])
        tb_ext = sb2("tb_ext", [C + 1, 1])
        tg_col = sb2("tg_col", [C, 1])
        qw = sb2("qw", [D, D])
        qb_row = sb2("qb_row", [1, D])
        g_col = sb2("g_col", [D, 1])
        b_col = sb2("b_col", [D, 1])
        k_rows = sb2("k_rows", [C + 1, GT, 4, ROWS])
        k_arr = sb2("k_arr", [C + 1, GT, 4 * ROWS])
        q_rows = sb2("q_rows", [D, GT, 4, ROWS])
        q_arr = sb2("q_arr", [D, GT, 4 * ROWS])
        qb_rows = sb2("qb_rows", [1, GT, 4, ROWS])
        v_arr = sb2("v_arr", [C + 1, D])
        k_low = sb2("k_low", [P, 1])
        q_low = sb2("q_low", [P, 1])
        zero = sb2("zero", [P, 1])
        v1 = sb2("v1", [P, NT, D])
        v_stage = sb2("v_stage", [P, QT, H1, ROWS])
        q_gain = sb1("q_gain", [D, D])
        last_one = sb1("last_one", [1, P])
        cstats = sb1("cstats", [P, NT, 6])
        cmv = sb1("cmv", [P, NT, 2])
        cvar = sb1("cvar", [P, NT])
        crstd = sb1("crstd", [P, NT])
        ld4, ld4c, ldw6 = sem("ld4"), sem("ld4c"), sem("ldw6")
        rows_zero, rows_ones, zc_ones, rows_filled, gains_in = (
            sem(n) for n in ("rows_zero", "rows_ones", "zc_ones", "rows_filled", "gains_in"))
        stc, mvc, vec, rsc, zc_ready, bias_done, bias_read, zct_done, zct_read, v1_done, v1_read = (
            sem(n) for n in ("stc", "mvc", "vec", "rsc", "zc_ready", "bias_done", "bias_read", "zct_done", "zct_read",
                             "v1_done", "v1_read"))
        o_t = sb1("o_t", [P, 2, H0 // 2, P])
        z1 = sb1("z1", [P, 2, D])
        b1_cols = sb1("b1_cols", [P, NR])
        wg_raw = sb1("wg_raw", [E, D])
        wg_shift = sb1("wg_shift", [E, D])
        wgt_hi = sb1("wgt_hi", [P, E], F16)
        wgt_lo = sb1("wgt_lo", [P, E], F16)
        logit_max = sb1("logit_max", [P, NT])
        prob, rank, logits = (temp_v(NT * E).rearrange("p (t e) -> p t e", t=NT) for _ in range(3))
        later, earlier = (temp_v(E * E).rearrange("p (e o) -> p e o", e=E) for _ in range(2))
        esum, einv, csum = (temp_v(NT) for _ in range(3))
        over, over_eq = (temp_v(4 * E * E).rearrange("p (t e o) -> p t e o", t=4, e=E) for _ in range(2))
        o_front, o_back, side_bank, y_bank, z_bank, g_bank = banks[0], banks[1], banks[2:4], banks[4:6], banks[6], banks[7]
        ld_w1, ld_wg, ld_b1, ld_f0 = sem("ld_w1"), sem("ld_wg"), sem("ld_b1"), sem("ld_f0")
        o_t_done, o_t_read, y1_done, x1_ready = (
            sem(n) for n in ("o_t_done", "o_t_read", "y1_done", "x1_ready"))
        st1, mv1, ve1, rs1, z1_ready, z1t_done, z1_hi_ready, z1_lo_ready = (
            sem(n) for n in ("st1", "mv1", "ve1", "rs1", "z1_ready", "z1t_done", "z1_hi_ready", "z1_lo_ready"))
        wg_shifted, wgt_done, wgt_hi_ready, wgt_lo_ready, gates_done = (
            sem(n) for n in ("wg_shifted", "wgt_done", "wgt_hi_ready", "wgt_lo_ready", "gates_done"))
        w1_shifted, w1_bias, w1t_done, w1t_hi_ready, w1t_lo_ready = (
            sem(n) for n in ("w1_shifted", "w1_bias", "w1t_done", "w1t_hi_ready", "w1t_lo_ready"))
        masks_set, route, prob_ready, logits_read, logits_shifted, weights_scaled = (
            sem(n) for n in ("masks_set", "route", "prob_ready", "logits_read", "logits_shifted", "weights_scaled"))
        LAG_PROJECT, LAG_Z, LAG_ZT, LAG_GATE = 1, 2, 3, 4
        ROUTE_AT = LAG_GATE + 4
        GATES = NT // 4
        LAST = ROUTE_AT + NT
        W1_AT, BIAS_AT, ZC_AT, V_AT = 5, 8, 11, 15
        W1_UNITS = NR // 4

        def route_tiles(dve, n, stage):
            four = slice(4 * n, 4 * n + 4)
            p, r, e_sum, e_inv, c_sum = prob[:, four, :], rank[:, four, :], esum[:, four], einv[:, four], csum[:, four]
            at_start = 15 * n

            def chained(k):
                dve.wait_ge(route, at_start + k)
            if stage == 0:
                dve.wait_ge(logits_read, 4 * n + 4)
                nc.vector.tensor_reduce(logit_max[:, four], logits[:, four, :], AX.X, ALU.max).then_inc(route, 1)
                chained(1)
                nc.vector.tensor_tensor(logits[:, four, :], logits[:, four, :],
                                        logit_max[:, four].unsqueeze(2).to_broadcast([P, 4, E]),
                                        ALU.subtract).then_inc(logits_shifted, 1)
            if stage == 1:
                dve.wait_ge(prob_ready, n + 1)
                nc.vector.tensor_reduce(e_sum, p, AX.X, ALU.add).then_inc(route, 1)
                chained(2)
                nc.vector.reciprocal(e_inv, e_sum).then_inc(route, 1)
                chained(3)
                nc.vector.tensor_tensor(p, p, e_inv.unsqueeze(2).to_broadcast([P, 4, E]), ALU.mult).then_inc(route, 1)
                chained(4)
                dve.wait_ge(masks_set, 4)
                other = p.unsqueeze(2).to_broadcast([P, 4, E, E])
                own = p.unsqueeze(3).to_broadcast([P, 4, E, E])
                nc.vector.tensor_tensor(over[:, :, :, :], other, own, ALU.is_gt).then_inc(route, 1)
                nc.vector.tensor_tensor(over_eq[:, :, :, :], other, own, ALU.is_ge).then_inc(route, 1)
            if stage == 2:
                chained(6)
                nc.vector.tensor_tensor(over[:, :, :, :], over[:, :, :, :],
                                        later[:, :, :].unsqueeze(1).to_broadcast([P, 4, E, E]), ALU.mult).then_inc(route, 1)
                nc.vector.tensor_tensor(over_eq[:, :, :, :], over_eq[:, :, :, :],
                                        earlier[:, :, :].unsqueeze(1).to_broadcast([P, 4, E, E]),
                                        ALU.mult).then_inc(route, 1)
                chained(8)
                nc.vector.tensor_tensor(over[:, :, :, :], over[:, :, :, :], over_eq[:, :, :, :], ALU.add).then_inc(route, 1)
                chained(9)
                nc.vector.tensor_reduce(r, over[:, :, :, :], AX.X, ALU.add).then_inc(route, 1)
                chained(10)
                nc.vector.scalar_tensor_tensor(p, r, 1.5, p, ALU.is_lt, ALU.mult).then_inc(route, 1)
                chained(11)
                nc.vector.tensor_reduce(e_sum, p, AX.X, ALU.add).then_inc(route, 1)
            if stage == 3:
                chained(12)
                nc.vector.tensor_scalar(c_sum, e_sum, 1e-9, None, ALU.add).then_inc(route, 1)
                chained(13)
                nc.vector.reciprocal(e_inv, c_sum).then_inc(route, 1)
                chained(14)
                nc.vector.tensor_tensor(c_sum, e_sum, e_inv, ALU.mult).then_inc(route, 1)
                nc.vector.tensor_scalar(e_inv, e_inv, 1.0 / W_SCALE, None, ALU.mult).then_inc(weights_scaled, 1)
                dve.wait_ge(weights_scaled, n + 1)
                nc.vector.tensor_tensor(gate[:, four, :], p, e_inv.unsqueeze(2).to_broadcast([P, 4, E]), ALU.mult)
                chained(15)
                dve.wait_ge(ld_f0, 32)
                for t in range(4 * n, 4 * n + 4):
                    last = nc.vector.scalar_tensor_tensor(xres[:, t, :], fbo_bc[:, :], csum[:, t:t + 1], xres[:, t, :],
                                                   ALU.mult, ALU.add)
                if n == GATES - 1:
                    last.then_inc(route, 1)
                    dve.wait_ge(route, 15 * GATES + 1)

        with nc.Block() as block:
            @block.sync
            def _(sp):
                sp.dma_start(wg_raw[:, :], f0_wg).then_inc(ld_wg, 16)
                sp.dma_start(b1_cols[:, :], f0_b1).then_inc(ld_b1, 16)
                sp.dma_start(ctx_n, ctx_tok).then_inc(ld4c, 16)
                with nc.allow_non_contiguous_dma(reason="a number per partition"):
                    for dst, src in ((kw_ext[0:C, :], l1_kw), (kw_ext[C:C + 1, :], l1_kb.unsqueeze(0)),
                                     (vw_ext[0:C, :], l1_vw), (vw_ext[C:C + 1, :], l1_vb.unsqueeze(0)),
                                     (tb_ext[0:C, :], l1_tb.unsqueeze(1)), (tg_col[:, :], l1_tg.unsqueeze(1)),
                                     (qw[:, :], l1_qw), (qb_row[:, :], l1_qb.unsqueeze(0)),
                                     (g_col[:, :], l1_g.unsqueeze(1)), (b_col[:, :], l1_b.unsqueeze(1))):
                        sp.dma_start(dst, src).then_inc(ld4, 16)
                sp.dma_start(w1_raw, f0_w1).then_inc(ld_w1, 16)
                sp.dma_start(fwo_t[:, :, :], f0_wo_t).then_inc(ld_f0, 16)
                sp.dma_start(fbo_bc[:, :], f0_bo.partition_broadcast(P)).then_inc(ld_f0, 16)
                for side, src in ((0, f1_wg), (1, f1_wu)):
                    for i in range(FT):
                        sp.dma_start(gu_raw[0:height[i], side, i, :], src[P * i:P * i + height[i], :]).then_inc(ldw6, 16)
                sp.dma_start(wd_raw[:, :], f1_wd).then_inc(ldw6, 16)

            @block.tensor
            def _(pe):
                for i in range(LAST):
                    t = i
                    if t < NT:
                        wait(pe, o_t_read, 2 * t)
                        for c in range(H0 // 2):
                            last = nc.tensor.transpose((o_front, o_back)[c // 4][:, P * (c % 4):P * (c % 4) + P],
                                                       arena_o[:, (t * 8 + c) * P:(t * 8 + c) * P + P], ident[:, :])
                        last.then_inc(o_t_done, 1)
                    if i == LAG_PROJECT:
                        pe.wait_ge(wg_shifted, 2)
                        nc.tensor.transpose(z_bank[:, 0:E], wg_shift[:, :], ident[0:E, 0:E]).then_inc(wgt_done, 1)
                    if 0 <= i - W1_AT < W1_UNITS:
                        n = i - W1_AT
                        pe.wait_ge(w1_bias, n + 1)
                        wait(pe, w1t_lo_ready, n)
                        for j in range(4):
                            last = nc.tensor.transpose(side_bank[0][:, P * j:P * j + P], w1_raw[:, 4 * n + j, :],
                                                       ident[:, :])
                        last.then_inc(w1t_done, 1)
                    t = i - LAG_PROJECT
                    if 0 <= t < NT:
                        pe.wait_ge(o_t_read, 2 * t + 2)
                        wait(pe, x1_ready, t - 1)
                        for c in range(H0 // 2):
                            last = nc.tensor.matmul(y_bank[t % 2][:, 0:D], o_t[:, t % 2, c, :], wo[:, c, :],
                                                    start=(c == 0), stop=(c == H0 // 2 - 1))
                        last.then_inc(y1_done, 1)
                    t = i - LAG_ZT
                    if 0 <= t < NT:
                        pe.wait_ge(z1_ready, t + 1)
                        pe.wait_ge(wgt_lo_ready, 1)
                        wait(pe, z1_lo_ready, t)
                        nc.tensor.transpose(z_bank[:, 0:P], z1[:, t % 2, :], ident[:, :]).then_inc(z1t_done, 1)
                    t = i - LAG_GATE
                    if 0 <= t < NT:
                        pe.wait_ge(z1_lo_ready, t + 1)
                        wait(pe, logits_read, t)
                        tokens = slice(P * t, P * t + P)
                        nc.tensor.matmul(g_bank[:, 0:E], zt_hi[:, tokens], wgt_hi[:, :], start=True, stop=False)
                        nc.tensor.matmul(g_bank[:, 0:E], zt_lo[:, tokens], wgt_hi[:, :], start=False, stop=False)
                        nc.tensor.matmul(g_bank[:, 0:E], zt_hi[:, tokens], wgt_lo[:, :], start=False,
                                         stop=True).then_inc(gates_done, 1)
                    if i == BIAS_AT:
                        bank = side_bank[1]
                        pe.wait_ge(rows_filled, 9)
                        pe.wait_ge(rows_ones, 3)
                        pe.wait_ge(gains_in, 6)
                        nc.tensor.matmul(bank[:, :], q_gain[:, :], q_rows[:, :, :, :].rearrange("p g j r -> p (g j r)"),
                                         start=True, stop=False)
                        nc.tensor.matmul(bank[:, :], last_one[:, :], qb_rows[:, :, :, :].rearrange("p g j r -> p (g j r)"),
                                         start=False, stop=True).then_inc(bias_done, 1)
                    if i == BIAS_AT + 1:
                        bank = side_bank[1]
                        pe.wait_ge(bias_read, 1)
                        nc.tensor.matmul(bank[C:C + 1, 0:D], tb_ext[:, :], vw_ext[:, :], start=True, stop=True)\
                            .then_inc(bias_done, 1)
                    if i == BIAS_AT + 2:
                        pe.wait_ge(bias_read, 2)
                        nc.tensor.matmul(side_bank[1][C:C + 1, :], tb_ext[:, :],
                                         k_rows[:, :, :, :].rearrange("p g j r -> p (g j r)"), start=True,
                                         stop=True).then_inc(bias_done, 1)
                    if 0 <= i - ZC_AT < NT // 4:
                        n = i - ZC_AT
                        pe.wait_ge(zc_ready, 4 * n + 4)
                        if n == 0:
                            pe.wait_ge(bias_read, 3)
                        wait(pe, zct_read, n)
                        for j in range(4):
                            last = nc.tensor.transpose(side_bank[1][0:C, P * j:P * j + P],
                                                       ctx_n[:, 4 * n + j, :], ident[:, :])
                        last.then_inc(zct_done, 1)
                    if 0 <= i - V_AT < NT // 4:
                        n = i - V_AT
                        pe.wait_ge(zct_read, NT // 4)
                        wait(pe, v1_read, n)
                        if n == 0:
                            pe.wait_ge(gains_in, 6)
                            pe.wait_ge(zc_ones, 1)
                        for j in range(4):
                            t = 4 * n + j
                            last = nc.tensor.matmul(side_bank[1][:, P * j:P * j + P],
                                                    zc_t[:, P * t:P * t + P], v_arr[:, :], start=True, stop=True)
                        last.then_inc(v1_done, 1)

            @block.scalar
            def _(act):
                for i in range(LAST):
                    t = i
                    if t < NT:
                        act.wait_ge(o_t_done, t + 1)
                        wait(act, y1_done, t - 1)
                        for half, bank in enumerate((o_front, o_back)):
                            nc.scalar.activation(o_t[:, t % 2, 4 * half:4 * half + 4, :],
                                                 bank[:, :].rearrange("p (c q) -> p c q", c=4), ACT.Copy).then_inc(o_t_read, 1)
                    if 0 <= i - W1_AT < W1_UNITS:
                        n = i - W1_AT
                        act.wait_ge(w1t_done, n + 1)
                        nc.scalar.activation(w1t_hi[:, 512 * n:512 * n + 512], side_bank[0][:, :], ACT.Copy,
                                             scale=W_SCALE).then_inc(w1t_hi_ready, 1)
                    if i == BIAS_AT + 1:
                        act.wait_ge(bias_done, 1)
                        nc.scalar.activation(q_arr[:, :, :].rearrange("p g r -> p (g r)"), side_bank[1][:, :],
                                             ACT.Copy).then_inc(bias_read, 1)
                    if i == BIAS_AT + 2:
                        act.wait_ge(bias_done, 2)
                        nc.scalar.activation(v_arr[C:C + 1, :], side_bank[1][C:C + 1, 0:D], ACT.Copy).then_inc(bias_read, 1)
                    if i == BIAS_AT + 3:
                        act.wait_ge(bias_done, 3)
                        nc.scalar.activation(k_arr[C:C + 1, :, :].rearrange("p g r -> p (g r)"),
                                             side_bank[1][C:C + 1, :], ACT.Copy).then_inc(bias_read, 1)
                    if 0 <= i - 1 - ZC_AT < NT // 4:
                        n = i - 1 - ZC_AT
                        act.wait_ge(zct_done, n + 1)
                        nc.scalar.activation(zc_t[0:C, 512 * n:512 * n + 512], side_bank[1][0:C, :],
                                             ACT.Copy).then_inc(zct_read, 1)
                    if 0 <= i - 1 - V_AT < NT // 4:
                        n = i - 1 - V_AT
                        act.wait_ge(v1_done, n + 1)
                        nc.scalar.activation(v1[:, 4 * n:4 * n + 4, :],
                                             side_bank[1][:, :].rearrange("p (t d) -> p t d", t=4),
                                             ACT.Copy).then_inc(v1_read, 1)
                    if i == LAG_PROJECT:
                        act.wait_ge(wgt_done, 1)
                        nc.scalar.activation(wgt_hi[:, :], z_bank[:, 0:E], ACT.Copy, scale=W_SCALE).then_inc(wgt_hi_ready, 1)
                    t = i - LAG_ZT
                    if 0 <= t < NT:
                        act.wait_ge(z1t_done, t + 1)
                        nc.scalar.activation(zt_hi[:, P * t:P * t + P], z_bank[:, 0:P], ACT.Copy).then_inc(z1_hi_ready, 1)
                    if i in (3, 4, 5):
                        act.wait_ge(ld4, 160)
                        act.wait_ge(rows_zero, 4)
                        w = slice(DH1 * (i - 3), DH1 * (i - 3) + DH1)
                        for dst, src in ((k_rows, kw_ext), (q_rows, qw), (qb_rows, qb_row)):
                            nc.scalar.activation(dst[:, :, :, w], src[:, :].rearrange("p (g j d) -> p g j d", g=GT, j=4),
                                                 ACT.Copy).then_inc(rows_filled, 1)
                    t = i - LAG_GATE
                    if 0 <= t < NT:
                        act.wait_ge(gates_done, t + 1)
                        nc.scalar.activation(logits[:, t, :], g_bank[:, 0:E], ACT.Copy).then_inc(logits_read, 1)
                    n = (i - ROUTE_AT) // 4
                    if i == ROUTE_AT + 4 * n and 0 <= n < GATES:
                        four = slice(4 * n, 4 * n + 4)
                        act.wait_ge(logits_shifted, n + 1)
                        nc.scalar.activation(prob[:, four, :], logits[:, four, :], ACT.Exp,
                                             scale=1.0 / W_SCALE).then_inc(prob_ready, 1)

            @block.gpsimd
            def _(pool):
                for m in (k_rows[:, :, :, :], q_rows[:, :, :, :], qb_rows[:, :, :, :], v_stage[:, :, :, :]):
                    nc.gpsimd.memset(m, 0.0).then_inc(rows_zero, 1)
                pool.wait_ge(rows_zero, 4)
                nc.gpsimd.memset(zc_t[C:C + 1, :], 1.0).then_inc(zc_ones, 1)
                pool.wait_ge(zc_ones, 1)
                nc.gpsimd.memset(later[:, :, :], 1.0).then_inc(masks_set, 1)
                nc.gpsimd.memset(earlier[:, :, :], 1.0).then_inc(masks_set, 1)
                pool.wait_ge(masks_set, 2)
                nc.gpsimd.affine_select(out=later[:, :, :], in_=later[:, :, :], compare_op=ALU.is_ge, fill=0.0,
                                        base=0, pattern=[[-1, E], [1, E]], channel_multiplier=0).then_inc(masks_set, 1)
                nc.gpsimd.affine_select(out=earlier[:, :, :], in_=earlier[:, :, :], compare_op=ALU.is_gt, fill=0.0,
                                        base=0, pattern=[[1, E], [-1, E]], channel_multiplier=0).then_inc(masks_set, 1)
                for t in range(NT):
                    n = t - W1_AT + 2
                    if 0 <= n < W1_UNITS:
                        pool.wait_ge(ld_w1, 16)
                        rows = slice(4 * n, 4 * n + 4)
                        nc.gpsimd.tensor_tensor(w1_raw[:, rows, 0:D - 1], w1_raw[:, rows, 0:D - 1],
                                                w1_raw[:, rows, D - 1:D].to_broadcast([P, 4, D - 1]),
                                                ALU.subtract).then_inc(w1_shifted, 1)
                    pool.wait_ge(mv1, t + 1)
                    nc.gpsimd.tensor_scalar(var_eps[:, t:t + 1], mv[:, t, 1:2], LN_EPS, None, ALU.add).then_inc(ve1, 1)
                    pool.wait_ge(ve1, t + 1)
                    nc.gpsimd.tensor_tensor(rstd[:, t:t + 1], var_eps[:, t:t + 1], minus_half[:, t:t + 1],
                                            ALU.pow).then_inc(rs1, 1)
                    if 7 <= t < 11:
                        four = slice(4 * (t - 7), 4 * (t - 7) + 4)
                        pool.wait_ge(vec, 1)
                        nc.gpsimd.tensor_tensor(crstd[:, four], cvar[:, four], minus_half[:, four],
                                                ALU.pow).then_inc(rsc, 1)

            @block.vector
            def _(dve):
                nc.vector.memset(z1[:, :, D - 1:D], 1.0)
                for i in range(LAST):
                    if 0 <= i - W1_AT < W1_UNITS:
                        n = i - W1_AT
                        dve.wait_ge(w1t_hi_ready, n + 1)
                        nc.vector.scalar_tensor_tensor(w1t_lo[:, 512 * n:512 * n + 512], side_bank[0][:, :], W_SCALE,
                                                       w1t_hi[:, 512 * n:512 * n + 512], ALU.mult,
                                                       ALU.subtract).then_inc(w1t_lo_ready, 1)
                    if i == 0:
                        dve.wait_ge(ld_wg, 16)
                        nc.vector.tensor_scalar(wg_shift[:, :], wg_raw[:, :], wg_raw[:, D - 1:D], None,
                                                ALU.subtract).then_inc(wg_shifted, 1)
                        dve.wait_ge(wg_shifted, 1)
                        nc.vector.memset(wg_shift[:, D - 1:D], 0.0).then_inc(wg_shifted, 1)
                    if i == LAG_PROJECT:
                        dve.wait_ge(wgt_hi_ready, 1)
                        nc.vector.scalar_tensor_tensor(wgt_lo[:, :], z_bank[:, 0:E], W_SCALE, wgt_hi[:, :], ALU.mult,
                                                       ALU.subtract).then_inc(wgt_lo_ready, 1)
                    t = i - LAG_PROJECT
                    if 0 <= t < NT:
                        dve.wait_ge(y1_done, t + 1)
                        nc.vector.tensor_tensor(xres[:, t, :], y_bank[t % 2][:, 0:D], xres[:, t, :],
                                                ALU.add).then_inc(x1_ready, 1)
                        dve.wait_ge(x1_ready, t + 1)
                        nc.vector.bn_stats(stats[:, t, :], xres[:, t, :]).then_inc(st1, 1)
                        dve.wait_ge(st1, t + 1)
                        nc.vector.bn_aggr(mv[:, t, :], stats[:, t, :]).then_inc(mv1, 1)
                    t = i - LAG_Z
                    if 0 <= t < NT:
                        dve.wait_ge(rs1, t + 1)
                        wait(dve, z1t_done, t - 1)
                        nc.vector.tensor_scalar(z1[:, t % 2, 0:D - 1], xres[:, t, 0:D - 1], mv[:, t, 0:1],
                                                rstd[:, t:t + 1], ALU.subtract, ALU.mult).then_inc(z1_ready, 1)
                    t = i - LAG_ZT
                    if 0 <= t < NT:
                        dve.wait_ge(z1_hi_ready, t + 1)
                        nc.vector.tensor_tensor(zt_lo[:, P * t:P * t + P], z_bank[:, 0:P], zt_hi[:, P * t:P * t + P],
                                                ALU.subtract).then_inc(z1_lo_ready, 1)
                    n = i - W1_AT + 1
                    if 0 <= n < W1_UNITS:
                        dve.wait_ge(w1_shifted, n + 1)
                        dve.wait_ge(ld_b1, 16)
                        nc.vector.tensor_copy(w1_raw[:, 4 * n:4 * n + 4, D - 1], b1_cols[:, 4 * n:4 * n + 4])\
                            .then_inc(w1_bias, 1)
                    if i == 1:
                        nc.vector.memset(tb_ext[C:C + 1, :], 1.0).then_inc(rows_ones, 1)
                        nc.vector.memset(zero[:, :], 0.0)
                        nc.vector.memset(last_one[:, P - 1:P], 1.0).then_inc(rows_ones, 1)
                        dve.wait_ge(rows_zero, 4)
                        nc.vector.memset(k_rows[C:C + 1, :, :, SHIFT_ROW:SHIFT_ROW + 1], 1.0).then_inc(rows_ones, 1)
                        nc.vector.memset(v_stage[:, :, :, DH1:DH1 + 1], 1.0)
                    if i == 0:
                        heads = ident[:, :].rearrange("p (j r) -> p j r", r=ROWS)
                        nc.vector.tensor_reduce(q_low[:, :], heads[:, :, DH1:2 * DH1], AX.XY, ALU.add,
                                                negate=True)
                        nc.vector.tensor_reduce(k_low[:, :], heads[:, :, 2 * DH1:3 * DH1], AX.XY, ALU.add,
                                                negate=True)
                    if 3 <= i < 7:
                        dve.wait_ge(ld4c, 16)
                        for t in range(4 * i - 12, 4 * i - 8):
                            nc.vector.bn_stats(cstats[:, t, :], ctx_n[:, t, :]).then_inc(stc, 1)
                    if 4 <= i < 8:
                        for t in range(4 * i - 16, 4 * i - 12):
                            dve.wait_ge(stc, t + 1)
                            nc.vector.bn_aggr(cmv[:, t, :], cstats[:, t, :]).then_inc(mvc, 1)
                    if i == 7:
                        dve.wait_ge(mvc, NT)
                        nc.vector.tensor_scalar(cvar[:, :], cmv[:, :, 1], LN_EPS, None, ALU.add).then_inc(vec, 1)
                    if i == 6:
                        dve.wait_ge(rows_filled, 9)
                        nc.vector.tensor_scalar(k_arr[0:C, :, :], k_rows[0:C, :, :, :].rearrange("p g j r -> p g (j r)"),
                                                tg_col[:, 0:1], None, ALU.mult).then_inc(gains_in, 1)
                        nc.vector.tensor_tensor(q_gain[:, :], ident[:, :], ident[:, D - 1:D].to_broadcast([D, D]),
                                                ALU.subtract).then_inc(gains_in, 1)
                        dve.wait_ge(gains_in, 2)
                        nc.vector.tensor_scalar(q_gain[:, :], q_gain[:, :], g_col[:, 0:1], None, ALU.mult).then_inc(gains_in, 1)
                        dve.wait_ge(gains_in, 3)
                        nc.vector.tensor_copy(q_gain[:, D - 1:D], b_col[:, :]).then_inc(gains_in, 1)
                        nc.vector.memset(last_one[:, 0:P - 1], 0.0).then_inc(gains_in, 1)
                        nc.vector.tensor_scalar(v_arr[0:C, :], vw_ext[0:C, :], tg_col[:, 0:1], None,
                                                ALU.mult).then_inc(gains_in, 1)
                    if ZC_AT - 1 <= i < ZC_AT + 3:
                        dve.wait_ge(rsc, i - ZC_AT + 2)
                        for t in range(4 * (i - ZC_AT) + 4, 4 * (i - ZC_AT) + 8):
                            nc.vector.tensor_scalar(ctx_n[:, t, :], ctx_n[:, t, :], cmv[:, t, 0:1], crstd[:, t:t + 1],
                                                    ALU.subtract, ALU.mult).then_inc(zc_ready, 1)
                    n = (i - ROUTE_AT) // 4
                    stage = (i - ROUTE_AT) % 4
                    if 0 <= n < GATES - 1 or n == GATES - 1 and stage == 0:
                        route_tiles(dve, n, stage)

        scratch.close()

        scratch = ExitStack()
        sig = temp_v(2 * HF).rearrange("p (r n) -> p r n", r=2)
        glu = temp_v(4 * HF).rearrange("p (r n) -> p r n", r=4)
        mix = sb1("mix", [P, 2, HF])
        mix_t = sb1("mix_t", [P, 2, HF // P, P])
        k_half = sb1("k_half", [P, 2, 2, S], F16)
        k_mix = sb1("k_mix", [P, 2, 2, S], F16)
        q_half = sb1("q_half", [P, 2, 2, S], F16)
        z2 = sb1("z2", [P, 2, D])
        stats2 = sb1("stats2", [P, 2, 6])
        mv_x2 = sb1("mv_x2", [P, 2, 2])
        var_x2 = sb1("var_x2", [P, 2])
        rstd_x2 = sb1("rstd_x2", [P, 2])
        z2_t = ctx_halves[:, :].bitcast(F32)
        q_mix = arena_v[:, 0:GT * N].rearrange("p (g n) -> p g n", g=GT)
        k_zeros = arena_o[:, :].rearrange("p (j g n) -> p j g n", j=4, g=GT)
        k_mask = arena_o[:, :].bitcast(F16).rearrange("p (j g n) -> p j g n", j=4, g=GT)
        h_bank, mt_bank, kq_bank, y2_bank = banks[0:4], banks[4], banks[5], banks[6:8]
        h_done, sig_ready, glu_ready, mixed, mix_t_done, mix_t_read, y2_done, x2_ready = (
            sem(n) for n in ("h_done", "sig_ready", "glu_ready", "mixed", "mix_t_done", "mix_t_read", "y2_done",
                             "x2_ready"))
        k_done, k_half_ready, k_mixed, k_zeroed, q_done, q_half_ready, q_mixed = (
            sem(n) for n in ("k_done", "k_half_ready", "k_mixed", "k_zeroed", "q_done", "q_half_ready", "q_mixed"))
        k_placed = [sem("k_placed_even"), sem("k_placed_odd")]
        x2_seen, st2, mv2, var2_ready, rs2, z2_ready, z2t_done, z2t_read = (
            sem(n) for n in ("x2_seen", "st2", "mv2", "var2_ready", "rs2", "z2_ready", "z2t_done", "z2t_read"))
        w6 = sem("w6")
        MIXES = E - 1
        AT_ZERO, AT_KEYS, AT_TRANSPOSE, AT_COPY, AT_NORMAL, AT_QUERIES, AT_PROJECT, AT_Z2T, AT_Z2T_READ = (
            0, 1, 3, 4, 3, 5, 6, 6, 7)
        LAG_Z2, LAG_Q = 2, 4

        def tiles_of(eng, tile):
            for r in range(LAG_Q):
                tile(0, r)
            with eng.Fori(0, (NT - LAG_Q) // 2) as k:
                tile(k, LAG_Q)
                tile(k, LAG_Q + 1)
            for r in range(LAG_Q, 2 * LAG_Q):
                tile((NT - LAG_Q) // 2, r)

        def has(k, r):
            return not isinstance(k, int) or 0 <= 2 * k + r < NT

        def q_bank(k, r):
            return kq_bank if has(k, r) else h_bank[r % 4]

        def pair_place(tiles, k, r):
            return tiles[:, 2 * (r % 2):2 * (r % 2) + 2, bass.ds((k + r // 2) * S, S)]

        with nc.Block() as block:
            @block.tensor
            def _(pe):
                def pair(bank, weights, moving, k, r):
                    for g in range(2):
                        last = nc.tensor.matmul(bank[:, S * g:S * g + S], weights[:, 2 * (r % 2) + g, :],
                                                moving[:, bass.ds((k + r // 2) * S, S)], start=True, stop=True)
                    return last

                def tile(k, r):
                    t = k * 2 + r
                    for e in range(E):
                        if has(k, r):
                            tokens = bass.ds(t * P, P)
                            bank = h_bank[e % 4]
                            wait(pe, glu_ready, k * (2 * E) + (r * E + e - 3))
                            w = slice(2 * HF * e, 2 * HF * e + 2 * HF)
                            nc.tensor.matmul(bank[:, :], zt_hi[:, tokens], w1t_hi[:, w], start=True, stop=False)
                            nc.tensor.matmul(bank[:, :], zt_lo[:, tokens], w1t_hi[:, w], start=False, stop=False)
                            nc.tensor.matmul(bank[:, :], zt_hi[:, tokens], w1t_lo[:, w], start=False,
                                             stop=True).then_inc(h_done, 1)
                        if has(k, r) and e == AT_KEYS:
                            wait(pe, k_mixed, k * 2 + r)
                            wait(pe, q_mixed, k * 2 + (r - LAG_Q))
                            pair(kq_bank, k_arr, zc_t, k, r).then_inc(k_done, 1)
                        if has(k, r - 1) and e == AT_TRANSPOSE:
                            pe.wait_ge(mixed, k * (2 * MIXES) + r * MIXES)
                            wait(pe, mix_t_read, k * 2 + (r - 1))
                            for c in range(HF // P):
                                last = nc.tensor.transpose(mt_bank[:, P * c:P * c + P],
                                                           mix[:, (r - 1) % 2, P * c:P * c + P], ident[:, :])
                            last.then_inc(mix_t_done, 1)
                        if has(k, r - LAG_Q) and e == AT_QUERIES:
                            if has(k, r):
                                pe.wait_ge(k_mixed, k * 2 + (r + 1))
                                wait(pe, q_mixed, k * 2 + (r - LAG_Q))
                            pe.wait_ge(z2t_read, k * 2 + (r - 2 - r % 2))
                            pair(q_bank(k, r), q_arr, z2_t, k, r - LAG_Q).then_inc(q_done, 1)
                        if has(k, r - 1) and e == AT_PROJECT:
                            pe.wait_ge(mix_t_read, k * 2 + r)
                            wait(pe, x2_ready, k * 2 + (r - 2))
                            wait(pe, z2t_read, k * 2 + (r - 3))
                            for c in range(HF // P):
                                last = nc.tensor.matmul(y2_bank[(r - 1) % 2][:, 0:D], mix_t[:, (r - 1) % 2, c, :],
                                                        fwo_t[:, c, :], start=(c == 0), stop=(c == HF // P - 1))
                            last.then_inc(y2_done, 1)
                        if has(k, r - LAG_Z2) and e == AT_Z2T:
                            pe.wait_ge(z2_ready, k * 2 + (r - LAG_Z2 + 1))
                            nc.tensor.transpose(y2_bank[r % 2][:, P:2 * P], z2[:, r % 2, :], ident[:, :])\
                                .then_inc(z2t_done, 1)
                tiles_of(pe, tile)

            @block.scalar
            def _(act):
                def tile(k, r):
                    for e in range(E):
                        if has(k, r):
                            act.wait_ge(h_done, k * (2 * E) + (r * E + e + 1))
                            wait(act, glu_ready, k * (2 * E) + (r * E + e - 1))
                            nc.scalar.activation(sig[:, e % 2, :], h_bank[e % 4][:, HF:2 * HF], ACT.Sigmoid,
                                                 scale=1.0 / W_SCALE).then_inc(sig_ready, 1)
                        if has(k, r) and e == AT_ZERO:
                            g = 2 * (r % 2)
                            nc.scalar.activation(k_zeros[:, :, g:g + 2, bass.ds((k + r // 2) * (S // 2), S // 2)],
                                                 zero[:, 0:1].unsqueeze(2).unsqueeze(3).to_broadcast([P, 4, 2, S // 2]),
                                                 ACT.Copy).then_inc(k_zeroed, 1)
                        if has(k, r) and e == AT_KEYS:
                            act.wait_ge(k_done, k * 2 + (r + 1))
                            wait(act, k_mixed, k * 2 + (r - 1))
                            nc.scalar.activation(k_half[:, r % 2, :, :], kq_bank[:, :].rearrange("p (g n) -> p g n", g=2),
                                                 ACT.Copy).then_inc(k_half_ready, 1)
                        if has(k, r - 1) and e == AT_COPY:
                            act.wait_ge(mix_t_done, k * 2 + r)
                            nc.scalar.activation(mix_t[:, (r - 1) % 2, :, :],
                                                 mt_bank[:, 0:HF].rearrange("p (c q) -> p c q", q=P),
                                                 ACT.Copy).then_inc(mix_t_read, 1)
                        if has(k, r - LAG_Q) and e == AT_QUERIES:
                            act.wait_ge(q_done, k * 2 + (r - LAG_Q + 1))
                            wait(act, q_mixed, k * 2 + (r - LAG_Q - 1) if r > LAG_Q else 0)
                            nc.scalar.activation(q_half[:, r % 2, :, :], q_bank(k, r)[:, :].rearrange("p (g n) -> p g n", g=2),
                                                 ACT.Copy).then_inc(q_half_ready, 1)
                        if has(k, r - LAG_Z2) and e == AT_Z2T_READ:
                            act.wait_ge(z2t_done, k * 2 + (r - LAG_Z2 + 1))
                            nc.scalar.activation(z2_t[:, bass.ds((k * 2 + (r - LAG_Z2)) * P, P)], y2_bank[r % 2][:, P:2 * P],
                                                 ACT.Copy).then_inc(z2t_read, 1)
                tiles_of(act, tile)

            @block.vector
            def _(dve):
                ROUTE_PLACES = [(0, 0, 1), (0, 0, 4), (0, 1, 2)]
                nc.vector.memset(z2[:, :, D - 1:D], 1.0)

                def weight_scales():
                    nc.vector.memset(ones[:, :], 1.0).then_inc(w6, 1)
                    dve.wait_ge(ldw6, 112)
                    for side in range(2):
                        for i in range(FT):
                            p = height[i]
                            nc.vector.tensor_reduce(gu_max[0:p, side, i:i + 1], gu_raw[0:p, side, i, :], AX.X, ALU.max,
                                                    apply_absolute_value=True).then_inc(w6, 1)
                    nc.vector.tensor_reduce(wd_max[:, :], wd_raw[:, :], AX.X, ALU.max, apply_absolute_value=True).then_inc(w6, 1)
                    dve.wait_ge(w6, 8)
                    for i in range(FT):
                        p = height[i]
                        nc.vector.tensor_scalar(gu_scale[0:p, :, i], gu_max[0:p, :, i], 1.0 / QMAX, None, ALU.mult).then_inc(w6, 1)
                    nc.vector.tensor_scalar(wd_scale[:, :], wd_max[:, :], 1.0 / QMAX, None, ALU.mult).then_inc(w6, 1)
                    dve.wait_ge(w6, 12)
                    for i in range(FT):
                        p = height[i]
                        nc.vector.reciprocal(gu_inv[0:p, :, i], gu_scale[0:p, :, i]).then_inc(w6, 1)
                    nc.vector.reciprocal(wd_inv[:, :], wd_scale[:, :]).then_inc(w6, 1)
                    nc.vector.tensor_scalar(wd_diag[:, :], ident[:, :], wd_scale[:, 0:1], None, ALU.mult).then_inc(w6, 1)

                def split(half, bank, low, dst):
                    return nc.vector.scalar_tensor_tensor(dst, half, low[:, 0:1],
                                                          bank[:, :].rearrange("p (g n) -> p g n", g=2), ALU.mult, ALU.add)

                def tile(k, r):
                    if isinstance(k, int) and 2 * k + r == NT + LAG_Z2:
                        weight_scales()
                    for e in range(E):
                        if has(k, r):
                            dve.wait_ge(sig_ready, k * (2 * E) + (r * E + e + 1))
                            if e >= 4:
                                dve.wait_ge(mixed, k * (2 * MIXES) + (r * MIXES + max(e - 4, 1)))
                            elif has(k, r - 1):
                                dve.wait_ge(mixed, k * (2 * MIXES) + ((r - 1) * MIXES + e + 4))
                            nc.vector.scalar_tensor_tensor(glu[:, e % 4, :], sig[:, e % 2, :],
                                                           gate[:, bass.ds(k * 2 + r, 1), e:e + 1].rearrange("p a b -> p (a b)"),
                                                           h_bank[e % 4][:, 0:HF], ALU.mult,
                                                           ALU.mult).then_inc(glu_ready, 1)
                            if isinstance(k, int) and (k, r, e) in ROUTE_PLACES:
                                route_tiles(dve, GATES - 1, ROUTE_PLACES.index((k, r, e)) + 1)
                        if has(k, r) and e == AT_KEYS:
                            dve.wait_ge(k_half_ready, k * 2 + (r + 1))
                            wait(dve, k_placed[r % 2], k * 64 + r // 2 * 64)
                            split(k_half[:, r % 2, :, :], kq_bank, k_low, k_mix[:, r % 2, :, :]).then_inc(k_mixed, 1)
                        if has(k, r - LAG_Z2) and e == AT_NORMAL:
                            dve.wait_ge(rs2, k * 2 + (r - LAG_Z2 + 1))
                            wait(dve, z2t_done, k * 2 + (r - LAG_Z2 - 1))
                            nc.vector.tensor_scalar(z2[:, r % 2, 0:D - 1],
                                                    xres[:, bass.ds(k * 2 + (r - LAG_Z2), 1), 0:D - 1]
                                                    .rearrange("p t d -> p (t d)"), mv_x2[:, r % 2, 0:1],
                                                    rstd_x2[:, r % 2:r % 2 + 1], ALU.subtract, ALU.mult).then_inc(z2_ready, 1)
                        if has(k, r - LAG_Q) and e == AT_QUERIES:
                            dve.wait_ge(q_half_ready, k * 2 + (r - LAG_Q + 1))
                            split(q_half[:, r % 2, :, :], q_bank(k, r), q_low, pair_place(q_mix, k, r - LAG_Q)).then_inc(q_mixed, 1)
                    if has(k, r - 1):
                        row = xres[:, bass.ds(k * 2 + (r - 1), 1), :]
                        p = (r - 1) % 2
                        dve.wait_ge(y2_done, k * 2 + r)
                        nc.vector.tensor_tensor(row, y2_bank[p][:, 0:D].unsqueeze(1), row, ALU.add).then_inc(x2_ready, 1)
                        dve.wait_ge(x2_ready, k * 2 + r)
                        dve.sem_inc(x2_seen, 1)
                        nc.vector.bn_stats(stats2[:, p, :], row).then_inc(st2, 1)
                        dve.wait_ge(st2, k * 2 + r)
                        dve.sem_inc(x2_seen, 1)
                        nc.vector.bn_aggr(mv_x2[:, p, :], stats2[:, p, :]).then_inc(mv2, 1)
                        dve.wait_ge(mv2, k * 2 + r)
                        nc.vector.tensor_scalar(var_x2[:, p:p + 1], mv_x2[:, p, 1:2], LN_EPS, None,
                                                ALU.add).then_inc(var2_ready, 1)
                tiles_of(dve, tile)

            @block.gpsimd
            def _(pool):
                def tile(k, r):
                    for e in range(1, E):
                        if has(k, r):
                            pool.wait_ge(glu_ready, k * (2 * E) + (r * E + e + 1))
                            if e == 1:
                                wait(pool, mix_t_done, k * 2 + (r - 1))
                            else:
                                pool.wait_ge(mixed, k * (2 * MIXES) + (r * MIXES + e - 1))
                            nc.gpsimd.tensor_tensor(mix[:, r % 2, :], glu[:, 0, :] if e == 1 else mix[:, r % 2, :],
                                                    glu[:, e % 4, :], ALU.add).then_inc(mixed, 1)
                        if has(k, r - LAG_Z2) and e == AT_NORMAL - 1:
                            p = slice(r % 2, r % 2 + 1)
                            pool.wait_ge(var2_ready, k * 2 + (r - LAG_Z2 + 1))
                            nc.gpsimd.tensor_tensor(rstd_x2[:, p], var_x2[:, p], minus_half[:, 0:1], ALU.pow).then_inc(rs2, 1)
                tiles_of(pool, tile)

            @block.sync
            def _(sp):
                def tile(k, r):
                    if not has(k, r):
                        return
                    g = 2 * (r % 2)
                    places = [k_mask[ROWS * j:ROWS * j + ROWS, j, g:g + 2, bass.ds((k + r // 2) * S, S)] for j in range(4)]
                    if not isinstance(k, int):
                        work_out(sp, (k * 2 + (r + 1),), places)
                    sp.wait_ge(k_zeroed, k * 2 + (r + 1))
                    sp.wait_ge(k_mixed, k * 2 + (r + 1))
                    for j, place in enumerate(places):
                        sp.dma_start(place, k_mix[ROWS * j:ROWS * j + ROWS, r % 2, :, :]).then_inc(k_placed[r % 2], 16)
                tiles_of(sp, tile)
                for placed in k_placed:
                    sp.wait_ge(placed, 64 * NT // 2)
        scratch.close()

        scratch = ExitStack()
        RING1 = 4
        at = GT * N // 2
        p1 = temp_v(RING1 * QT * S).rearrange("p (r n) -> p r n", r=RING1)
        neg_max1 = sb1("neg_max1", [P, 2, 4 * QT])
        neg_max1_t = sb1("neg_max1_t", [4 * QT, 2, P], F16)
        y_sb = temp_v(2 * S).rearrange("p (r n) -> p r n", r=2)
        y_inv = sb1("y_inv", [P, 2, QT, 4])
        y_norm = sb1("y_norm", [P, 2, QT, 4, DH1])
        score_bank, max_bank, y_bank, shift_bank, yt_bank = banks[0:2], banks[2:4], banks[4:6], banks[6], banks[7]
        LEAD_MAX, LEAD_SHIFT, LAG_PV, LAG_Y, LAG_YT, LAG_FINISH = 11, 6, 3, 7, 9, 10
        SCALE1 = float(DH1) ** -0.5
        max1_done, max1_read, shift1_done, shift1_read, scores1_done, p1_ready, staged, pv1_done = (
            sem(n) for n in ("max1_done", "max1_read", "shift1_done", "shift1_read", "scores1_done", "p1_ready",
                             "staged", "pv1_done"))
        y1_read, y1t_done, y1_inverted, y1t_read, x3_ready = (
            sem(n) for n in ("y1_read", "y1t_done", "y1_inverted", "y1t_read", "x3_ready"))
        shift1_row = [sem("shift1_row_even"), sem("shift1_row_odd")]

        PEELED = 14

        def steps1(eng, step):
            for s in range(-LEAD_MAX, PEELED):
                step(0, s)
            with eng.Fori(0, B - 2) as b:
                for s in range(PEELED, PEELED + H1):
                    step(b, s)
            for s in range(PEELED, 2 * H1 + LAG_FINISH + 2):
                step(B - 2, s)

        def group(b, s):
            return b * GT + s // 4

        with nc.Block() as block:
            @block.tensor
            def _(pe):
                def maxima(b, s):
                    g, j = (s // 4) % GT, s % 4
                    wait(pe, max1_read, count(b, s) - 1)
                    for q in range(QT):
                        last = nc.tensor.matmul(max_bank[s % 2][:, S * q:S * q + S],
                                                q_mix[:, g, bass.ds((b + s // H1) * S + P * q, P)],
                                                k_mask[:, j, g, bass.ds((b + s // H1) * S, S)], start=True, stop=True)
                    last.then_inc(max1_done, 1)

                def shift(b, s):
                    pe.wait_ge(max1_read, count(b, s) + 4)
                    wait(pe, shift1_read, group(b, s))
                    nc.tensor.transpose(shift_bank[0:4 * QT, 0:P], neg_max1[:, (s // 4) % 2, :],
                                        ident[:, :]).then_inc(shift1_done, 1)

                def scores(b, s):
                    g, j = (s // 4) % GT, s % 4
                    if j == 0:
                        pe.wait_ge(shift1_row[(s // 4) % 2], b * 32 + 16 * (s // 8 + 1))
                    wait(pe, p1_ready, count(b, s) - 1)
                    for k in range(QT):
                        last = nc.tensor.matmul(score_bank[s % 2][:, S * k:S * k + S],
                                                k_mask[:, j, g, bass.ds((b + s // H1) * S + P * k, P)],
                                                q_mix[:, g, bass.ds((b + s // H1) * S, S)], start=True, stop=True)
                    last.then_inc(scores1_done, 1)

                def values(b, s):
                    g, j = s // 4, s % 4
                    if j == 0:
                        wait(pe, y1_read, group(b, s) - 1)
                        pe.wait_ge(staged, b * GT + (g + 1))
                    if not there(b, s + LAG_PV):
                        pe.wait_ge(p1_ready, count(b, s) + 1)
                    for k in range(QT):
                        last = nc.tensor.matmul(y_bank[g % 2][ROWS * j:ROWS * j + ROWS, 0:S], v_stage[:, k, s % H1, :],
                                                p1[:, s % RING1, S * k:S * k + S], start=(k == 0), stop=(k == QT - 1))
                    last.then_inc(pv1_done, 1)

                def back(b, s):
                    g = s // 4
                    pe.wait_ge(y1_read, b * GT + (g + 1))
                    wait(pe, y1t_read, group(b, s))
                    for q in range(QT):
                        last = nc.tensor.transpose(yt_bank[:, P * q:P * q + P], y_sb[:, g % 2, P * q:P * q + P],
                                                   ident[:, :])
                    last.then_inc(y1t_done, 1)

                def max_query(b, s, q):
                    return q_mix[:, (s // 4) % GT, bass.ds((b + s // H1) * S + P * q, P)]

                def max_keys(b, s):
                    return k_mask[:, s % 4, (s // 4) % GT, bass.ds((b + s // H1) * S, S)]

                def score_keys(b, s, k):
                    return k_mask[:, s % 4, (s // 4) % GT, bass.ds((b + s // H1) * S + P * k, P)]

                def score_queries(b, s):
                    return q_mix[:, (s // 4) % GT, bass.ds((b + s // H1) * S, S)]

                def step(b, s):
                    if not isinstance(b, int):
                        work_out(pe, (count(b, s) - 1, count(b, s + LEAD_MAX) - 1),
                                 (max_query(b, s + LEAD_MAX, 0), max_query(b, s + LEAD_MAX, 1), max_keys(b, s + LEAD_MAX),
                                  score_keys(b, s, 0), score_keys(b, s, 1), score_queries(b, s)))
                    if there(b, s):
                        scores(b, s)
                    if there(b, s + LEAD_MAX):
                        maxima(b, s + LEAD_MAX)
                    if (s + LEAD_SHIFT) % 4 == 0 and there(b, s + LEAD_SHIFT):
                        shift(b, s + LEAD_SHIFT)
                    if there(b, s - LAG_PV):
                        values(b, s - LAG_PV)
                    if (s - LAG_YT) % 4 == 0 and there(b, s - LAG_YT):
                        back(b, s - LAG_YT)
                steps1(pe, step)

            @block.scalar
            def _(act):
                def shift_out(b, s):
                    g = (s // 4) % 2
                    act.wait_ge(shift1_done, b * GT + (s // 4 + 1))
                    wait(act, shift1_row[g], b * 32 + 16 * (s // 8))
                    nc.scalar.activation(neg_max1_t[:, g, :], shift_bank[0:4 * QT, 0:P], ACT.Copy).then_inc(shift1_read, 1)

                def step(b, s):
                    if there(b, s):
                        act.wait_ge(scores1_done, count(b, s) + 1)
                        wait(act, pv1_done, count(b, s) + 1 - RING1)
                        nc.scalar.activation(p1[:, s % RING1, :], score_bank[s % 2][:, :], ACT.Exp,
                                             scale=SCALE1).then_inc(p1_ready, 1)
                    u = s + LEAD_SHIFT - 1
                    if u % 4 == 0 and there(b, u):
                        shift_out(b, u)
                    u = s - LAG_Y
                    if u % 4 == 0 and there(b, u):
                        act.wait_ge(pv1_done, count(b, u) + 4)
                        wait(act, y1t_done, group(b, u) - 1)
                        nc.scalar.activation(y_sb[:, (u // 4) % 2, :], y_bank[(u // 4) % 2][:, 0:S],
                                             ACT.Copy).then_inc(y1_read, 1)
                steps1(act, step)

            @block.vector
            def _(dve):
                def max_of(b, s):
                    g, j = (s // 4) % 2, s % 4
                    dve.wait_ge(max1_done, count(b, s) + 1)
                    if j == 0:
                        wait(dve, shift1_done, group(b, s) - 1)
                    nc.vector.tensor_reduce(neg_max1[:, g, QT * j:QT * j + QT],
                                            max_bank[s % 2][:, :].rearrange("p (q k) -> p q k", q=QT),
                                            AX.X, ALU.max, negate=True).then_inc(max1_read, 1)

                def finish(b, s):
                    g = (s // 4) % 2
                    y = yt_bank[:, 0:QT * P].rearrange("p (q j r) -> p q j r", q=QT, j=4)
                    dve.wait_ge(y1t_done, b * GT + (s // 4 + 1))
                    nc.vector.reciprocal(y_inv[:, g, :, :], y[:, :, :, DH1]).then_inc(y1_inverted, 1)
                    dve.wait_ge(y1_inverted, b * GT + (s // 4 + 1))
                    wait(dve, x3_ready, group(b, s) - 1)
                    nc.vector.tensor_tensor(y_norm[:, g, :, :, :], y[:, :, :, 0:DH1],
                                            y_inv[:, g, :, :].unsqueeze(3).to_broadcast([P, QT, 4, DH1]),
                                            ALU.mult).then_inc(y1t_read, 1)

                def step(b, s):
                    if there(b, s + LEAD_MAX):
                        max_of(b, s + LEAD_MAX)
                    u = s - LAG_FINISH
                    if u % 4 == 0 and there(b, u):
                        finish(b, u)
                    u = s - LAG_FINISH - 1
                    if u % H1 == H1 - 4 and there(b, u):
                        dve.wait_ge(x3_ready, b * GT + (u // 4 + 1))
                        for q in range(QT):
                            t = bass.ds((b + u // H1) * QT + q, 1)
                            nc.vector.bn_stats(stats[:, t, :], xres[:, t, :])
                steps1(dve, step)

            @block.gpsimd
            def _(pool):
                def on_grid(n):
                    def put(dst, inv):
                        if n == 0:
                            return nc.gpsimd.tensor_scalar(dst, dst, inv, MAGIC, ALU.mult, ALU.add)
                        if n == 1:
                            return nc.gpsimd.tensor_scalar(dst, dst, MAGIC + QMAX, MAGIC - QMAX - 1.0, ALU.min, ALU.max)
                        return nc.gpsimd.tensor_scalar(dst, dst, MAGIC, None, ALU.subtract)
                    pool.wait_ge(w6, 17 + 7 * n)
                    for side in range(2):
                        for i in range(FT):
                            p = height[i]
                            put(gu_raw[0:p, side, i, :], gu_inv[0:p, side, i:i + 1]).then_inc(w6, 1)
                    put(wd_raw[:, :], wd_inv[:, 0:1]).then_inc(w6, 1)

                def step(b, s):
                    u = s + LEAD_SHIFT
                    if u % 4 == 0 and there(b, u):
                        h = u % H1
                        wait(pool, pv1_done, count(b, u) + 4 - H1)
                        nc.gpsimd.tensor_copy(v_stage[:, :, h:h + 4, 0:DH1],
                                              v1[:, bass.ds((b + u // H1) * QT, QT), DH1 * h:DH1 * h + 4 * DH1]
                                              .rearrange("p t (h d) -> p t h d", h=4)).then_inc(staged, 1)
                    if isinstance(b, int) and count(b, s) in (0, 4, 8):
                        on_grid(s // 4)
                    u = s - LAG_FINISH
                    if u % 4 == 0 and there(b, u):
                        h = u % H1
                        pool.wait_ge(y1t_read, b * GT + (u // 4 + 1))
                        rows = xres[:, bass.ds((b + u // H1) * QT, QT), DH1 * h:DH1 * h + 4 * DH1]
                        nc.gpsimd.tensor_tensor(rows, rows, y_norm[:, (u // 4) % 2, :, :, :]
                                                .rearrange("p q j d -> p q (j d)"), ALU.add).then_inc(x3_ready, 1)
                steps1(pool, step)

            @block.sync
            def _(sp):
                def step(b, s):
                    u = s + LEAD_SHIFT
                    if u % 4 == 0 and there(b, u):
                        g = (u // 4) % 2
                        sp.wait_ge(shift1_read, b * GT + (u // 4 + 1))
                        sp.dma_start(q_mix[SHIFT_ROW:P:ROWS, (u // 4) % GT, bass.ds((b + u // H1) * S, S)],
                                     neg_max1_t[:, g, :]).then_inc(shift1_row[g], 16)
                steps1(sp, step)
        scratch.close()
        layer1.close()

        scratch = ExitStack()
        CH = N // 512
        at = 0
        z3 = temp_v(N).rearrange("p (t d) -> p t d", t=NT)
        grid = temp_v(N)
        gated = temp_v(512 * 2).rearrange("p (r n) -> p r n", r=2)
        hidden = arena_o[:, 0:FT * N].rearrange("p (i n) -> p i n", i=FT)
        hidden_q = arena_o[:, FT * N:FT * N + FT * N // 2].bitcast(BF16).rearrange("p (i n) -> p i n", i=FT)
        gu_t = sb1("gu_t", [D, 2, FT * P], BF16)
        wd_t = sb1("wd_t", [P, FT, D], BF16)
        x_q = zt_halves[:, 0:N].bitcast(BF16)
        wd_row = sb1("wd_row", [P, D])
        clips = sb1("clips", [P, 2])
        clip_sig = sb1("clip_sig", [P, 2])
        x_tops = sb1("x_tops", [P, CH])
        x_max = sb1("x_max", [P, 1])
        x_all = sb1("x_all", [P, 1])
        x_scale = sb1("x_scale", [P, 1])
        x_inv = sb1("x_inv", [P, 1])
        gu_cols = sb1("gu_cols", [P, 2, FT])
        h_max = sb1("h_max", [P, FT * CH])
        h_top = sb1("h_top", [P, 1])
        h_all = sb1("h_all", [P, 1])
        h_scale = sb1("h_scale", [P, 1])
        h_inv = sb1("h_inv", [P, 1])
        y_part = grid.rearrange("p (c t d) -> p c t d", c=CH, t=4)
        h_cleared, ld6, mv3, ve3, rs3, wt_done, wt_read, z3_ready, clip_ready, x_chain = (
            sem(n) for n in ("h_cleared", "ld6", "mv3", "ve3", "rs3", "wt_done", "wt_read", "z3_ready", "clip_ready",
                             "x_chain"))
        x_reduced, z3t_done, grid_ready, xq_ready, gu_done, gated_ready, hidden_ready, h_maxed, h_reduced = (
            sem(n) for n in ("x_reduced", "z3t_done", "grid_ready", "xq_ready", "gu_done", "gated_ready",
                             "hidden_ready", "h_maxed", "h_reduced"))
        x_topped, on_grid, last_out_ready = sem("x_topped"), sem("on_grid"), sem("last_out_ready")
        h_grid, hq_ready, y3_done, y3_read, out_ready, stored, h_chain = (
            sem(n) for n in ("h_grid", "hq_ready", "y3_done", "y3_read", "out_ready", "stored", "h_chain"))
        UNITS_H = FT * CH

        with nc.Block() as block:
            @block.sync
            def _(sp):
                sp.dma_start(clips[:, 0:1], f1_cx.partition_broadcast(P)).then_inc(ld6, 16)
                sp.dma_start(clips[:, 1:2], f1_cd.partition_broadcast(P)).then_inc(ld6, 16)
                for c in range(CH):
                    if c < CH - 1:
                        sp.wait_ge(out_ready, c + 1)
                    else:
                        sp.wait_ge(last_out_ready, 1)
                    sp.dma_start(out[:, 4 * c:4 * c + 4, :], xres[:, 4 * c:4 * c + 4, :]).then_inc(stored, 16)
                sp.wait_ge(stored, 16 * CH)

            @block.gpsimd
            def _(pool):
                pool.wait_ge(ve3, 1)
                for c in range(CH):
                    four = slice(4 * c, 4 * c + 4)
                    nc.gpsimd.tensor_tensor(rstd[:, four], var_eps[:, four], minus_half[:, four], ALU.pow).then_inc(rs3, 1)
                pool.wait_ge(x_chain, 1)
                nc.gpsimd.partition_all_reduce(x_all[:, :], x_max[:, :], P, bass.bass_isa.ReduceOp.max).then_inc(x_reduced, 1)
                pool.wait_ge(h_chain, 1)
                nc.gpsimd.partition_all_reduce(h_all[:, :], h_top[:, :], P, bass.bass_isa.ReduceOp.max).then_inc(h_reduced, 1)
                for c in range(CH - 1):
                    four = slice(4 * c, 4 * c + 4)
                    pool.wait_ge(y3_read, c + 1)
                    nc.gpsimd.tensor_tensor(xres[:, four, :], xres[:, four, :], y_part[:, c, :, :], ALU.add).then_inc(out_ready, 1)

            @block.scalar
            def _(act):
                act.wait_ge(ld6, 32)
                nc.scalar.activation(clip_sig[:, :], clips[:, :], ACT.Sigmoid).then_inc(clip_ready, 1)
                nc.scalar.activation(gated[:, 0, 0:2], clips[:, :], ACT.Silu)
                for n in range(CH):
                    act.wait_ge(grid_ready, n + 1)
                    nc.scalar.activation(x_q[:, 512 * n:512 * n + 512], grid[:, 512 * n:512 * n + 512], ACT.Copy,
                                         bias=-MAGIC).then_inc(xq_ready, 1)
                act.wait_ge(x_chain, 5)
                for n in range(UNITS_H):
                    i = n // CH
                    p = height[i]
                    act.wait_ge(gu_done, n + 1)
                    wait(act, hidden_ready, n - 1)
                    nc.scalar.activation(gated[0:p, n % 2, :], banks[4 + 2 * (n % 2)][0:p, :], ACT.Silu,
                                         scale=gu_cols[0:p, 0, i:i + 1]).then_inc(gated_ready, 1)
                for m in range(UNITS_H):
                    i, c = m % FT, m // FT
                    w = slice(512 * c, 512 * c + 512)
                    p = height[i]
                    act.wait_ge(h_grid, m + 1)
                    nc.scalar.activation(hidden_q[0:p, i, w], hidden[0:p, i, w], ACT.Copy, bias=-MAGIC).then_inc(hq_ready, 1)

            @block.vector
            def _(dve):
                for t in range(NT):
                    nc.vector.bn_aggr(mv[:, t, :], stats[:, t, :]).then_inc(mv3, 1)
                nc.vector.memset(h_max[:, :], 0.0).then_inc(h_cleared, 1)
                dve.wait_ge(mv3, NT)
                nc.vector.tensor_scalar(var_eps[:, :], mv[:, :, 1], LN_EPS, None, ALU.add).then_inc(ve3, 1)
                for side in range(2):
                    dve.wait_ge(wt_done, side + 1)
                    nc.vector.tensor_copy(gu_t[:, side, 0:FF], banks[side][:, 0:FF]).then_inc(wt_read, 1)
                dve.wait_ge(wt_done, 3)
                for i in range(FT):
                    p = height[i]
                    nc.vector.tensor_copy(wd_t[0:p, i, :], banks[2][0:p, D * i:D * i + D]).then_inc(wt_read, 1)
                for c in range(CH):
                    dve.wait_ge(rs3, c + 1)
                    for t in range(4 * c, 4 * c + 4):
                        nc.vector.tensor_scalar(z3[:, t, :], xres[:, t, :], mv[:, t, 0:1], rstd[:, t:t + 1],
                                                ALU.subtract, ALU.mult).then_inc(z3_ready, 1)
                    dve.wait_ge(z3_ready, 4 * c + 4)
                    nc.vector.tensor_reduce(x_tops[:, c:c + 1], z3[:, 4 * c:4 * c + 4, :], AX.XY, ALU.max,
                                            apply_absolute_value=True).then_inc(x_topped, 1)
                dve.wait_ge(x_topped, CH)
                nc.vector.tensor_reduce(x_max[:, :], x_tops[:, :], AX.X, ALU.max).then_inc(x_chain, 1)
                dve.wait_ge(x_reduced, 1)
                dve.wait_ge(clip_ready, 1)
                nc.vector.tensor_scalar(x_scale[:, :], x_all[:, :], clip_sig[:, 0:1], 1.0 / QMAX, ALU.mult, ALU.mult)\
                    .then_inc(x_chain, 1)
                dve.wait_ge(x_chain, 2)
                nc.vector.reciprocal(x_inv[:, :], x_scale[:, :]).then_inc(x_chain, 1)
                nc.vector.tensor_scalar(gu_cols[:, :, 0:FT - 1], gu_scale[:, :, 0:FT - 1], x_scale[:, 0:1], None,
                                        ALU.mult).then_inc(x_chain, 1)
                p = height[FT - 1]
                nc.vector.tensor_scalar(gu_cols[0:p, :, FT - 1], gu_scale[0:p, :, FT - 1], x_scale[0:p, 0:1], None,
                                        ALU.mult).then_inc(x_chain, 1)
                dve.wait_ge(x_chain, 5)
                for n in range(CH + 1):
                    if n < CH:
                        dve.wait_ge(z3t_done, n + 1)
                        nc.vector.tensor_scalar(grid[:, 512 * n:512 * n + 512], banks[4 + n][:, :], x_inv[:, 0:1], MAGIC,
                                                ALU.mult, ALU.add).then_inc(on_grid, 1)
                    if n > 0:
                        w = grid[:, 512 * n - 512:512 * n]
                        dve.wait_ge(on_grid, n)
                        nc.vector.tensor_scalar(w, w, MAGIC + QMAX, MAGIC - QMAX - 1.0, ALU.min, ALU.max).then_inc(grid_ready, 1)
                dve.wait_ge(h_cleared, 1)
                def place(n):
                    return hidden[0:height[n // CH], n // CH, 512 * (n % CH):512 * (n % CH) + 512]

                for n in range(UNITS_H + 1):
                    if n < UNITS_H:
                        i = n // CH
                        p = height[i]
                        dve.wait_ge(gated_ready, n + 1)
                        nc.vector.scalar_tensor_tensor(place(n), banks[5 + 2 * (n % 2)][0:p, :], gu_cols[0:p, 1, i:i + 1],
                                                       gated[0:p, n % 2, :], ALU.mult, ALU.mult).then_inc(hidden_ready, 1)
                    if n > 0:
                        dve.wait_ge(hidden_ready, n)
                        nc.vector.tensor_reduce(h_max[0:height[(n - 1) // CH], n - 1:n], place(n - 1), AX.X, ALU.max,
                                                apply_absolute_value=True).then_inc(h_maxed, 1)
                dve.wait_ge(h_maxed, UNITS_H)
                nc.vector.tensor_reduce(h_top[:, :], h_max[:, :], AX.X, ALU.max).then_inc(h_chain, 1)
                dve.wait_ge(h_reduced, 1)
                nc.vector.tensor_scalar(h_scale[:, :], h_all[:, :], clip_sig[:, 1:2], 1.0 / QMAX, ALU.mult, ALU.mult)\
                    .then_inc(h_chain, 1)
                dve.wait_ge(h_chain, 2)
                nc.vector.reciprocal(h_inv[:, :], h_scale[:, :]).then_inc(h_chain, 1)
                dve.wait_ge(wt_done, 4)
                nc.vector.tensor_scalar(wd_row[:, :], banks[3][:, 0:D], h_scale[:, 0:1], None, ALU.mult).then_inc(h_chain, 1)
                dve.wait_ge(h_chain, 4)
                order = [CH * i + c for c in range(CH) for i in range(FT)]
                for m in range(UNITS_H + 1):
                    if m < UNITS_H:
                        h = place(order[m])
                        nc.vector.tensor_scalar(h, h, h_inv[0:height[order[m] // CH], 0:1], MAGIC, ALU.mult,
                                                ALU.add).then_inc(on_grid, 1)
                    if m > 0:
                        h = place(order[m - 1])
                        dve.wait_ge(on_grid, CH + m)
                        nc.vector.tensor_scalar(h, h, MAGIC + QMAX, MAGIC - QMAX - 1.0, ALU.min, ALU.max).then_inc(h_grid, 1)
                for c in range(CH):
                    dve.wait_ge(y3_done, c + 1)
                    nc.vector.tensor_tensor(y_part[:, c, :, :], banks[4 + c][:, :].rearrange("p (t d) -> p t d", t=4),
                                            wd_row[:, :].unsqueeze(1).to_broadcast([P, 4, D]), ALU.mult).then_inc(y3_read, 1)
                dve.wait_ge(y3_read, CH)
                nc.vector.tensor_tensor(xres[:, NT - 4:NT, :], xres[:, NT - 4:NT, :], y_part[:, CH - 1, :, :],
                                        ALU.add).then_inc(last_out_ready, 1)

            @block.tensor
            def _(pe):
                for side in range(2):
                    for i in range(FT):
                        p = height[i]
                        last = nc.tensor.transpose(banks[side][:, P * i:P * i + p], gu_raw[0:p, side, i, :], ident[0:p, 0:p])
                    last.then_inc(wt_done, 1)
                for i in range(FT):
                    p = height[i]
                    last = nc.tensor.transpose(banks[2][0:p, D * i:D * i + D], wd_raw[:, P * i:P * i + p], ident[:, :])
                last.then_inc(wt_done, 1)
                nc.tensor.matmul(banks[3][:, 0:D], ones[:, :], wd_diag[:, :], start=True, stop=True).then_inc(wt_done, 1)
                pe.wait_ge(wt_read, 2 + FT)
                for n in range(CH):
                    pe.wait_ge(z3_ready, 4 * n + 4)
                    for j in range(4):
                        last = nc.tensor.transpose(banks[4 + n][:, P * j:P * j + P], z3[:, 4 * n + j, :], ident[:, :])
                    last.then_inc(z3t_done, 1)
                for n in range(UNITS_H):
                    i, c = n // CH, n % CH
                    p = height[i]
                    pe.wait_ge(xq_ready, CH)
                    wait(pe, hidden_ready, n - 1)
                    nc.tensor.matmul(banks[4 + 2 * (n % 2)][0:p, :], gu_t[:, 0, P * i:P * i + p],
                                     x_q[:, 512 * c:512 * c + 512], start=True, stop=True)
                    nc.tensor.matmul(banks[5 + 2 * (n % 2)][0:p, :], gu_t[:, 1, P * i:P * i + p],
                                     x_q[:, 512 * c:512 * c + 512], start=True, stop=True).then_inc(gu_done, 1)
                for c in range(CH):
                    for j in range(4):
                        t = 4 * c + j
                        for i in range(FT):
                            p = height[i]
                            pe.wait_ge(hq_ready, FT * c + i + 1)
                            last = nc.tensor.matmul(banks[4 + c][:, P * j:P * j + P], hidden_q[0:p, i, P * t:P * t + P],
                                                    wd_t[0:p, i, :], start=(i == 0), stop=(i == FT - 1))
                    last.then_inc(y3_done, 1)
        scratch.close()


def laid_out(inputs):
    import numpy as _np
    a = {k: _np.ascontiguousarray(v) for k, v in inputs.items()}

    def tiles(m):
        return _np.ascontiguousarray(m.reshape(-1, P, m.shape[-1]).transpose(1, 0, 2))

    def heads_t(w):
        return _np.ascontiguousarray(w.reshape(w.shape[0], H0, DH0).transpose(2, 1, 0))

    return {
        "x": tiles(a["x"].reshape(N, D)),
        "ctx_tok": tiles(a["ctx_768"].reshape(N, C)),
        "ctx_t": _np.ascontiguousarray(a["ctx_768"].reshape(N, C).T),
        "l0_wq_t": heads_t(a["L0_xattn_Wq"]),
        "l0_wk_t": heads_t(a["L0_xattn_Wk"]),
        "l0_wv": a["L0_xattn_Wv"],
        "l0_wo": tiles(a["L0_xattn_Wo"]),
        "l0_bo": a["L0_xattn_bo"],
        "f0_wg": a["L0_ffn_Wg"],
        "f0_w1": tiles(a["L0_ffn_W1"].reshape(-1, D)),
        "f0_b1": _np.ascontiguousarray(a["L0_ffn_b1"].reshape(-1, P).T),
        "f0_wo_t": tiles(_np.ascontiguousarray(a["L0_ffn_Wo"].T)),
        "f0_bo": a["L0_ffn_bo"],
        "l1_qw": a["L1_xattn_q_w"], "l1_qb": a["L1_xattn_q_b"],
        "l1_kw": a["L1_xattn_k_w"], "l1_kb": a["L1_xattn_k_b"],
        "l1_vw": a["L1_xattn_v_w"], "l1_vb": a["L1_xattn_v_b"],
        "l1_g": a["L1_xattn_ln_g"], "l1_b": a["L1_xattn_ln_b"],
        "l1_tg": a["L1_xattn_tln_g"], "l1_tb": a["L1_xattn_tln_b"],
        "f1_cx": a["L1_ffn_clip_x"], "f1_cd": a["L1_ffn_clip_down"],
        "f1_wg": a["L1_ffn_w_gate"], "f1_wu": a["L1_ffn_w_up"], "f1_wd": a["L1_ffn_w_down"],
    }


def kernel(**inputs):
    import numpy as _np
    import concourse.bacc as _bacc
    from concourse import mybir as _mybir
    from concourse.bass_utils import run_bass_kernel_spmd as _run

    nc = _bacc.Bacc("TRN2", target_bir_lowering=False, num_devices=1)
    arrays, args = {}, {}
    for name, a in laid_out(inputs).items():
        arrays[f"in_{name}"] = a
        args[name] = nc.dram_tensor(f"in_{name}", a.shape, _mybir.dt.from_np(a.dtype), kind="ExternalInput").ap()
    out = nc.dram_tensor("out", (P, NT, D), F32, kind="ExternalOutput").ap()
    cross_ffn_network(nc, out=out, **args)
    r = _run(nc, [arrays], core_ids=[0])
    return _np.ascontiguousarray(r.results[0]["out"].transpose(1, 0, 2)).reshape(B, S, D)
```
